# Optimizing a Trainium2 kernel written in Bass

```python
import numpy as np
import jax
import jax.numpy as jnp

def _softmax(x, axis=-1):
    return jax.nn.softmax(x, axis=axis)

def _gelu(x):
    return jax.nn.gelu(x, approximate=True)

def _silu(x):
    return jax.nn.silu(x)

def _sigmoid(x):
    return jax.nn.sigmoid(x)

def _layernorm(x, axis=-1, eps=1e-05):
    m = jnp.mean(x, axis=axis, keepdims=True)
    v = jnp.var(x, axis=axis, keepdims=True)
    return (x - m) / jnp.sqrt(v + eps)

def _scatter_add(tgt, idx, src, axis=0):
    return tgt.at[idx].add(src)

def _segment_sum(src, seg, n):
    return jax.ops.segment_sum(src, seg, n)
kernel_name = 'mk_decoder_postln_d4_seqx_r8_7da68e'

def setup_inputs(seed: int=0):
    np.random.seed(seed)
    _w = jnp.asarray

    def _rec_inputs():
        import jax
        import jax.numpy as jnp
        _rk = jax.random.key(seed)
        x = -0.0002928 + 1 * jax.random.normal(jax.random.fold_in(_rk, 1), (4, 512, 128), jnp.float32)
        _lenS = 512 - jax.random.randint(jax.random.fold_in(_rk, 7), (4,), 0, max(1, 512 // 4) + 1, jnp.int32)
        _lenS2 = 154 - jax.random.randint(jax.random.fold_in(_rk, 8), (4,), 0, max(1, 154 // 4) + 1, jnp.int32)
        _ctx_768P = jax.random.normal(jax.random.fold_in(_rk, 11), (4, 16, 96), jnp.float32)
        _ctx_768c = jax.random.dirichlet(jax.random.fold_in(_rk, 511), 0.3 * jnp.ones((16,), jnp.float32), (4, 154))
        _ctx_768t = jnp.einsum('bsk,bkd->bsd', _ctx_768c, _ctx_768P)
        _ctx_768t = _ctx_768t * jax.lax.rsqrt(jnp.mean(jnp.square(_ctx_768t)) + 1e-12) * 0.953939
        ctx_768 = 2.09791e-05 + 1.00001 * (_ctx_768t + 0.3 * jax.random.normal(jax.random.fold_in(_rk, 611), (4, 154, 96), jnp.float32))
        _validS = jnp.arange(512)[None, :] < _lenS[:, None]
        _validS2 = jnp.arange(154)[None, :] < _lenS2[:, None]
        _causal = jnp.tril(jnp.ones((512, 512), dtype=bool))
        mask_BxS2_bf1 = jnp.ones((4, 154), dtype=bool)
        mask_1x1xSxS2_bk0 = jnp.logical_not(jnp.broadcast_to(_validS2[0:1, None, None, :], (1, 1, 512, 154)))
        return (x, ctx_768, mask_BxS2_bf1, mask_1x1xSxS2_bk0)
    x, ctx_768, mask_BxS2_bf1, mask_1x1xSxS2_bk0 = _rec_inputs()

    def _L0_attn_setup():
        import jax, jax.numpy as jnp
        import numpy as np
        import math
        D_MODEL = 128
        LAYER_ID = 6
        NUM_LAYERS = 12
        B, T = (8, 256)
        MIN_P = -1e+38

        def _init_params():
            C = D_MODEL
            r01 = LAYER_ID / (NUM_LAYERS - 1)
            r1a0 = 1.0 - LAYER_ID / NUM_LAYERS
            h = np.arange(C, dtype=np.float32)
            decay_speed = -5.0 + 8.0 * (h / (C - 1)) ** (0.7 + 1.3 * r01)
            zigzag = ((np.arange(C) + 1) % 3 - 1).astype(np.float32) * 0.5
            U = np.float32(math.log(0.3)) + zigzag
            xx = (np.arange(C, dtype=np.float32) / C).reshape(1, 1, C)
            tmk = xx ** r1a0
            tmv = xx ** r1a0 + 0.3 * r01
            tmr = xx ** (0.5 * r1a0)
            return (jnp.asarray(decay_speed), jnp.asarray(U), jnp.asarray(tmk, jnp.float32), jnp.asarray(tmv, jnp.float32), jnp.asarray(tmr, jnp.float32))

        def _wkv(W, U, k, v):
            w = -jnp.exp(W)
            Bb, Tt, Cc = k.shape
            aa0 = jnp.zeros((Bb, Cc), k.dtype)
            bb0 = jnp.zeros((Bb, Cc), k.dtype)
            pp0 = jnp.full((Bb, Cc), MIN_P, k.dtype)

            def step(carry, kv_t):
                aa, bb, pp = carry
                kt, vt = kv_t
                ww = U + kt
                p = jnp.maximum(pp, ww)
                e1 = jnp.exp(pp - p)
                e2 = jnp.exp(ww - p)
                y = (e1 * aa + e2 * vt) / (e1 * bb + e2)
                ww2 = pp + w
                p2 = jnp.maximum(ww2, kt)
                e1b = jnp.exp(ww2 - p2)
                e2b = jnp.exp(kt - p2)
                return ((e1b * aa + e2b * vt, e1b * bb + e2b, p2), y)
            kT = jnp.swapaxes(k, 0, 1)
            vT = jnp.swapaxes(v, 0, 1)
            _, yT = jax.lax.scan(step, (aa0, bb0, pp0), (kT, vT))
            return jnp.swapaxes(yT, 0, 1)

        def _reference_tuple_inner(x, W, U, time_mix_k, time_mix_v, time_mix_r, Wk, Wv, Wr, Wo):
            xs = jnp.pad(x, ((0, 0), (1, 0), (0, 0)))[:, :-1]
            xk = x * time_mix_k + xs * (1.0 - time_mix_k)
            xv = x * time_mix_v + xs * (1.0 - time_mix_v)
            xr = x * time_mix_r + xs * (1.0 - time_mix_r)
            K = jnp.einsum('btc,dc->btd', xk, Wk)
            V = jnp.einsum('btc,dc->btd', xv, Wv)
            R = jnp.einsum('btc,dc->btd', xr, Wr)
            wkv = _wkv(W, U, K, V)
            hidden = jax.lax.stop_gradient(wkv[:, -1, :])
            rwkv = jax.nn.sigmoid(R) * wkv
            output = jnp.einsum('btc,dc->btd', rwkv, Wo)
            return (output, hidden)
        key = jax.random.key(seed)
        k0, k1, k2, k3, k4 = jax.random.split(key, 5)
        W, U, tmk, tmv, tmr = _init_params()
        C = D_MODEL
        s = 1.0 / math.sqrt(C)
        return {'x': jax.random.normal(k0, (B, T, C), jnp.float32), 'W': W, 'U': U, 'time_mix_k': tmk, 'time_mix_v': tmv, 'time_mix_r': tmr, 'Wk': jax.random.normal(k1, (C, C), jnp.float32) * s, 'Wv': jax.random.normal(k2, (C, C), jnp.float32) * s, 'Wr': jax.random.normal(k3, (C, C), jnp.float32) * s, 'Wo': jax.random.normal(k4, (C, C), jnp.float32) * s}
    _L0_attn_all = _L0_attn_setup()
    _L0_attn_in = {k: v for k, v in _L0_attn_all.items() if k in ('W', 'U', 'time_mix_k', 'time_mix_v', 'time_mix_r', 'Wk', 'Wv', 'Wr', 'Wo')}
    del _L0_attn_all

    def _L0_xattn_setup():
        import jax, jax.numpy as jnp
        import numpy as np
        import math
        B, N, M = (4, 128, 128)
        DIM, CTX_DIM = (128, 96)
        HEADS, DIM_HEAD = (16, 64)
        INNER = HEADS * DIM_HEAD

        def layer_norm(t, g, eps=1e-05):
            mean = jnp.mean(t, axis=-1, keepdims=True)
            var = jnp.mean((t - mean) ** 2, axis=-1, keepdims=True)
            return (t - mean) * jax.lax.rsqrt(var + eps) * g
        key = jax.random.key(seed)
        ks = jax.random.split(key, 8)
        return {'x': jax.random.normal(ks[0], (B, N, DIM), jnp.float32), 'context': jax.random.normal(ks[1], (B, M, CTX_DIM), jnp.float32), 'mask': jnp.ones((B, M), dtype=bool), 'g_norm': jnp.ones((DIM,), jnp.float32), 'null_kv': jax.random.normal(ks[2], (2, DIM_HEAD), jnp.float32), 'Wq': jax.random.normal(ks[3], (DIM, INNER), jnp.float32) * DIM ** (-0.5), 'Wkv': jax.random.normal(ks[4], (CTX_DIM, 2 * INNER), jnp.float32) * CTX_DIM ** (-0.5), 'Wout': jax.random.normal(ks[5], (INNER, DIM), jnp.float32) * INNER ** (-0.5), 'g_out': jnp.ones((DIM,), jnp.float32)}
    _L0_xattn_all = _L0_xattn_setup()
    _L0_xattn_in = {k: v for k, v in _L0_xattn_all.items() if k in ('g_norm', 'null_kv', 'Wq', 'Wkv', 'Wout', 'g_out')}
    del _L0_xattn_all

    def _L0_ffn_setup():
        import jax, jax.numpy as jnp
        import numpy as np
        D_IN, D_HID = (128, 512)

        def _ternary(key, shape):
            return jax.random.randint(key, shape, -1, 2).astype(jnp.float32)

        def _tlin(x, w, s):
            return jnp.einsum('bsi,oi->bso', x, w) * s
        key = jax.random.key(seed)
        ks = jax.random.split(key, 12)
        inv = lambda fan: 1.0 / np.sqrt(fan).astype(np.float32)
        return {'x': jax.random.normal(ks[0], (4, 256, D_IN), dtype=jnp.float32), 'w1_w': _ternary(ks[1], (D_HID, D_IN)), 'w1_s': jax.random.uniform(ks[2], (D_HID,), dtype=jnp.float32) * inv(D_IN), 'w2_w': _ternary(ks[3], (D_HID, D_IN)), 'w2_s': jax.random.uniform(ks[4], (D_HID,), dtype=jnp.float32) * inv(D_IN), 'h1_w': _ternary(ks[5], (D_HID, D_HID)), 'h1_s': jax.random.uniform(ks[6], (D_HID,), dtype=jnp.float32) * inv(D_HID), 'h2_w': _ternary(ks[7], (D_HID, D_HID)), 'h2_s': jax.random.uniform(ks[8], (D_HID,), dtype=jnp.float32) * inv(D_HID), 'w3_w': _ternary(ks[9], (D_IN, D_HID)), 'w3_s': jax.random.uniform(ks[10], (D_IN,), dtype=jnp.float32) * inv(D_HID)}
    _L0_ffn_all = _L0_ffn_setup()
    _L0_ffn_in = {k: v for k, v in _L0_ffn_all.items() if k in ('w1_w', 'w1_s', 'w2_w', 'w2_s', 'h1_w', 'h1_s', 'h2_w', 'h2_s', 'w3_w', 'w3_s')}
    del _L0_ffn_all

    def _L1_attn_setup():
        import jax, jax.numpy as jnp
        import numpy as np
        B, SEQ, DIM = (2, 256, 128)
        H = 16
        DH = DIM // H
        LAT = 64
        CTX = SEQ - LAT
        SCALE = DH ** (-0.5)
        LN_EPS = 1e-05

        def _rotary_cos_sin(n):
            inv_freq = 1.0 / 10000.0 ** (jnp.arange(0, DH, 2, dtype=jnp.float32) / DH)
            freqs = jnp.arange(n, dtype=jnp.float32)[:, None] * inv_freq[None, :]
            emb = jnp.concatenate([freqs, freqs], axis=-1)
            return (jnp.cos(emb), jnp.sin(emb))

        def _rotate_half(t):
            t1, t2 = jnp.split(t, 2, axis=-1)
            return jnp.concatenate([-t2, t1], axis=-1)

        def _layernorm(t, g, b):
            m = jnp.mean(t, axis=-1, keepdims=True)
            v = jnp.var(t, axis=-1, keepdims=True)
            return (t - m) / jnp.sqrt(v + LN_EPS) * g + b
        key = jax.random.key(seed)
        ks = jax.random.split(key, 4)
        x = jax.random.normal(ks[0], (B, SEQ, DIM), dtype=jnp.float32)
        Wq = jax.random.normal(ks[1], (DIM, DIM), dtype=jnp.float32) * 0.02
        Wkv = jax.random.normal(ks[2], (DIM, DIM), dtype=jnp.float32) * 0.02
        Wo = jax.random.normal(ks[3], (DIM, DIM), dtype=jnp.float32) * 0.02
        bo = jnp.zeros((DIM,), dtype=jnp.float32)
        ln_g = jnp.ones((DH,), dtype=jnp.float32)
        ln_b = jnp.zeros((DH,), dtype=jnp.float32)
        return {'x': x, 'Wq': Wq, 'Wkv': Wkv, 'Wo': Wo, 'bo': bo, 'ln_g': ln_g, 'ln_b': ln_b}
    _L1_attn_all = _L1_attn_setup()
    _L1_attn_in = {k: v for k, v in _L1_attn_all.items() if k in ('Wq', 'Wkv', 'Wo', 'bo', 'ln_g', 'ln_b')}
    del _L1_attn_all

    def _L1_xattn_setup():
        import jax, jax.numpy as jnp
        import numpy as np
        HEADS = 16
        DIM_HEAD = 64
        key = jax.random.key(seed)
        ks = jax.random.split(key, 7)
        B, Nq, Dq = (4, 256, 128)
        Nk, Dc = (128, 96)
        inner = HEADS * DIM_HEAD
        sq = 1.0 / np.sqrt(Dq)
        sc = 1.0 / np.sqrt(Dc)
        si = 1.0 / np.sqrt(inner)
        return {'x': jax.random.normal(ks[0], (B, Nq, Dq), dtype=jnp.float32), 'context': jax.random.normal(ks[1], (B, Nk, Dc), dtype=jnp.float32), 'Wq': jax.random.normal(ks[2], (Dq, inner), dtype=jnp.float32) * sq, 'Wk': jax.random.normal(ks[3], (Dc, inner), dtype=jnp.float32) * sc, 'Wv': jax.random.normal(ks[4], (Dc, inner), dtype=jnp.float32) * sc, 'Wo': jax.random.normal(ks[5], (inner, Dq), dtype=jnp.float32) * si, 'bo': jax.random.normal(ks[6], (Dq,), dtype=jnp.float32) * 0.01}
    _L1_xattn_all = _L1_xattn_setup()
    _L1_xattn_in = {k: v for k, v in _L1_xattn_all.items() if k in ('Wq', 'Wk', 'Wv', 'Wo', 'bo')}
    del _L1_xattn_all

    def _L1_ffn_setup():
        import jax, jax.numpy as jnp
        import numpy as np
        DIM = 128
        DEPTH = 6
        HEADS = 16
        DIM_HEAD = 64
        WINDOW = 32
        INNER = HEADS * DIM_HEAD
        DIM_INNER = int(DIM * 4 * 2 / 3)
        QK_SCALE = 8.0

        def shift_tokens(t):
            a, s = jnp.split(t, 2, -1)
            s = jnp.pad(s, ((0, 0), (1, 0), (0, 0)))[:, :-1]
            return jnp.concatenate([a, s], -1)

        def l2norm(t):
            return t / jnp.maximum(jnp.linalg.norm(t, axis=-1, keepdims=True), 1e-12)

        def rotate_half(x):
            x1, x2 = jnp.split(x, 2, -1)
            return jnp.concatenate([-x2, x1], -1)

        def rotary_tables(n):
            half = jnp.arange(0, DIM_HEAD, 2, dtype=jnp.float32)
            inv_freq = 1.0 / 10000.0 ** (half / DIM_HEAD)
            t = jnp.arange(n, dtype=jnp.float32)
            freqs = t[:, None] * inv_freq[None, :]
            freqs = jnp.concatenate([freqs, freqs], -1)
            base_scale = (half + 0.4 * DIM_HEAD) / (1.4 * DIM_HEAD)
            power = (t - n // 2) / (WINDOW // 2)
            scale = base_scale[None, :] ** power[:, None]
            scale = jnp.concatenate([scale, scale], -1)
            return (freqs, scale)

        def local_attention(q, k, v):
            b, h, n, d = q.shape
            w = WINDOW
            nw = n // w
            bq = q.reshape(b, h, nw, w, d)
            bk = k.reshape(b, h, nw, w, d)
            bv = v.reshape(b, h, nw, w, d)

            def look(t):
                p = jnp.pad(t, ((0, 0), (0, 0), (1, 0), (0, 0), (0, 0)))
                return jnp.concatenate([p[:, :, :nw], p[:, :, 1:]], axis=3)
            bk2, bv2 = (look(bk), look(bv))
            seq = jnp.arange(n).reshape(nw, w)
            seq_p = jnp.pad(seq, ((1, 0), (0, 0)), constant_values=-1)
            jt = jnp.concatenate([seq_p[:nw], seq_p[1:]], axis=1)
            it = seq[:, :, None]
            jb = jt[:, None, :]
            mask = (it < jb) | (it > jb + w) | (jb == -1)
            sim = jnp.einsum('bhwie,bhwje->bhwij', bq, bk2) * QK_SCALE
            sim = jnp.where(mask, -jnp.finfo(sim.dtype).max, sim)
            attn = jax.nn.softmax(sim, -1)
            out = jnp.einsum('bhwij,bhwje->bhwie', attn, bv2)
            return out.reshape(b, h, n, d)

        def attn_layer(x, Wqkv, qs, ksc, Wo):
            b, n, _ = x.shape
            qkv = x @ Wqkv
            q, k, v = jnp.split(qkv, 3, -1)
            sh = lambda t: t.reshape(b, n, HEADS, DIM_HEAD).transpose(0, 2, 1, 3)
            q, k, v = (sh(q), sh(k), sh(v))
            q = l2norm(q) * qs
            k = l2norm(k) * ksc
            freqs, scale = rotary_tables(n)
            cos, sin = (jnp.cos(freqs), jnp.sin(freqs))
            q = q * cos * scale + rotate_half(q) * sin * scale
            inv = 1.0 / scale
            k = k * cos * inv + rotate_half(k) * sin * inv
            out = local_attention(q, k, v)
            out = out.transpose(0, 2, 1, 3).reshape(b, n, INNER)
            return out @ Wo

        def ffn_layer(x, g, bln, W1, b1, W2, b2):
            mu = x.mean(-1, keepdims=True)
            var = ((x - mu) ** 2).mean(-1, keepdims=True)
            xn = (x - mu) / jnp.sqrt(var + 1e-05) * g + bln
            hg = xn @ W1 + b1
            a, gate = jnp.split(hg, 2, -1)
            return a * jax.nn.gelu(gate, approximate=False) @ W2 + b2
        key = jax.random.key(seed)
        ks = jax.random.split(key, 8)
        B, N = (2, 256)
        init = lambda k, shape: jax.random.normal(k, shape, jnp.float32) * 0.02
        return {'x': jax.random.normal(ks[0], (B, N, DIM), jnp.float32), 'Wqkv': init(ks[1], (DEPTH, DIM, 3 * INNER)), 'q_scale': jnp.ones((DEPTH, DIM_HEAD), jnp.float32), 'k_scale': jnp.ones((DEPTH, DIM_HEAD), jnp.float32), 'Wo': init(ks[2], (DEPTH, INNER, DIM)), 'ln_g': jnp.ones((DEPTH, DIM), jnp.float32), 'ln_b': jnp.zeros((DEPTH, DIM), jnp.float32), 'W1': init(ks[3], (DEPTH, DIM, 2 * DIM_INNER)), 'b1': jnp.zeros((DEPTH, 2 * DIM_INNER), jnp.float32), 'W2': init(ks[4], (DEPTH, DIM_INNER, DIM)), 'b2': jnp.zeros((DEPTH, DIM), jnp.float32)}
    _L1_ffn_all = _L1_ffn_setup()
    _L1_ffn_in = {k: v for k, v in _L1_ffn_all.items() if k in ('Wqkv', 'q_scale', 'k_scale', 'Wo', 'ln_g', 'ln_b', 'W1', 'b1', 'W2', 'b2')}
    del _L1_ffn_all

    def _L2_attn_setup():
        import jax, jax.numpy as jnp
        import numpy as np
        D_MODEL = 128
        D_STATE = 16
        D_CONV = 4
        EXPAND = 2
        D_INNER = D_MODEL * EXPAND

        def soft_clamp(x, lo, hi, sharp):
            c = (hi + lo) / 2.0
            r = (hi - lo) / 2.0
            return jnp.tanh((x - c) / (r + 1e-08) * sharp) / sharp * r + c
        key = jax.random.key(seed)
        ks = jax.random.split(key, 9)
        B, L = (2, 128)
        x = jax.random.normal(ks[0], (B, L, D_MODEL), jnp.float32)
        norm_w = jnp.ones((D_MODEL,), jnp.float32)
        W_in = jax.random.normal(ks[1], (2 * D_INNER, D_MODEL), jnp.float32) * 0.02
        conv_w = jax.random.normal(ks[2], (D_INNER, 1, D_CONV), jnp.float32) * 0.02
        conv_b = jnp.zeros((D_INNER,), jnp.float32)
        W_dt = jax.random.normal(ks[3], (D_INNER, D_INNER), jnp.float32) * 0.02
        b_dt = jnp.full((D_INNER,), -2.0, jnp.float32)
        W_B = jax.random.normal(ks[4], (D_STATE, D_INNER), jnp.float32) * 0.02
        W_C = jax.random.normal(ks[5], (D_STATE, D_INNER), jnp.float32) * 0.02
        A_log = jax.random.normal(ks[6], (D_INNER, D_STATE), jnp.float32) * 0.1
        D_param = jnp.full((D_INNER,), 0.1, jnp.float32)
        W_out = jax.random.normal(ks[7], (D_MODEL, D_INNER), jnp.float32) * 0.02
        residual_scale = jnp.asarray(0.3, jnp.float32)
        return dict(x=x, norm_w=norm_w, W_in=W_in, conv_w=conv_w, conv_b=conv_b, W_dt=W_dt, b_dt=b_dt, W_B=W_B, W_C=W_C, A_log=A_log, D_param=D_param, W_out=W_out, residual_scale=residual_scale)
    _L2_attn_all = _L2_attn_setup()
    _L2_attn_in = {k: v for k, v in _L2_attn_all.items() if k in ('norm_w', 'W_in', 'conv_w', 'conv_b', 'W_dt', 'b_dt', 'W_B', 'W_C', 'A_log', 'D_param', 'W_out', 'residual_scale')}
    del _L2_attn_all

    def _L2_xattn_setup():
        import jax, jax.numpy as jnp
        import numpy as np
        B, T, Q_DIM, KV_DIM = (4, 256, 128, 96)
        HEADS, DIM_HEAD = (16, 64)
        INNER = HEADS * DIM_HEAD
        NUM_FRAMES, NUM_PATCHES = (8, 32)
        LN_EPS = 1e-05

        def diagonal_frame_mask(num_patches, num_frames):
            fid = np.repeat(np.arange(num_frames), num_patches)
            m = fid[:, None] == fid[None, :]
            return jnp.asarray(m[None, None])
        key = jax.random.key(seed)
        ks = jax.random.split(key, 6)
        s = lambda d: 1.0 / np.sqrt(d)
        return {'x': jax.random.normal(ks[0], (B, T, Q_DIM), jnp.float32), 'context': jax.random.normal(ks[1], (B, T, KV_DIM), jnp.float32), 'ln_gamma': jnp.ones((Q_DIM,), jnp.float32), 'ln_beta': jnp.zeros((Q_DIM,), jnp.float32), 'Wq': jax.random.normal(ks[2], (Q_DIM, INNER), jnp.float32) * s(Q_DIM), 'Wkv': jax.random.normal(ks[3], (KV_DIM, 2 * INNER), jnp.float32) * s(KV_DIM), 'Wo': jax.random.normal(ks[4], (INNER, Q_DIM), jnp.float32) * s(INNER), 'bo': jnp.zeros((Q_DIM,), jnp.float32), 'mask': diagonal_frame_mask(NUM_PATCHES, NUM_FRAMES)}
    _L2_xattn_all = _L2_xattn_setup()
    _L2_xattn_in = {k: v for k, v in _L2_xattn_all.items() if k in ('ln_gamma', 'ln_beta', 'Wq', 'Wkv', 'Wo', 'bo')}
    del _L2_xattn_all

    def _L2_ffn_setup():
        import jax, jax.numpy as jnp
        import numpy as np
        B, S, D_MODEL, D_HIDDEN = (4, 256, 128, 512)

        def act_quant(x):
            scale = 127.0 / jnp.clip(jnp.max(jnp.abs(x), axis=-1, keepdims=True), 1e-05)
            return jnp.clip(jnp.round(x * scale), -128, 127) / scale

        def weight_quant(w):
            scale = 1.0 / jnp.clip(jnp.mean(jnp.abs(w)), 1e-05)
            return jnp.clip(jnp.round(w * scale), -1, 1) / scale

        def bit_linear(x, w):
            xq = x + jax.lax.stop_gradient(act_quant(x) - x)
            wq = w + jax.lax.stop_gradient(weight_quant(w) - w)
            return jnp.einsum('bsd,hd->bsh', xq, wq)

        def depthwise_conv1d(x_bcl, w, b):
            y = jax.lax.conv_general_dilated(x_bcl, w, window_strides=(1,), padding=[(1, 1)], dimension_numbers=('NCH', 'OIH', 'NCH'), feature_group_count=x_bcl.shape[1])
            return y + b[None, :, None]
        key = jax.random.key(seed)
        ks = jax.random.split(key, 5)
        lim1 = 1.0 / np.sqrt(D_MODEL)
        lim2 = 1.0 / np.sqrt(D_HIDDEN)
        limc = 1.0 / np.sqrt(3.0)
        return {'x': jax.random.normal(ks[0], (B, S, D_MODEL), dtype=jnp.float32), 'w1': jax.random.uniform(ks[1], (D_HIDDEN, D_MODEL), jnp.float32, -lim1, lim1), 'conv_w': jax.random.uniform(ks[2], (D_HIDDEN, 1, 3), jnp.float32, -limc, limc), 'conv_b': jax.random.uniform(ks[3], (D_HIDDEN,), jnp.float32, -limc, limc), 'w2': jax.random.uniform(ks[4], (D_MODEL, D_HIDDEN), jnp.float32, -lim2, lim2)}
    _L2_ffn_all = _L2_ffn_setup()
    _L2_ffn_in = {k: v for k, v in _L2_ffn_all.items() if k in ('w1', 'conv_w', 'conv_b', 'w2')}
    del _L2_ffn_all

    def _L3_attn_setup():
        import jax, jax.numpy as jnp
        import numpy as np
        import math
        EMBED = 128
        HEADS = 16
        HEAD_DIM = EMBED // HEADS
        B, N = (2, 256)
        key = jax.random.key(seed)
        ks = jax.random.split(key, 8)
        s = 1.0 / math.sqrt(EMBED)
        Wq = jax.random.uniform(ks[0], (EMBED, EMBED), jnp.float32, -s, s)
        bq = jax.random.uniform(ks[1], (EMBED,), jnp.float32, -s, s)
        Wk = jax.random.uniform(ks[2], (EMBED, EMBED), jnp.float32, -s, s)
        bk = jax.random.uniform(ks[3], (EMBED,), jnp.float32, -s, s)
        Wv = jax.random.uniform(ks[4], (EMBED, EMBED), jnp.float32, -s, s)
        bv = jax.random.uniform(ks[5], (EMBED,), jnp.float32, -s, s)
        Wp = jax.random.normal(ks[6], (HEAD_DIM, HEAD_DIM), jnp.float32)
        x = jax.random.normal(ks[7], (B, N, EMBED), jnp.float32)
        return {'x': x, 'Wq': Wq, 'bq': bq, 'Wk': Wk, 'bk': bk, 'Wv': Wv, 'bv': bv, 'Wp': Wp}
    _L3_attn_all = _L3_attn_setup()
    _L3_attn_in = {k: v for k, v in _L3_attn_all.items() if k in ('Wq', 'bq', 'Wk', 'bk', 'Wv', 'bv', 'Wp')}
    del _L3_attn_all

    def _L3_xattn_setup():
        import jax, jax.numpy as jnp
        import numpy as np
        NUM_HEADS = 16
        key = jax.random.key(seed)
        ks = jax.random.split(key, 8)
        dim, cond_dim = (128, 96)
        B, N, condN = (4, 256, 128)
        s = lambda k, shp, fan: jax.random.normal(k, shp, dtype=jnp.float32) * fan ** (-0.5)
        return {'x': jax.random.normal(ks[0], (B, N, dim), dtype=jnp.float32), 'cond': jax.random.normal(ks[1], (B, condN, cond_dim), dtype=jnp.float32), 'q_w': s(ks[2], (dim, dim), dim), 'q_b': jnp.zeros((dim,), jnp.float32), 'kv_w': s(ks[3], (cond_dim, 2 * dim), cond_dim), 'kv_b': jnp.zeros((2 * dim,), jnp.float32), 'proj_w': s(ks[4], (dim, dim), dim), 'proj_b': jnp.zeros((dim,), jnp.float32)}
    _L3_xattn_all = _L3_xattn_setup()
    _L3_xattn_in = {k: v for k, v in _L3_xattn_all.items() if k in ('q_w', 'q_b', 'kv_w', 'kv_b', 'proj_w', 'proj_b')}
    del _L3_xattn_all

    def _L3_ffn_setup():
        import jax, jax.numpy as jnp
        import numpy as np
        D = 128
        H = 256
        E = 8
        K = 2
        B, S = (4, 256)

        def _ffn(x, w1, w2, w3):
            return jax.nn.silu(x @ w1.T) * (x @ w3.T) @ w2.T
        key = jax.random.key(seed)
        ks = jax.random.split(key, 9)
        sc = 0.02
        return {'h': jax.random.normal(ks[0], (B, S, D), jnp.float32), 'sw1': jax.random.normal(ks[1], (H, D), jnp.float32) * sc, 'sw2': jax.random.normal(ks[2], (D, H), jnp.float32) * sc, 'sw3': jax.random.normal(ks[3], (H, D), jnp.float32) * sc, 'W1': jax.random.normal(ks[4], (E, H, D), jnp.float32) * sc, 'W2': jax.random.normal(ks[5], (E, D, H), jnp.float32) * sc, 'W3': jax.random.normal(ks[6], (E, H, D), jnp.float32) * sc, 'Wg': jax.random.normal(ks[7], (E, D), jnp.float32) * sc}
    _L3_ffn_all = _L3_ffn_setup()
    _L3_ffn_in = {k: v for k, v in _L3_ffn_all.items() if k in ('sw1', 'sw2', 'sw3', 'W1', 'W2', 'W3', 'Wg')}
    del _L3_ffn_all
    return {'x': x, 'ctx_768': ctx_768, 'mask_BxS2_bf1': mask_BxS2_bf1, 'mask_1x1xSxS2_bk0': mask_1x1xSxS2_bk0, 'L0_attn_W': _L0_attn_in['W'], 'L0_attn_U': _L0_attn_in['U'], 'L0_attn_time_mix_k': _L0_attn_in['time_mix_k'], 'L0_attn_time_mix_v': _L0_attn_in['time_mix_v'], 'L0_attn_time_mix_r': _L0_attn_in['time_mix_r'], 'L0_attn_Wk': _L0_attn_in['Wk'], 'L0_attn_Wv': _L0_attn_in['Wv'], 'L0_attn_Wr': _L0_attn_in['Wr'], 'L0_attn_Wo': _L0_attn_in['Wo'], 'L0_xattn_g_norm': _L0_xattn_in['g_norm'], 'L0_xattn_null_kv': _L0_xattn_in['null_kv'], 'L0_xattn_Wq': _L0_xattn_in['Wq'], 'L0_xattn_Wkv': _L0_xattn_in['Wkv'], 'L0_xattn_Wout': _L0_xattn_in['Wout'], 'L0_xattn_g_out': _L0_xattn_in['g_out'], 'L0_ffn_w1_w': _L0_ffn_in['w1_w'], 'L0_ffn_w1_s': _L0_ffn_in['w1_s'], 'L0_ffn_w2_w': _L0_ffn_in['w2_w'], 'L0_ffn_w2_s': _L0_ffn_in['w2_s'], 'L0_ffn_h1_w': _L0_ffn_in['h1_w'], 'L0_ffn_h1_s': _L0_ffn_in['h1_s'], 'L0_ffn_h2_w': _L0_ffn_in['h2_w'], 'L0_ffn_h2_s': _L0_ffn_in['h2_s'], 'L0_ffn_w3_w': _L0_ffn_in['w3_w'], 'L0_ffn_w3_s': _L0_ffn_in['w3_s'], 'L1_attn_Wq': _L1_attn_in['Wq'], 'L1_attn_Wkv': _L1_attn_in['Wkv'], 'L1_attn_Wo': _L1_attn_in['Wo'], 'L1_attn_bo': _L1_attn_in['bo'], 'L1_attn_ln_g': _L1_attn_in['ln_g'], 'L1_attn_ln_b': _L1_attn_in['ln_b'], 'L1_xattn_Wq': _L1_xattn_in['Wq'], 'L1_xattn_Wk': _L1_xattn_in['Wk'], 'L1_xattn_Wv': _L1_xattn_in['Wv'], 'L1_xattn_Wo': _L1_xattn_in['Wo'], 'L1_xattn_bo': _L1_xattn_in['bo'], 'L1_ffn_Wqkv': _L1_ffn_in['Wqkv'], 'L1_ffn_q_scale': _L1_ffn_in['q_scale'], 'L1_ffn_k_scale': _L1_ffn_in['k_scale'], 'L1_ffn_Wo': _L1_ffn_in['Wo'], 'L1_ffn_ln_g': _L1_ffn_in['ln_g'], 'L1_ffn_ln_b': _L1_ffn_in['ln_b'], 'L1_ffn_W1': _L1_ffn_in['W1'], 'L1_ffn_b1': _L1_ffn_in['b1'], 'L1_ffn_W2': _L1_ffn_in['W2'], 'L1_ffn_b2': _L1_ffn_in['b2'], 'L2_attn_norm_w': _L2_attn_in['norm_w'], 'L2_attn_W_in': _L2_attn_in['W_in'], 'L2_attn_conv_w': _L2_attn_in['conv_w'], 'L2_attn_conv_b': _L2_attn_in['conv_b'], 'L2_attn_W_dt': _L2_attn_in['W_dt'], 'L2_attn_b_dt': _L2_attn_in['b_dt'], 'L2_attn_W_B': _L2_attn_in['W_B'], 'L2_attn_W_C': _L2_attn_in['W_C'], 'L2_attn_A_log': _L2_attn_in['A_log'], 'L2_attn_D_param': _L2_attn_in['D_param'], 'L2_attn_W_out': _L2_attn_in['W_out'], 'L2_attn_residual_scale': _L2_attn_in['residual_scale'], 'L2_xattn_ln_gamma': _L2_xattn_in['ln_gamma'], 'L2_xattn_ln_beta': _L2_xattn_in['ln_beta'], 'L2_xattn_Wq': _L2_xattn_in['Wq'], 'L2_xattn_Wkv': _L2_xattn_in['Wkv'], 'L2_xattn_Wo': _L2_xattn_in['Wo'], 'L2_xattn_bo': _L2_xattn_in['bo'], 'L2_ffn_w1': _L2_ffn_in['w1'], 'L2_ffn_conv_w': _L2_ffn_in['conv_w'], 'L2_ffn_conv_b': _L2_ffn_in['conv_b'], 'L2_ffn_w2': _L2_ffn_in['w2'], 'L3_attn_Wq': _L3_attn_in['Wq'], 'L3_attn_bq': _L3_attn_in['bq'], 'L3_attn_Wk': _L3_attn_in['Wk'], 'L3_attn_bk': _L3_attn_in['bk'], 'L3_attn_Wv': _L3_attn_in['Wv'], 'L3_attn_bv': _L3_attn_in['bv'], 'L3_attn_Wp': _L3_attn_in['Wp'], 'L3_xattn_q_w': _L3_xattn_in['q_w'], 'L3_xattn_q_b': _L3_xattn_in['q_b'], 'L3_xattn_kv_w': _L3_xattn_in['kv_w'], 'L3_xattn_kv_b': _L3_xattn_in['kv_b'], 'L3_xattn_proj_w': _L3_xattn_in['proj_w'], 'L3_xattn_proj_b': _L3_xattn_in['proj_b'], 'L3_ffn_sw1': _L3_ffn_in['sw1'], 'L3_ffn_sw2': _L3_ffn_in['sw2'], 'L3_ffn_sw3': _L3_ffn_in['sw3'], 'L3_ffn_W1': _L3_ffn_in['W1'], 'L3_ffn_W2': _L3_ffn_in['W2'], 'L3_ffn_W3': _L3_ffn_in['W3'], 'L3_ffn_Wg': _L3_ffn_in['Wg']}

def reference(x, ctx_768, mask_BxS2_bf1, mask_1x1xSxS2_bk0, L0_attn_W, L0_attn_U, L0_attn_time_mix_k, L0_attn_time_mix_v, L0_attn_time_mix_r, L0_attn_Wk, L0_attn_Wv, L0_attn_Wr, L0_attn_Wo, L0_xattn_g_norm, L0_xattn_null_kv, L0_xattn_Wq, L0_xattn_Wkv, L0_xattn_Wout, L0_xattn_g_out, L0_ffn_w1_w, L0_ffn_w1_s, L0_ffn_w2_w, L0_ffn_w2_s, L0_ffn_h1_w, L0_ffn_h1_s, L0_ffn_h2_w, L0_ffn_h2_s, L0_ffn_w3_w, L0_ffn_w3_s, L1_attn_Wq, L1_attn_Wkv, L1_attn_Wo, L1_attn_bo, L1_attn_ln_g, L1_attn_ln_b, L1_xattn_Wq, L1_xattn_Wk, L1_xattn_Wv, L1_xattn_Wo, L1_xattn_bo, L1_ffn_Wqkv, L1_ffn_q_scale, L1_ffn_k_scale, L1_ffn_Wo, L1_ffn_ln_g, L1_ffn_ln_b, L1_ffn_W1, L1_ffn_b1, L1_ffn_W2, L1_ffn_b2, L2_attn_norm_w, L2_attn_W_in, L2_attn_conv_w, L2_attn_conv_b, L2_attn_W_dt, L2_attn_b_dt, L2_attn_W_B, L2_attn_W_C, L2_attn_A_log, L2_attn_D_param, L2_attn_W_out, L2_attn_residual_scale, L2_xattn_ln_gamma, L2_xattn_ln_beta, L2_xattn_Wq, L2_xattn_Wkv, L2_xattn_Wo, L2_xattn_bo, L2_ffn_w1, L2_ffn_conv_w, L2_ffn_conv_b, L2_ffn_w2, L3_attn_Wq, L3_attn_bq, L3_attn_Wk, L3_attn_bk, L3_attn_Wv, L3_attn_bv, L3_attn_Wp, L3_xattn_q_w, L3_xattn_q_b, L3_xattn_kv_w, L3_xattn_kv_b, L3_xattn_proj_w, L3_xattn_proj_b, L3_ffn_sw1, L3_ffn_sw2, L3_ffn_sw3, L3_ffn_W1, L3_ffn_W2, L3_ffn_W3, L3_ffn_Wg):
    import jax
    import jax.numpy as jnp

    def _L0_attn_ref(x, W, U, time_mix_k, time_mix_v, time_mix_r, Wk, Wv, Wr, Wo):
        import jax, jax.numpy as jnp
        import numpy as np
        import math
        D_MODEL = 128
        LAYER_ID = 6
        NUM_LAYERS = 12
        B, T = (8, 256)
        MIN_P = -1e+38

        def _init_params():
            C = D_MODEL
            r01 = LAYER_ID / (NUM_LAYERS - 1)
            r1a0 = 1.0 - LAYER_ID / NUM_LAYERS
            h = np.arange(C, dtype=np.float32)
            decay_speed = -5.0 + 8.0 * (h / (C - 1)) ** (0.7 + 1.3 * r01)
            zigzag = ((np.arange(C) + 1) % 3 - 1).astype(np.float32) * 0.5
            U = np.float32(math.log(0.3)) + zigzag
            xx = (np.arange(C, dtype=np.float32) / C).reshape(1, 1, C)
            tmk = xx ** r1a0
            tmv = xx ** r1a0 + 0.3 * r01
            tmr = xx ** (0.5 * r1a0)
            return (jnp.asarray(decay_speed), jnp.asarray(U), jnp.asarray(tmk, jnp.float32), jnp.asarray(tmv, jnp.float32), jnp.asarray(tmr, jnp.float32))

        def _wkv(W, U, k, v):
            w = -jnp.exp(W)
            Bb, Tt, Cc = k.shape
            aa0 = jnp.zeros((Bb, Cc), k.dtype)
            bb0 = jnp.zeros((Bb, Cc), k.dtype)
            pp0 = jnp.full((Bb, Cc), MIN_P, k.dtype)

            def step(carry, kv_t):
                aa, bb, pp = carry
                kt, vt = kv_t
                ww = U + kt
                p = jnp.maximum(pp, ww)
                e1 = jnp.exp(pp - p)
                e2 = jnp.exp(ww - p)
                y = (e1 * aa + e2 * vt) / (e1 * bb + e2)
                ww2 = pp + w
                p2 = jnp.maximum(ww2, kt)
                e1b = jnp.exp(ww2 - p2)
                e2b = jnp.exp(kt - p2)
                return ((e1b * aa + e2b * vt, e1b * bb + e2b, p2), y)
            kT = jnp.swapaxes(k, 0, 1)
            vT = jnp.swapaxes(v, 0, 1)
            _, yT = jax.lax.scan(step, (aa0, bb0, pp0), (kT, vT))
            return jnp.swapaxes(yT, 0, 1)

        def _reference_tuple_inner(x, W, U, time_mix_k, time_mix_v, time_mix_r, Wk, Wv, Wr, Wo):
            xs = jnp.pad(x, ((0, 0), (1, 0), (0, 0)))[:, :-1]
            xk = x * time_mix_k + xs * (1.0 - time_mix_k)
            xv = x * time_mix_v + xs * (1.0 - time_mix_v)
            xr = x * time_mix_r + xs * (1.0 - time_mix_r)
            K = jnp.einsum('btc,dc->btd', xk, Wk)
            V = jnp.einsum('btc,dc->btd', xv, Wv)
            R = jnp.einsum('btc,dc->btd', xr, Wr)
            wkv = _wkv(W, U, K, V)
            hidden = jax.lax.stop_gradient(wkv[:, -1, :])
            rwkv = jax.nn.sigmoid(R) * wkv
            output = jnp.einsum('btc,dc->btd', rwkv, Wo)
            return (output, hidden)
        return _reference_tuple_inner(x, W, U, time_mix_k, time_mix_v, time_mix_r, Wk, Wv, Wr, Wo)[0]

    def _L0_xattn_ref(x, context, mask, g_norm, null_kv, Wq, Wkv, Wout, g_out):
        import jax, jax.numpy as jnp
        import numpy as np
        import math
        B, N, M = (4, 128, 128)
        DIM, CTX_DIM = (128, 96)
        HEADS, DIM_HEAD = (16, 64)
        INNER = HEADS * DIM_HEAD

        def layer_norm(t, g, eps=1e-05):
            mean = jnp.mean(t, axis=-1, keepdims=True)
            var = jnp.mean((t - mean) ** 2, axis=-1, keepdims=True)
            return (t - mean) * jax.lax.rsqrt(var + eps) * g
        b = x.shape[0]
        scale = DIM_HEAD ** (-0.5)
        sqrt_scale = math.sqrt(scale)
        x = layer_norm(x, g_norm)
        q = x @ Wq
        kv = context @ Wkv
        k, v = jnp.split(kv, 2, axis=-1)

        def to_heads(t):
            return t.reshape(b, t.shape[1], HEADS, DIM_HEAD).transpose(0, 2, 1, 3)
        q, k, v = (to_heads(q), to_heads(k), to_heads(v))
        nk = jnp.broadcast_to(null_kv[0], (b, HEADS, 1, DIM_HEAD))
        nv = jnp.broadcast_to(null_kv[1], (b, HEADS, 1, DIM_HEAD))
        k = jnp.concatenate([nk, k], axis=2)
        v = jnp.concatenate([nv, v], axis=2)
        q = q * sqrt_scale
        k = k * sqrt_scale
        sim = jnp.einsum('bhid,bhjd->bhij', q, k)
        max_neg = -jnp.finfo(sim.dtype).max
        full_mask = jnp.pad(mask, ((0, 0), (1, 0)), constant_values=True)
        sim = jnp.where(full_mask[:, None, None, :], sim, max_neg)
        attn = jax.nn.softmax(sim.astype(jnp.float32), axis=-1).astype(sim.dtype)
        out = jnp.einsum('bhij,bhjd->bhid', attn, v)
        out = out.transpose(0, 2, 1, 3).reshape(b, -1, INNER)
        out = out @ Wout
        return layer_norm(out, g_out)

    def _L0_ffn_ref(x, w1_w, w1_s, w2_w, w2_s, h1_w, h1_s, h2_w, h2_s, w3_w, w3_s):
        import jax, jax.numpy as jnp
        import numpy as np
        D_IN, D_HID = (128, 512)

        def _ternary(key, shape):
            return jax.random.randint(key, shape, -1, 2).astype(jnp.float32)

        def _tlin(x, w, s):
            return jnp.einsum('bsi,oi->bso', x, w) * s
        h = jax.nn.silu(_tlin(x, w1_w, w1_s)) * _tlin(x, w2_w, w2_s)
        h = jax.nn.gelu(_tlin(h, h1_w, h1_s), approximate=False)
        h = jax.nn.gelu(_tlin(h, h2_w, h2_s), approximate=False)
        return _tlin(h, w3_w, w3_s)

    def _L1_attn_ref(x, Wq, Wkv, Wo, bo, ln_g, ln_b):
        import jax, jax.numpy as jnp
        import numpy as np
        B, SEQ, DIM = (2, 256, 128)
        H = 16
        DH = DIM // H
        LAT = 64
        CTX = SEQ - LAT
        SCALE = DH ** (-0.5)
        LN_EPS = 1e-05

        def _rotary_cos_sin(n):
            inv_freq = 1.0 / 10000.0 ** (jnp.arange(0, DH, 2, dtype=jnp.float32) / DH)
            freqs = jnp.arange(n, dtype=jnp.float32)[:, None] * inv_freq[None, :]
            emb = jnp.concatenate([freqs, freqs], axis=-1)
            return (jnp.cos(emb), jnp.sin(emb))

        def _rotate_half(t):
            t1, t2 = jnp.split(t, 2, axis=-1)
            return jnp.concatenate([-t2, t1], axis=-1)

        def _layernorm(t, g, b):
            m = jnp.mean(t, axis=-1, keepdims=True)
            v = jnp.var(t, axis=-1, keepdims=True)
            return (t - m) / jnp.sqrt(v + LN_EPS) * g + b
        b, n, d = x.shape
        neg = -jnp.finfo(x.dtype).max
        q = x @ Wq.T
        kv = x @ Wkv.T

        def split_heads(t):
            return t.reshape(b, n, H, DH).transpose(0, 2, 1, 3).reshape(b * H, n, DH)
        q = split_heads(q)
        kv = split_heads(kv)
        cos, sin = _rotary_cos_sin(n)
        q = q * cos + _rotate_half(q) * sin
        kv = kv * cos + _rotate_half(kv) * sin
        q_lat = q[:, CTX:] * SCALE
        q_ctx = q[:, :CTX] * SCALE
        lkv = _layernorm(kv, ln_g, ln_b)
        lkv_ctx = lkv[:, :CTX]
        lsim = jnp.einsum('bid,bjd->bij', q_lat, lkv)
        lat = n - CTX
        causal = jnp.triu(jnp.ones((lat, lat), dtype=bool), 1)
        mask = jnp.concatenate([jnp.zeros((lat, CTX), dtype=bool), causal], axis=-1)
        lsim = jnp.where(mask, neg, lsim)
        attn = jax.nn.softmax(lsim, axis=-1)
        out = jnp.einsum('bij,bjd->bid', attn, lkv)
        lsim_ctx = jnp.einsum('bid,bjd->bij', q_ctx, lkv_ctx)
        attn_ctx = jax.nn.softmax(lsim_ctx, axis=-1)
        out_ctx = jnp.einsum('bij,bjd->bid', attn_ctx, lkv_ctx)

        def merge_heads(t):
            m = t.shape[1]
            return t.reshape(b, H, m, DH).transpose(0, 2, 1, 3).reshape(b, m, H * DH)
        out_all = jnp.concatenate([merge_heads(out), merge_heads(out_ctx)], axis=1)
        return out_all @ Wo.T + bo

    def _L1_xattn_ref(x, context, Wq, Wk, Wv, Wo, bo):
        import jax, jax.numpy as jnp
        import numpy as np
        HEADS = 16
        DIM_HEAD = 64
        B, Nq, _ = x.shape
        Nk = context.shape[1]
        h, dh = (HEADS, DIM_HEAD)
        q = (x @ Wq).reshape(B, Nq, h, dh)
        k = (context @ Wk).reshape(B, Nk, h, dh)
        v = (context @ Wv).reshape(B, Nk, h, dh)
        scale = 1.0 / jnp.sqrt(jnp.asarray(dh, dtype=x.dtype))
        scores = jnp.einsum('bqhd,bkhd->bhqk', q, k) * scale
        attn = jax.nn.softmax(scores, axis=-1)
        out = jnp.einsum('bhqk,bkhd->bqhd', attn, v).reshape(B, Nq, h * dh)
        return out @ Wo + bo

    def _L1_ffn_ref(x, Wqkv, q_scale, k_scale, Wo, ln_g, ln_b, W1, b1, W2, b2):
        import jax, jax.numpy as jnp
        import numpy as np
        DIM = 128
        DEPTH = 6
        HEADS = 16
        DIM_HEAD = 64
        WINDOW = 32
        INNER = HEADS * DIM_HEAD
        DIM_INNER = int(DIM * 4 * 2 / 3)
        QK_SCALE = 8.0

        def shift_tokens(t):
            a, s = jnp.split(t, 2, -1)
            s = jnp.pad(s, ((0, 0), (1, 0), (0, 0)))[:, :-1]
            return jnp.concatenate([a, s], -1)

        def l2norm(t):
            return t / jnp.maximum(jnp.linalg.norm(t, axis=-1, keepdims=True), 1e-12)

        def rotate_half(x):
            x1, x2 = jnp.split(x, 2, -1)
            return jnp.concatenate([-x2, x1], -1)

        def rotary_tables(n):
            half = jnp.arange(0, DIM_HEAD, 2, dtype=jnp.float32)
            inv_freq = 1.0 / 10000.0 ** (half / DIM_HEAD)
            t = jnp.arange(n, dtype=jnp.float32)
            freqs = t[:, None] * inv_freq[None, :]
            freqs = jnp.concatenate([freqs, freqs], -1)
            base_scale = (half + 0.4 * DIM_HEAD) / (1.4 * DIM_HEAD)
            power = (t - n // 2) / (WINDOW // 2)
            scale = base_scale[None, :] ** power[:, None]
            scale = jnp.concatenate([scale, scale], -1)
            return (freqs, scale)

        def local_attention(q, k, v):
            b, h, n, d = q.shape
            w = WINDOW
            nw = n // w
            bq = q.reshape(b, h, nw, w, d)
            bk = k.reshape(b, h, nw, w, d)
            bv = v.reshape(b, h, nw, w, d)

            def look(t):
                p = jnp.pad(t, ((0, 0), (0, 0), (1, 0), (0, 0), (0, 0)))
                return jnp.concatenate([p[:, :, :nw], p[:, :, 1:]], axis=3)
            bk2, bv2 = (look(bk), look(bv))
            seq = jnp.arange(n).reshape(nw, w)
            seq_p = jnp.pad(seq, ((1, 0), (0, 0)), constant_values=-1)
            jt = jnp.concatenate([seq_p[:nw], seq_p[1:]], axis=1)
            it = seq[:, :, None]
            jb = jt[:, None, :]
            mask = (it < jb) | (it > jb + w) | (jb == -1)
            sim = jnp.einsum('bhwie,bhwje->bhwij', bq, bk2) * QK_SCALE
            sim = jnp.where(mask, -jnp.finfo(sim.dtype).max, sim)
            attn = jax.nn.softmax(sim, -1)
            out = jnp.einsum('bhwij,bhwje->bhwie', attn, bv2)
            return out.reshape(b, h, n, d)

        def attn_layer(x, Wqkv, qs, ksc, Wo):
            b, n, _ = x.shape
            qkv = x @ Wqkv
            q, k, v = jnp.split(qkv, 3, -1)
            sh = lambda t: t.reshape(b, n, HEADS, DIM_HEAD).transpose(0, 2, 1, 3)
            q, k, v = (sh(q), sh(k), sh(v))
            q = l2norm(q) * qs
            k = l2norm(k) * ksc
            freqs, scale = rotary_tables(n)
            cos, sin = (jnp.cos(freqs), jnp.sin(freqs))
            q = q * cos * scale + rotate_half(q) * sin * scale
            inv = 1.0 / scale
            k = k * cos * inv + rotate_half(k) * sin * inv
            out = local_attention(q, k, v)
            out = out.transpose(0, 2, 1, 3).reshape(b, n, INNER)
            return out @ Wo

        def ffn_layer(x, g, bln, W1, b1, W2, b2):
            mu = x.mean(-1, keepdims=True)
            var = ((x - mu) ** 2).mean(-1, keepdims=True)
            xn = (x - mu) / jnp.sqrt(var + 1e-05) * g + bln
            hg = xn @ W1 + b1
            a, gate = jnp.split(hg, 2, -1)
            return a * jax.nn.gelu(gate, approximate=False) @ W2 + b2
        for i in range(DEPTH):
            x = attn_layer(shift_tokens(x), Wqkv[i], q_scale[i], k_scale[i], Wo[i]) + x
            x = ffn_layer(shift_tokens(x), ln_g[i], ln_b[i], W1[i], b1[i], W2[i], b2[i]) + x
        return x

    def _L2_attn_ref(x, norm_w, W_in, conv_w, conv_b, W_dt, b_dt, W_B, W_C, A_log, D_param, W_out, residual_scale):
        import jax, jax.numpy as jnp
        import numpy as np
        D_MODEL = 128
        D_STATE = 16
        D_CONV = 4
        EXPAND = 2
        D_INNER = D_MODEL * EXPAND

        def soft_clamp(x, lo, hi, sharp):
            c = (hi + lo) / 2.0
            r = (hi - lo) / 2.0
            return jnp.tanh((x - c) / (r + 1e-08) * sharp) / sharp * r + c
        B, L, _ = x.shape
        var = jnp.mean(x * x, axis=-1, keepdims=True)
        xn = x * jax.lax.rsqrt(var + 1e-06) * norm_w
        proj = xn @ W_in.T
        x_branch, gate = (proj[..., :D_INNER], proj[..., D_INNER:])
        xc = jax.lax.conv_general_dilated(jnp.swapaxes(x_branch, 1, 2), conv_w, (1,), [(D_CONV - 1, 0)], dimension_numbers=('NCH', 'OIH', 'NCH'), feature_group_count=D_INNER)
        xc = xc + conv_b[None, :, None]
        xc = jnp.swapaxes(xc, 1, 2)
        xc = xc * jax.nn.sigmoid(xc)
        dt = soft_clamp(jax.nn.softplus(xc @ W_dt.T + b_dt), 0.001, 0.1, 0.5)
        Bp = xc @ W_B.T
        Cp = xc @ W_C.T
        A = -jnp.exp(soft_clamp(A_log, -5.0, 5.0, 0.5))
        dt_A = soft_clamp(dt[..., None] * A[None, None], -8.0, 8.0, 0.5)
        dA = jnp.exp(dt_A)
        dB = dt[..., None] * Bp[:, :, None, :]
        h0 = jnp.zeros((B, D_INNER, D_STATE), jnp.float32)

        def step(h, inp):
            dA_t, dB_t, x_t, C_t, t = inp
            h = h * dA_t + dB_t * x_t[:, :, None]
            nrm = jnp.sqrt(jnp.sum(h * h, axis=(1, 2), keepdims=True))
            fac = jnp.minimum(20.0 / (nrm + 1e-08), 1.0)
            h = jnp.where(t % 10 == 0, h * fac, h)
            y = jnp.einsum('bdn,bn->bd', h, C_t) + D_param * x_t
            return (h, y)
        xs = (jnp.swapaxes(dA, 0, 1), jnp.swapaxes(dB, 0, 1), jnp.swapaxes(xc, 0, 1), jnp.swapaxes(Cp, 0, 1), jnp.arange(L))
        _, ys = jax.lax.scan(step, h0, xs)
        x_ssm = jnp.swapaxes(ys, 0, 1)
        x_out = x_ssm * (gate * jax.nn.sigmoid(gate)) @ W_out.T
        scale = jax.nn.sigmoid(residual_scale) * 0.5
        return x + scale * x_out

    def _L2_xattn_ref(x, context, ln_gamma, ln_beta, Wq, Wkv, Wo, bo, mask):
        import jax, jax.numpy as jnp
        import numpy as np
        B, T, Q_DIM, KV_DIM = (4, 256, 128, 96)
        HEADS, DIM_HEAD = (16, 64)
        INNER = HEADS * DIM_HEAD
        NUM_FRAMES, NUM_PATCHES = (8, 32)
        LN_EPS = 1e-05

        def diagonal_frame_mask(num_patches, num_frames):
            fid = np.repeat(np.arange(num_frames), num_patches)
            m = fid[:, None] == fid[None, :]
            return jnp.asarray(m[None, None])
        mu = jnp.mean(x, axis=-1, keepdims=True)
        var = jnp.mean(jnp.square(x - mu), axis=-1, keepdims=True)
        xn = (x - mu) * jax.lax.rsqrt(var + LN_EPS) * ln_gamma + ln_beta
        scale = DIM_HEAD ** (-0.5)
        q = xn @ Wq
        kv = context @ Wkv
        k, v = jnp.split(kv, 2, axis=-1)
        split_heads = lambda t: t.reshape(t.shape[0], t.shape[1], HEADS, DIM_HEAD).transpose(0, 2, 1, 3)
        q, k, v = (split_heads(q), split_heads(k), split_heads(v))
        dots = jnp.einsum('bhnd,bhmd->bhnm', q, k) * scale
        dots = jnp.where(mask, dots, -jnp.inf)
        attn = jax.nn.softmax(dots, axis=-1)
        out = jnp.einsum('bhnm,bhmd->bhnd', attn, v)
        out = out.transpose(0, 2, 1, 3).reshape(x.shape[0], x.shape[1], INNER)
        return out @ Wo + bo

    def _L2_ffn_ref(x, w1, conv_w, conv_b, w2):
        import jax, jax.numpy as jnp
        import numpy as np
        B, S, D_MODEL, D_HIDDEN = (4, 256, 128, 512)

        def act_quant(x):
            scale = 127.0 / jnp.clip(jnp.max(jnp.abs(x), axis=-1, keepdims=True), 1e-05)
            return jnp.clip(jnp.round(x * scale), -128, 127) / scale

        def weight_quant(w):
            scale = 1.0 / jnp.clip(jnp.mean(jnp.abs(w)), 1e-05)
            return jnp.clip(jnp.round(w * scale), -1, 1) / scale

        def bit_linear(x, w):
            xq = x + jax.lax.stop_gradient(act_quant(x) - x)
            wq = w + jax.lax.stop_gradient(weight_quant(w) - w)
            return jnp.einsum('bsd,hd->bsh', xq, wq)

        def depthwise_conv1d(x_bcl, w, b):
            y = jax.lax.conv_general_dilated(x_bcl, w, window_strides=(1,), padding=[(1, 1)], dimension_numbers=('NCH', 'OIH', 'NCH'), feature_group_count=x_bcl.shape[1])
            return y + b[None, :, None]
        h = bit_linear(x, w1)
        h = depthwise_conv1d(h.transpose(0, 2, 1), conv_w, conv_b)
        h = h.transpose(0, 2, 1)
        h = jax.nn.silu(h)
        return bit_linear(h, w2)

    def _L3_attn_ref(x, Wq, bq, Wk, bk, Wv, bv, Wp):
        import jax, jax.numpy as jnp
        import numpy as np
        import math
        EMBED = 128
        HEADS = 16
        HEAD_DIM = EMBED // HEADS
        B, N = (2, 256)
        Bb, Nn, E = x.shape
        H, D = (HEADS, HEAD_DIM)
        q = (x @ Wq + bq).reshape(Bb, Nn, H, D)
        k = (x @ Wk + bk).reshape(Bb, Nn, H, D)
        v = (x @ Wv + bv).reshape(Bb, Nn, H, D)
        q = jnp.einsum('bnhe,ei->bnhi', q, Wp)
        k = jnp.einsum('bnhe,ei->bnhi', k, Wp)
        scores = jnp.einsum('bnhi,bmhi->bnhm', q, k) / math.sqrt(D)
        attn = jax.nn.softmax(scores, axis=-1)
        out = jnp.einsum('bnhm,bmhe->bnhe', attn, v).reshape(Bb, Nn, E)
        return out

    def _L3_xattn_ref(x, cond, q_w, q_b, kv_w, kv_b, proj_w, proj_b):
        import jax, jax.numpy as jnp
        import numpy as np
        NUM_HEADS = 16
        B, N, C = x.shape
        condN = cond.shape[1]
        H = NUM_HEADS
        hd = C // H
        scale = hd ** (-0.5)
        q = (x @ q_w + q_b).reshape(B, N, H, hd).transpose(0, 2, 1, 3)
        kv = (cond @ kv_w + kv_b).reshape(B, condN, 2, H, hd)
        k = kv[:, :, 0].transpose(0, 2, 1, 3)
        v = kv[:, :, 1].transpose(0, 2, 1, 3)
        attn = jnp.einsum('bhnd,bhmd->bhnm', q * scale, k)
        attn = jax.nn.softmax(attn, axis=-1)
        out = jnp.einsum('bhnm,bhmd->bhnd', attn, v)
        out = out.transpose(0, 2, 1, 3).reshape(B, N, C)
        return out @ proj_w + proj_b

    def _L3_ffn_ref(h, sw1, sw2, sw3, W1, W2, W3, Wg):
        import jax, jax.numpy as jnp
        import numpy as np
        D = 128
        H = 256
        E = 8
        K = 2
        B, S = (4, 256)

        def _ffn(x, w1, w2, w3):
            return jax.nn.silu(x @ w1.T) * (x @ w3.T) @ w2.T
        b, s, d = h.shape
        hf = h.reshape(-1, d)
        T = hf.shape[0]
        shared_y = _ffn(hf, sw1, sw2, sw3)
        scores = jax.nn.softmax(hf @ Wg.T, axis=-1)
        vals, ids = jax.lax.top_k(scores, K)
        w = vals / vals.sum(axis=-1, keepdims=True)
        combine = jnp.zeros((T, E), hf.dtype).at[jnp.arange(T)[:, None], ids].add(w)
        y = shared_y
        for e in range(E):
            y = y + combine[:, e:e + 1] * _ffn(hf, W1[e], W2[e], W3[e])
        return y.reshape(b, s, d)
    x = _layernorm(x + _L0_attn_ref(x, L0_attn_W, L0_attn_U, L0_attn_time_mix_k, L0_attn_time_mix_v, L0_attn_time_mix_r, L0_attn_Wk, L0_attn_Wv, L0_attn_Wr, L0_attn_Wo), axis=-1)
    x = _layernorm(x + _L0_xattn_ref(x, ctx_768, mask_BxS2_bf1, L0_xattn_g_norm, L0_xattn_null_kv, L0_xattn_Wq, L0_xattn_Wkv, L0_xattn_Wout, L0_xattn_g_out), axis=-1)
    x = _layernorm(x + _L0_ffn_ref(x, L0_ffn_w1_w, L0_ffn_w1_s, L0_ffn_w2_w, L0_ffn_w2_s, L0_ffn_h1_w, L0_ffn_h1_s, L0_ffn_h2_w, L0_ffn_h2_s, L0_ffn_w3_w, L0_ffn_w3_s), axis=-1)
    x = _layernorm(x + _L1_attn_ref(x, L1_attn_Wq, L1_attn_Wkv, L1_attn_Wo, L1_attn_bo, L1_attn_ln_g, L1_attn_ln_b), axis=-1)
    x = _layernorm(x + _L1_xattn_ref(x, ctx_768, L1_xattn_Wq, L1_xattn_Wk, L1_xattn_Wv, L1_xattn_Wo, L1_xattn_bo), axis=-1)
    x = _layernorm(x + _L1_ffn_ref(x, L1_ffn_Wqkv, L1_ffn_q_scale, L1_ffn_k_scale, L1_ffn_Wo, L1_ffn_ln_g, L1_ffn_ln_b, L1_ffn_W1, L1_ffn_b1, L1_ffn_W2, L1_ffn_b2), axis=-1)
    x = _layernorm(x + _L2_attn_ref(x, L2_attn_norm_w, L2_attn_W_in, L2_attn_conv_w, L2_attn_conv_b, L2_attn_W_dt, L2_attn_b_dt, L2_attn_W_B, L2_attn_W_C, L2_attn_A_log, L2_attn_D_param, L2_attn_W_out, L2_attn_residual_scale), axis=-1)
    x = _layernorm(x + _L2_xattn_ref(x, ctx_768, L2_xattn_ln_gamma, L2_xattn_ln_beta, L2_xattn_Wq, L2_xattn_Wkv, L2_xattn_Wo, L2_xattn_bo, mask_1x1xSxS2_bk0), axis=-1)
    x = _layernorm(x + _L2_ffn_ref(x, L2_ffn_w1, L2_ffn_conv_w, L2_ffn_conv_b, L2_ffn_w2), axis=-1)
    x = _layernorm(x + _L3_attn_ref(x, L3_attn_Wq, L3_attn_bq, L3_attn_Wk, L3_attn_bk, L3_attn_Wv, L3_attn_bv, L3_attn_Wp), axis=-1)
    x = _layernorm(x + _L3_xattn_ref(x, ctx_768, L3_xattn_q_w, L3_xattn_q_b, L3_xattn_kv_w, L3_xattn_kv_b, L3_xattn_proj_w, L3_xattn_proj_b), axis=-1)
    x = _layernorm(x + _L3_ffn_ref(x, L3_ffn_sw1, L3_ffn_sw2, L3_ffn_sw3, L3_ffn_W1, L3_ffn_W2, L3_ffn_W3, L3_ffn_Wg), axis=-1)
    return x

_drawn_inputs = setup_inputs


def setup_inputs(seed=0):
    import zlib

    import numpy as np

    out = dict(_drawn_inputs(seed))
    spreads = {'L0_xattn_g_norm': (1.0, 0.2),
     'L0_xattn_g_out': (1.0, 0.2),
     'L1_attn_bo': (0.0, 0.1),
     'L1_attn_ln_g': (1.0, 0.6),
     'L1_attn_ln_b': (0.0, 0.553),
     'L1_ffn_q_scale': (1.0, 0.6),
     'L1_ffn_k_scale': (1.0, 0.6),
     'L1_ffn_ln_g': (1.0, 0.6),
     'L1_ffn_ln_b': (0.0, 0.8),
     'L1_ffn_b1': (0.0, 0.8),
     'L1_ffn_b2': (0.0, 0.1),
     'L2_attn_norm_w': (1.0, 0.6),
     'L2_attn_conv_b': (0.0, 0.8),
     'L2_attn_b_dt': (-2.0, 0.6),
     'L2_attn_D_param': (0.10000000149011612, 0.6),
     'L2_xattn_ln_gamma': (1.0, 0.2),
     'L2_xattn_ln_beta': (0.0, 0.304),
     'L2_xattn_bo': (0.0, 0.1),
     'L3_xattn_q_b': (0.0, 0.396),
     'L3_xattn_kv_b': (0.0, 0.1),
     'L3_xattn_proj_b': (0.0, 0.1)}
    factors = {'L0_attn_U': 3.117,
     'L0_attn_time_mix_r': 3.384,
     'L0_xattn_null_kv': 3.253,
     'L0_ffn_w1_w': 8.0,
     'L0_ffn_w1_s': 8.0,
     'L0_ffn_w2_w': 8.0,
     'L0_ffn_w2_s': 8.0,
     'L0_ffn_h1_w': 8.0,
     'L0_ffn_h1_s': 8.0,
     'L0_ffn_h2_w': 8.0,
     'L0_ffn_h2_s': 8.0,
     'L0_ffn_w3_w': 8.0,
     'L0_ffn_w3_s': 8.0,
     'L1_attn_Wq': 3.422,
     'L1_xattn_bo': 6.689,
     'L1_ffn_W1': 4.155,
     'L1_ffn_W2': 4.177,
     'L2_attn_W_in': 8.0,
     'L2_attn_conv_w': 8.0,
     'L2_attn_W_dt': 8.0,
     'L2_attn_W_B': 8.0,
     'L2_attn_W_C': 8.0,
     'L2_attn_A_log': 8.0,
     'L2_attn_W_out': 8.0,
     'L3_attn_bq': 4.11,
     'L3_attn_bk': 8.0,
     'L3_ffn_sw1': 7.195,
     'L3_ffn_sw2': 6.924,
     'L3_ffn_sw3': 7.066,
     'L3_ffn_W1': 8.0,
     'L3_ffn_W2': 8.0,
     'L3_ffn_W3': 8.0,
     'L3_ffn_Wg': 8.0}
    for name, (base, spread) in spreads.items():
        noise = np.random.default_rng([zlib.crc32(name.encode()), seed]).standard_normal(out[name].shape)
        drawn = base * np.exp(spread * noise) if base else spread * noise
        out[name] = jnp.asarray(drawn.astype(out[name].dtype))
    for name, factor in factors.items():
        out[name] = (out[name] * factor).astype(out[name].dtype)
    return out
```

```python
from contextlib import ExitStack, contextmanager
import math

import numpy as np

import concourse.bass as bass
from concourse import mybir

P = 128
B, S, D = 4, 512, 128
TILE = 128
QT = S // TILE
CTX_LEN, CTX_D = 154, 96
HEADS = 16
DH = 64
INNER = HEADS * DH
CHUNKS = INNER // P
SH = D // HEADS
LAT = S - (256 - 64)
DEPTH = 6
WINDOW = 32
LOCAL_KEYS = WINDOW + TILE
FFN_INNER = int(D * 4 * 2 / 3)
SSM_D, SSM_N, CONV = 256, 16, 4
EXPERTS, EXPERT_H = 8, 256
LN_EPS = 1e-5
MASKED = -1e30
PAD = 4

F32 = mybir.dt.float32
U8 = mybir.dt.uint8
U32 = mybir.dt.uint32
ALU = mybir.AluOpType
ACT = mybir.ActivationFunctionType
AX_X = mybir.AxisListType.X


class Chain:

    def __init__(self, eng, sem):
        self.eng, self.sem, self.steps = eng, sem, 0

    def __call__(self, ins):
        self.steps += 1
        ins.then_inc(self.sem, 1)
        self.eng.wait_ge(self.sem, self.steps)


class Stage:

    def __init__(self, block, bank, stale):
        self.block, self.bank, self.stale, self.used = block, bank, stale, 0

    def sem(self, name):
        self.used += 1
        return self.bank[self.used - 1]


class Core:

    BANK = 28

    def __init__(self, nc, ctx, dram, cols):
        self.nc, self.ctx, self.dram, self.cols = nc, ctx, dram, cols
        self.parity = 0
        self.banks = [[ctx.enter_context(nc.semaphore(f"bank{i}_{j}")) for j in range(self.BANK)]
                      for i in range(2)]
        self.spans = [range(bank[0].num, bank[-1].num + 1) for bank in self.banks]
        self.loaded = [ctx.enter_context(nc.semaphore(f"weights_loaded{i}")) for i in range(2)]
        self.resident_loaded = ctx.enter_context(nc.semaphore("resident_loaded"))
        self.tokens_loaded = ctx.enter_context(nc.semaphore("tokens_loaded"))
        self.stored = ctx.enter_context(nc.semaphore("stored"))
        self.ps = [ctx.enter_context(nc.psum_tensor(f"ps{i}", [P, 512], F32)) for i in range(8)]
        self.XP = self.buf("XP", [P, PAD + S])
        self.X = self.XP[:, PAD:PAD + S]
        self.Y = self.buf("Y", [P, S])
        self.ctxT = self.buf("ctxT", [CTX_D, CTX_LEN])
        self.const = self.buf("const", [P, cols["const"]["width"]])
        self.rwkv = self.buf("rwkv", [P, cols["L0a"]["width"]])
        self.arena_width = max(v["width"] for k, v in cols.items() if k not in ("const", "L0a"))
        self.arenas = [self.buf(f"arena{i}", [P, self.arena_width]) for i in range(2)]
        self.ident = self.c("ident")
        self.average = self.c("average")

    def buf(self, name, shape, dt=F32):
        return self.ctx.enter_context(self.nc.sbuf_tensor(name, shape, dt))

    def c(self, name):
        lo, hi = self.cols["const"][name]
        return self.const[:, lo:hi]

    def weights(self, pack, arena):
        mem = self.rwkv if arena is None else self.arenas[arena]

        def view(name, a=0, b=None):
            lo, hi = self.cols[pack][name]
            return mem[:, lo + a:(hi if b is None else lo + b)]
        return view

    @contextmanager
    def stage(self):
        self.parity ^= 1
        with self.nc.Block() as block:
            yield Stage(block, self.banks[self.parity], self.spans[1 - self.parity])


def turn(core, arena, prefetch):
    with core.nc.Block() as block:
        @block.sync
        def _(sp):
            for span in core.spans:
                sp.sem_clear(span)
            sp.wait_ge(core.loaded[arena], 16)
            sp.sem_clear(core.loaded[arena])
            if prefetch is not None:
                width = prefetch.shape[-1]
                sp.dma_start(core.arenas[1 - arena][:, 0:width], prefetch).then_inc(core.loaded[1 - arena], 16)


def normalize(core, src, dst, add=None, gain=None, shift=None, centred=True, eps=LN_EPS):
    nc = core.nc
    with core.stage() as st, ExitStack() as mem:
        z, d, sq, std = (mem.enter_context(nc.sbuf_tensor(f"norm_{n}_{core.nc.next_id()}", [P, S], F32)) for n in ("z", "d", "sq", "std"))
        epsc = mem.enter_context(nc.sbuf_tensor(f"norm_eps_{core.nc.next_id()}", [P, 1], F32))
        z_ready, mean_ready, d_ready = st.sem("z_ready"), st.sem("mean_ready"), st.sem("d_ready")
        sq_ready, var_ready, std_ready = st.sem("sq_ready"), st.sem("var_ready"), st.sem("std_ready")
        dve_step, eps_ready = st.sem("dve_step"), st.sem("eps_ready")
        mean, var = core.ps[0], core.ps[1]
        summed = z[:, :] if add is not None else src
        centre = d[:, :] if centred else summed

        @st.block.sync
        def _(sp):
            sp.sem_clear(st.stale)

        @st.block.gpsimd
        def _(pool):
            nc.gpsimd.memset(epsc[:, :], eps).then_inc(eps_ready, 1)

        @st.block.vector
        def _(dve):
            link = Chain(dve, dve_step)
            if add is not None:
                nc.vector.tensor_tensor(summed, src, add, ALU.add).then_inc(z_ready, 1)
                dve.wait_ge(z_ready, 1)
            if centred:
                dve.wait_ge(mean_ready, 1)
                nc.vector.tensor_tensor(centre, summed, mean[:, :], ALU.subtract).then_inc(d_ready, 1)
                dve.wait_ge(d_ready, 1)
            dve.wait_ge(std_ready, 1)
            link(nc.vector.reciprocal(std[:, :], std[:, :]))
            if gain is None:
                link(nc.vector.tensor_tensor(dst, centre, std[:, :], ALU.mult))
            elif shift is None:
                link(nc.vector.scalar_tensor_tensor(out=dst, in0=centre, scalar=gain, in1=std[:, :],
                                                    op0=ALU.mult, op1=ALU.mult))
            else:
                link(nc.vector.tensor_tensor(std[:, :], centre, std[:, :], ALU.mult))
                link(nc.vector.tensor_scalar(dst, std[:, :], gain, shift, ALU.mult, ALU.add))

        @st.block.tensor
        def _(pe):
            if add is not None:
                pe.wait_ge(z_ready, 1)
            if centred:
                nc.tensor.matmul(mean[:, :], core.average, summed, start=True, stop=True).then_inc(mean_ready, 1)
            pe.wait_ge(sq_ready, 1)
            nc.tensor.matmul(var[:, :], core.average, sq[:, :], start=True, stop=True).then_inc(var_ready, 1)

        @st.block.scalar
        def _(act):
            if centred:
                act.wait_ge(d_ready, 1)
            elif add is not None:
                act.wait_ge(z_ready, 1)
            nc.scalar.activation(sq[:, :], centre, ACT.Square).then_inc(sq_ready, 1)
            act.wait_ge(eps_ready, 1)
            act.wait_ge(var_ready, 1)
            nc.scalar.activation(std[:, :], var[:, :], ACT.Sqrt, bias=epsc[:, 0:1]).then_inc(std_ready, 1)


def dense(core, count, w, rhs, dst, kcount=1, func=None, scale=None, bias=None, n=S, also=None):
    nc = core.nc
    with core.stage() as st:
        product_ready = st.sem("product_ready")
        act_done, dve_done = st.sem("act_done"), st.sem("dve_done")
        BANKS = 6

        def on_scalar(m):
            return func is not None or m % 2 == 0

        @st.block.sync
        def _(sp):
            sp.sem_clear(st.stale)

        @st.block.tensor
        def _(pe):
            for m in range(count):
                if m >= BANKS:
                    if func is not None:
                        pe.wait_ge(act_done, m - BANKS + 1)
                    else:
                        pe.wait_ge(act_done if m % 2 == 0 else dve_done, (m - BANKS) // 2 + 1)
                for k in range(kcount):
                    lhs = w(k, m)
                    mm = nc.tensor.matmul(core.ps[m % BANKS][0:lhs.shape[-1], 0:n], lhs, rhs(k),
                                          start=(k == 0), stop=(k == kcount - 1))
                mm.then_inc(product_ready, 1)

        @st.block.scalar
        def _(act):
            for m in range(count):
                if on_scalar(m):
                    out = dst(m)
                    act.wait_ge(product_ready, m + 1)
                    nc.scalar.activation(out, core.ps[m % BANKS][0:out.shape[0], 0:n], func or ACT.Identity,
                                         bias=0.0 if bias is None else bias(m),
                                         scale=1.0 if scale is None else scale(m)).then_inc(act_done, 1)

        @st.block.vector
        def _(dve):
            for m in range(count):
                if not on_scalar(m):
                    out = dst(m)
                    dve.wait_ge(product_ready, m + 1)
                    nc.vector.tensor_scalar(out, core.ps[m % BANKS][0:out.shape[0], 0:n],
                                            1.0 if scale is None else scale(m),
                                            0.0 if bias is None else bias(m), ALU.mult, ALU.add).then_inc(dve_done, 1)


def gated(core, count, w_act, w_lin, rhs, dst, func, act_scale=None, act_bias=None, lin_op=ALU.mult, lin=None):
    nc = core.nc
    with core.stage() as st, nc.sbuf_tensor(f"gate_{nc.next_id()}", [P, 2, S], F32) as gate:
        products_ready, gate_ready, gated_ready = st.sem("products"), st.sem("gate"), st.sem("gated")

        @st.block.sync
        def _(sp):
            sp.sem_clear(st.stale)

        @st.block.tensor
        def _(pe):
            for m in range(count):
                if m >= 3:
                    pe.wait_ge(gated_ready, m - 2)
                for i, w in enumerate((w_act, w_lin)):
                    lhs = w(m)
                    mm = nc.tensor.matmul(core.ps[2 * (m % 3) + i][0:lhs.shape[-1], :], lhs, rhs,
                                          start=True, stop=True)
                mm.then_inc(products_ready, 1)

        @st.block.scalar
        def _(act):
            for m in range(count):
                rows = dst(m).shape[0]
                act.wait_ge(products_ready, m + 1)
                if m >= 2:
                    act.wait_ge(gated_ready, m - 1)
                nc.scalar.activation(gate[0:rows, m % 2, :], core.ps[2 * (m % 3)][0:rows, :], func,
                                     bias=0.0 if act_bias is None else act_bias(m),
                                     scale=1.0 if act_scale is None else act_scale(m)).then_inc(gate_ready, 1)

        @st.block.vector
        def _(dve):
            for m in range(count):
                out = dst(m)
                rows = out.shape[0]
                dve.wait_ge(gate_ready, m + 1)
                nc.vector.scalar_tensor_tensor(out=out, in0=core.ps[2 * (m % 3) + 1][0:rows, :],
                                               scalar=1.0 if lin is None else lin(m), in1=gate[0:rows, m % 2, :],
                                               op0=lin_op, op1=ALU.mult).then_inc(gated_ready, 1)


def residual_norm(core):
    normalize(core, core.X, core.X, add=core.Y[:, :])



def rwkv(core):
    nc = core.nc
    w = core.weights("L0a", None)
    X, Xs = core.X, core.XP[:, PAD - 1:PAD - 1 + S]
    with ExitStack() as mem:
        def tmp(name, width=S):
            return mem.enter_context(nc.sbuf_tensor(f"rwkv_{name}", [P, width], F32))
        diff, xk, xv, xr, k, v, r = (tmp(n) for n in ("diff", "xk", "xv", "xr", "k", "v", "r"))
        decay = tmp("decay", 2)
        with core.stage() as st:
            mixed, product_ready, dve_step, evac = (st.sem(n) for n in ("mixed", "product_ready", "dve_step", "evac"))

            @st.block.sync
            def _(sp):
                sp.sem_clear(st.stale)

            @st.block.vector
            def _(dve):
                link = Chain(dve, dve_step)
                link(nc.vector.tensor_tensor(diff[:, :], X, Xs, ALU.subtract))
                for out, mix in ((xk, "mix_k"), (xv, "mix_v"), (xr, "mix_r")):
                    nc.vector.scalar_tensor_tensor(out=out[:, :], in0=diff[:, :], scalar=w(mix), in1=Xs,
                                                   op0=ALU.mult, op1=ALU.add).then_inc(mixed, 1)
                dve.wait_ge(evac, 1)
                nc.vector.tensor_scalar(decay[:, 1:2], decay[:, 0:1], -1.0, None, ALU.mult).then_inc(dve_step, 1)

            @st.block.tensor
            def _(pe):
                for i, (src, name) in enumerate(((xk, "Wk"), (xv, "Wv"), (xr, "Wr"))):
                    pe.wait_ge(mixed, i + 1)
                    nc.tensor.matmul(core.ps[i][:, :], w(name), src[:, :], start=True, stop=True)\
                      .then_inc(product_ready, 1)

            @st.block.scalar
            def _(act):
                nc.scalar.activation(decay[:, 0:1], w("W"), ACT.Exp).then_inc(evac, 1)
                for i, (dst, f) in enumerate(((k, ACT.Copy), (v, ACT.Copy), (r, ACT.Sigmoid))):
                    act.wait_ge(product_ready, i + 1)
                    nc.scalar.activation(dst[:, :], core.ps[i][:, :], f).then_inc(evac, 1)

        PP, AA, BB = (tmp(n, S + 1) for n in ("PP", "AA", "BB"))
        e1b, e2b, e1, e2, kv, pmax, num = (tmp(n) for n in ("e1b", "e2b", "e1", "e2", "kv", "pmax", "num"))
        with core.stage() as st:
            args_ready, exp_ready, dve_step = (st.sem(n) for n in ("args_ready", "exp_ready", "dve_step"))
            before, now = slice(0, S), slice(1, S + 1)
            neg_decay = decay[:, 1:2]

            @st.block.sync
            def _(sp):
                sp.sem_clear(st.stale)

            @st.block.vector
            def _(dve):
                link = Chain(dve, dve_step)
                link(nc.vector.memset(PP[:, 0:1], -1e38))
                link(nc.vector.memset(AA[:, 0:1], 0.0))
                link(nc.vector.memset(BB[:, 0:1], 0.0))
                link(nc.vector.tensor_tensor_scan(PP[:, now], neg_decay.broadcast_to([P, S]), k[:, :], -1e38,
                                                  ALU.add, ALU.max))
                nc.vector.scalar_tensor_tensor(out=e1b[:, :], in0=PP[:, before], scalar=neg_decay, in1=PP[:, now],
                                               op0=ALU.add, op1=ALU.subtract).then_inc(args_ready, 1)
                nc.vector.tensor_tensor(e2b[:, :], k[:, :], PP[:, now], ALU.subtract).then_inc(args_ready, 1)
                link(nc.vector.scalar_tensor_tensor(out=pmax[:, :], in0=k[:, :], scalar=w("U"), in1=PP[:, before],
                                                    op0=ALU.add, op1=ALU.max))
                nc.vector.tensor_tensor(e1[:, :], PP[:, before], pmax[:, :], ALU.subtract).then_inc(args_ready, 1)
                nc.vector.scalar_tensor_tensor(out=e2[:, :], in0=k[:, :], scalar=w("U"), in1=pmax[:, :],
                                               op0=ALU.add, op1=ALU.subtract).then_inc(args_ready, 1)
                dve.wait_ge(exp_ready, 2)
                link(nc.vector.tensor_tensor(kv[:, :], e2b[:, :], v[:, :], ALU.mult))
                link(nc.vector.tensor_tensor_scan(AA[:, now], e1b[:, :], kv[:, :], 0.0, ALU.mult, ALU.add))
                link(nc.vector.tensor_tensor_scan(BB[:, now], e1b[:, :], e2b[:, :], 0.0, ALU.mult, ALU.add))
                dve.wait_ge(exp_ready, 4)
                link(nc.vector.tensor_tensor(num[:, :], e1[:, :], AA[:, before], ALU.mult))
                link(nc.vector.tensor_tensor(kv[:, :], e2[:, :], v[:, :], ALU.mult))
                link(nc.vector.tensor_tensor(num[:, :], num[:, :], kv[:, :], ALU.add))
                link(nc.vector.tensor_tensor(kv[:, :], e1[:, :], BB[:, before], ALU.mult))
                link(nc.vector.tensor_tensor(kv[:, :], kv[:, :], e2[:, :], ALU.add))
                link(nc.vector.reciprocal(kv[:, :], kv[:, :]))
                link(nc.vector.tensor_tensor(num[:, :], num[:, :], kv[:, :], ALU.mult))
                link(nc.vector.tensor_tensor(num[:, :], num[:, :], r[:, :], ALU.mult))

            @st.block.scalar
            def _(act):
                for i, e in enumerate((e1b, e2b, e1, e2)):
                    act.wait_ge(args_ready, i + 1)
                    nc.scalar.activation(e[:, :], e[:, :], ACT.Exp).then_inc(exp_ready, 1)

        dense(core, 1, lambda j, m: w("Wo"), lambda j: num[:, :], lambda m: core.Y[:, :])
    residual_norm(core)



def attention_tile(core, qt, dh, q_of, k_of, v_of, key_parts, bias=None, bias_cols=None, w_out=None, out_bias=None,
                   mid_bias=None):
    nc = core.nc
    keys = sum(n for _, n in key_parts)
    even_parts = len({n for _, n in key_parts}) == 1
    width = HEADS * dh
    chunks = width // P
    with core.stage() as st, ExitStack() as mem:
        def tmp(name, shape):
            return mem.enter_context(nc.sbuf_tensor(f"attn_{name}_{nc.next_id()}", shape, F32))
        SC, PT, OUT, PROJ = core.ps[0:3], core.ps[3:5], core.ps[5:7], core.ps[7]
        probs = tmp("probs", [P, 3, keys])
        pts = tmp("pts", [P, 2, len(key_parts), P])
        negmax, total, recip = tmp("negmax", [P, HEADS]), tmp("total", [P, HEADS]), tmp("recip", [P, HEADS])
        osb = tmp("osb", [P, width])
        oT = tmp("oT", [P, chunks, P])
        scores_ready, max_ready, probs_ready = (st.sem(n) for n in ("scores_ready", "max_ready", "probs_ready"))
        turned, turned_act, turned_dve = (st.sem(n) for n in ("turned", "turned_act", "turned_dve"))
        heads_done, dve_step, out_ready, out_turned, outT_ready, projected, y_ready = (
            st.sem(n) for n in ("heads_done", "dve_step", "out_ready", "out_turned", "outT_ready", "projected",
                                "y_ready"))
        copies = 1 if even_parts else len(key_parts)

        def copy_turned(op, h, sem):
            if even_parts:
                n = key_parts[0][1]
                op(pts[0:n, h % 2, :, :], PT[h % 2][0:n, 0:len(key_parts) * P]
                   .rearrange("p (c q) -> p c q", q=P)).then_inc(sem, 1)
            else:
                for i, (_, n) in enumerate(key_parts):
                    op(pts[0:n, h % 2, i, :], PT[h % 2][0:n, i * P:(i + 1) * P]).then_inc(sem, 1)

        @st.block.sync
        def _(sp):
            sp.sem_clear(st.stale)

        @st.block.tensor
        def _(pe):
            for u in range(HEADS + 2):
                if u < HEADS:
                    if u >= 3:
                        pe.wait_ge(probs_ready, u - 2)
                    nc.tensor.matmul(SC[u % 3][:, 0:keys], q_of(u), k_of(u), start=True, stop=True)\
                      .then_inc(scores_ready, 1)
                if 1 <= u <= HEADS:
                    h = u - 1
                    pe.wait_ge(probs_ready, h + 1)
                    if h >= 2:
                        pe.wait_ge(turned_act if h % 2 else turned_dve, copies * (h // 2))
                    for i, (first, n) in enumerate(key_parts):
                        mm = nc.tensor.transpose(PT[h % 2][0:n, i * P:(i + 1) * P],
                                                 probs[:, h % 3, first:first + n], core.ident)
                    mm.then_inc(turned, 1)
                if u >= 2:
                    h = u - 2
                    pe.wait_ge(turned_act if h % 2 else turned_dve, copies * (h // 2 + 1))
                    col = h * dh
                    for i, (_, n) in enumerate(key_parts):
                        mm = nc.tensor.matmul(OUT[col // 512][:, col % 512:col % 512 + dh],
                                              pts[0:n, h % 2, i, :], v_of(h, i),
                                              start=(i == 0), stop=(i == len(key_parts) - 1))
                    mm.then_inc(heads_done, 1)
            pe.wait_ge(out_ready, (width + 511) // 512)
            for c in range(chunks):
                mm = nc.tensor.transpose(SC[c // 4][:, (c % 4) * P:(c % 4 + 1) * P],
                                         osb[:, c * P:(c + 1) * P], core.ident)
                if c % 4 == 3 or c == chunks - 1:
                    mm.then_inc(out_turned, 1)
            if w_out is not None:
                for c in range(chunks):
                    if c % 4 == 0:
                        pe.wait_ge(outT_ready, c // 4 + 1)
                    mm = nc.tensor.matmul(PROJ[:, 0:P], w_out(c), oT[:, c, :], start=(c == 0), stop=(c == chunks - 1))
                mm.then_inc(projected, 1)

        @st.block.scalar
        def _(act):
            for u in range(HEADS + 1):
                if u < HEADS:
                    act.wait_ge(max_ready, u + 1)
                    if u >= 3:
                        act.wait_ge(turned, u - 2)
                    nc.scalar.activation(probs[:, u % 3, :], SC[u % 3][:, 0:keys], ACT.Exp, bias=negmax[:, u:u + 1],
                                         accum_out=total[:, u:u + 1]).then_inc(probs_ready, 1)
                h = u - 1
                if h >= 0 and h % 2 == 1:
                    act.wait_ge(turned, h + 1)
                    if h >= 2:
                        act.wait_ge(heads_done, h - 1)
                    copy_turned(nc.scalar.copy, h, turned_act)
            for c in range(0, chunks, 4):
                n = min(4, chunks - c)
                act.wait_ge(out_turned, c // 4 + 1)
                src = SC[c // 4][:, 0:n * P].rearrange("p (c q) -> p c q", q=P)
                if w_out is not None:
                    nc.scalar.activation(oT[:, c:c + n, :], src, ACT.Identity,
                                         bias=0.0 if mid_bias is None else mid_bias).then_inc(outT_ready, 1)
                else:
                    nc.scalar.activation(core.Y[:, bass.ds(qt * TILE, TILE)], SC[0][:, 0:P], ACT.Identity,
                                         bias=out_bias).then_inc(y_ready, 1)
            if w_out is not None:
                act.wait_ge(projected, 1)
                nc.scalar.activation(core.Y[:, bass.ds(qt * TILE, TILE)], PROJ[:, 0:P], ACT.Identity,
                                     bias=0.0 if out_bias is None else out_bias).then_inc(y_ready, 1)

        @st.block.vector
        def _(dve):
            link = Chain(dve, dve_step)
            for u in range(HEADS + 1):
                if u < HEADS:
                    dve.wait_ge(scores_ready, u + 1)
                    if bias is not None:
                        lo, hi = bias_cols
                        link(nc.vector.tensor_tensor(SC[u % 3][:, lo:hi], SC[u % 3][:, lo:hi], bias, ALU.add))
                    nc.vector.tensor_reduce(negmax[:, u:u + 1], SC[u % 3][:, 0:keys], AX_X, ALU.max, negate=True)\
                      .then_inc(max_ready, 1)
                h = u - 1
                if h >= 0 and h % 2 == 0:
                    dve.wait_ge(turned, h + 1)
                    if h >= 2:
                        dve.wait_ge(heads_done, h - 1)
                    copy_turned(nc.vector.tensor_copy, h, turned_dve)
            dve.wait_ge(probs_ready, HEADS)
            link(nc.vector.reciprocal(recip[:, :], total[:, :]))
            dve.wait_ge(heads_done, HEADS)
            for half in range((width + 511) // 512):
                n = min(512, width) // dh
                nc.vector.tensor_tensor(osb[:, half * 512:half * 512 + n * dh].rearrange("p (h d) -> p h d", d=dh),
                                        OUT[half][:, 0:n * dh].rearrange("p (h d) -> p h d", d=dh),
                                        recip[:, half * n:(half + 1) * n].unsqueeze(2).broadcast_to([P, n, dh]),
                                        ALU.mult).then_inc(out_ready, 1)


def copy_queries(core, src, dst, qt):
    nc = core.nc
    with core.stage() as st:
        copied = st.sem("copied")

        @st.block.sync
        def _(sp):
            sp.sem_clear(st.stale)

        half = src.shape[1] // 2

        @st.block.gpsimd
        def _(pool):
            nc.gpsimd.tensor_copy(dst[:, 0:half, :], src[:, 0:half, bass.ds(qt * TILE, TILE)]).then_inc(copied, 1)

        @st.block.vector
        def _(dve):
            nc.vector.tensor_copy(dst[:, half:, :], src[:, half:, bass.ds(qt * TILE, TILE)]).then_inc(copied, 1)



def cross_wide(core, b, w, src, has_null, scale, mask, out_bias, tag):
    nc = core.nc
    keys = CTX_LEN + 2 * has_null
    part = keys // 2
    with ExitStack() as mem:
        def tmp(name, shape, dt=F32):
            return mem.enter_context(nc.sbuf_tensor(f"{tag}_{name}_{nc.next_id()}", shape, dt))
        Q, K, V = tmp("Q", [P, CHUNKS, S]), tmp("K", [P, CHUNKS, keys]), tmp("V", [part, 2, INNER])
        q_tile = tmp("q_tile", [P, CHUNKS, TILE])
        dense(core, CHUNKS, lambda j, m: w("Wq", m * P, (m + 1) * P), lambda j: src, lambda m: Q[:, m, :],
              scale=lambda m: scale)
        dense(core, CHUNKS, lambda j, m: w("Wk", m * P, (m + 1) * P)[0:CTX_D, :], lambda j: core.ctxT[:, :],
              lambda m: K[:, m, 0:CTX_LEN], n=CTX_LEN)
        if mask is not None:
            rows = QT if mask == "per_query" else 1
            bias = tmp("bias", [P, rows, keys])
            mask_raw = tmp("mask_raw", [P, QT * CTX_LEN // 4], U32)
            mask_u8 = mask_raw[:, :].bitcast(U8)[:, 0:rows * CTX_LEN].rearrange("p (t k) -> p t k", t=rows)
        with core.stage() as st:
            product_ready, evac, mask_loaded, null_loaded, step = (
                st.sem(n) for n in ("product_ready", "evac", "mask_loaded", "null_loaded", "step"))

            @st.block.sync
            def _(sp):
                sp.sem_clear(st.stale)
                if mask == "per_query":
                    sp.dma_start(mask_raw[:, :], core.dram["mask_q"])\
                      .then_inc(mask_loaded, 16)
                elif mask == "per_batch":
                    sp.dma_start(mask_u8[:, 0, :], core.dram["mask_b"][b, :].partition_broadcast(P))\
                      .then_inc(mask_loaded, 16)

            @st.block.tensor
            def _(pe):
                for g in range(4):
                    i, half = g // 2, g % 2
                    n = min(part, CTX_LEN - i * part)
                    nc.tensor.matmul(core.ps[g][0:n, :], core.ctxT[:, i * part:i * part + n],
                                     w("Wv", half * 512, (half + 1) * 512)[0:CTX_D, :], start=True, stop=True)\
                      .then_inc(product_ready, 1)

            @st.block.vector
            def _(dve):
                link = Chain(dve, step)
                if has_null:
                    link(nc.vector.tensor_copy(K[:, :, CTX_LEN:CTX_LEN + 1],
                                               w("null_k").unsqueeze(1).broadcast_to([P, CHUNKS, 1])))
                    link(nc.vector.memset(K[:, :, CTX_LEN + 1:keys], 0.0))
                if mask is not None:
                    dve.wait_ge(mask_loaded, 16)
                    link(nc.vector.tensor_scalar(bias[:, :, 0:CTX_LEN], mask_u8[:, :, :], 1.0, -MASKED,
                                                 ALU.subtract, ALU.mult))
                    if has_null:
                        link(nc.vector.memset(bias[:, :, CTX_LEN:CTX_LEN + 1], 0.0))
                        link(nc.vector.memset(bias[:, :, CTX_LEN + 1:keys], MASKED))

            @st.block.scalar
            def _(act):
                for g in range(4):
                    i, half = g // 2, g % 2
                    n = min(part, CTX_LEN - i * part)
                    act.wait_ge(product_ready, g + 1)
                    nc.scalar.copy(V[0:n, i, half * 512:(half + 1) * 512], core.ps[g][0:n, :]).then_inc(evac, 1)
                if has_null:
                    act.dma_start(V[CTX_LEN - part:keys - part, 1, :], core.dram["null_v"]).then_inc(null_loaded, 16)
                    act.wait_ge(null_loaded, 16)

        def tile(qt):
            copy_queries(core, Q, q_tile, qt)
            attention_tile(
                core, qt, DH,
                lambda h: q_tile[DH * (h % 2):DH * (h % 2) + DH, h // 2, :],
                lambda h: K[DH * (h % 2):DH * (h % 2) + DH, h // 2, :],
                lambda h, i: V[:, i, h * DH:(h + 1) * DH],
                [(0, part), (part, part)],
                bias=None if mask is None else
                (bias[:, bass.ds(qt, 1), :].rearrange("p a k -> p (a k)") if mask == "per_query" else bias[:, 0, :]),
                bias_cols=(0, keys), w_out=lambda c: w("Wo", c * P, (c + 1) * P), out_bias=out_bias)

        with nc.Fori(0, QT) as qt:
            tile(qt)


def cross_null(core, b, arena):
    w = core.weights("L0x", arena)
    with core.nc.sbuf_tensor(f"l0x_xn{core.nc.next_id()}", [P, S], F32) as xn:
        normalize(core, core.X, xn[:, :], gain=w("g_norm"))
        cross_wide(core, b, w, xn[:, :], True, DH ** -0.5, "per_batch", None, "l0x")
    normalize(core, core.Y[:, :], core.Y[:, :], gain=w("g_out"))
    residual_norm(core)


def cross_plain(core, b, arena):
    w = core.weights("L1x", arena)
    cross_wide(core, b, w, core.X, False, DH ** -0.5, None, w("bo"), "l1x")
    residual_norm(core)


def cross_masked(core, b, arena):
    w = core.weights("L2x", arena)
    with core.nc.sbuf_tensor(f"l2x_xn{core.nc.next_id()}", [P, S], F32) as xn:
        normalize(core, core.X, xn[:, :], gain=w("gamma"), shift=w("beta"))
        cross_wide(core, b, w, xn[:, :], False, DH ** -0.5, "per_query", w("bo"), "l2x")
    residual_norm(core)



def ternary_ffn(core, b, arena):
    nc = core.nc
    w = core.weights("L0f", arena)
    H = 512
    M = H // P
    with nc.sbuf_tensor(f"l0f_a{nc.next_id()}", [P, M, S], F32) as a, \
            nc.sbuf_tensor(f"l0f_b{nc.next_id()}", [P, M, S], F32) as h:
        gated(core, M, lambda m: w("w1", m * P, (m + 1) * P), lambda m: w("w2", m * P, (m + 1) * P), core.X,
              lambda m: a[:, m, :], ACT.Silu, act_scale=lambda m: w("s1", m, m + 1), lin=lambda m: w("s2", m, m + 1))
        dense(core, M, lambda k, m: w("h1", k * H + m * P, k * H + (m + 1) * P), lambda k: a[:, k, :],
              lambda m: h[:, m, :], kcount=M, func=ACT.Gelu, scale=lambda m: w("sh1", m, m + 1))
        dense(core, M, lambda k, m: w("h2", k * H + m * P, k * H + (m + 1) * P), lambda k: h[:, k, :],
              lambda m: a[:, m, :], kcount=M, func=ACT.Gelu, scale=lambda m: w("sh2", m, m + 1))
        dense(core, 1, lambda k, m: w("w3", k * P, (k + 1) * P), lambda k: a[:, k, :], lambda m: core.Y[:, :],
              kcount=M, scale=lambda m: w("s3"))
    residual_norm(core)



def add_residual(core, dst):
    nc = core.nc
    with core.stage() as st:
        added = st.sem("added")

        @st.block.sync
        def _(sp):
            sp.sem_clear(st.stale)

        @st.block.vector
        def _(dve):
            nc.vector.tensor_tensor(dst, core.X, core.Y[:, :], ALU.add).then_inc(added, 1)


def values_by_token(core, w, V):
    nc = core.nc
    with core.stage() as st:
        product_ready, evac = st.sem("product_ready"), st.sem("evac")

        @st.block.sync
        def _(sp):
            sp.sem_clear(st.stale)

        @st.block.tensor
        def _(pe):
            for t in range(QT):
                mm = nc.tensor.matmul(core.ps[0][:, t * D:(t + 1) * D], core.X[:, t * TILE:(t + 1) * TILE], w,
                                      start=True, stop=True)
            mm.then_inc(product_ready, 1)

        @st.block.scalar
        def _(act):
            act.wait_ge(product_ready, 1)
            nc.scalar.copy(V[:, :, :].rearrange("p t f -> p (t f)"), core.ps[0][:, :]).then_inc(evac, 1)


def spread_heads(core, src, QM):
    nc = core.nc
    masks = core.c("head_scale")
    with core.stage() as st:
        spread = st.sem("spread")

        @st.block.sync
        def _(sp):
            sp.sem_clear(st.stale)

        @st.block.vector
        def _(dve):
            for j in range(4):
                nc.vector.tensor_scalar(QM[:, j, :], src, masks[:, j:j + 1], None, ALU.mult).then_inc(spread, 1)


def narrow_tiles(core, QM, q_tile, K, v_of, key_parts, **kw):
    def tile(qt, kw):
        kw = dict(kw)
        if "bias_of" in kw:
            kw["bias"] = kw.pop("bias_of")(qt)
        copy_queries(core, QM, q_tile, qt)
        attention_tile(core, qt, SH,
                       lambda h: q_tile[32 * (h // 4):32 * (h // 4) + 32, h % 4, :],
                       lambda h: K[32 * (h // 4):32 * (h // 4) + 32, :],
                       v_of, key_parts, **kw)

    with core.nc.Fori(0, QT) as qt:
        tile(qt, kw)


FOUR_PARTS = [(i * P, P) for i in range(S // P)]



def latent_attention(core, b, arena):
    nc = core.nc
    w = core.weights("L1a", arena)
    with ExitStack() as mem:
        def tmp(name, shape):
            return mem.enter_context(nc.sbuf_tensor(f"l1a_{name}_{nc.next_id()}", shape, F32))
        qk, rot, part = tmp("qk", [P, QT, 2, D]), tmp("rot", [P, QT, 2, D]), tmp("part", [P, QT, 2, D])
        V = tmp("V", [P, QT, D])
        sq = tmp("sq", [P, QT, D])
        mean, std = tmp("mean", [P, QT * HEADS]), tmp("std", [P, QT * HEADS])
        eps = tmp("eps", [P, 1])
        K, QM, q_tile = tmp("K", [P, S]), tmp("QM", [P, 4, S]), tmp("q_tile", [P, 4, TILE])
        H4 = SH // 2
        with core.stage() as st:
            product_ready, evac, step, var_ready, std_ready, lkv_ready, turned, keys_ready = (
                st.sem(n) for n in ("product_ready", "evac", "step", "var_ready", "std_ready", "lkv_ready",
                                    "turned", "keys_ready"))
            eps_ready, q_ready = st.sem("eps_ready"), st.sem("q_ready")

            @st.block.sync
            def _(sp):
                sp.sem_clear(st.stale)

            @st.block.gpsimd
            def _(pool):
                nc.gpsimd.memset(eps[:, :], LN_EPS).then_inc(eps_ready, 1)

            @st.block.tensor
            def _(pe):
                for t in range(QT):
                    nc.tensor.matmul(core.ps[t][:, 0:2 * D], core.X[:, t * TILE:(t + 1) * TILE], w("Wqkv"),
                                     start=True, stop=True).then_inc(product_ready, 1)
                pe.wait_ge(q_ready, 1)
                for t in range(QT):
                    mm = nc.tensor.transpose(core.ps[4][:, t * P:(t + 1) * P], rot[:, t, 0, :], core.ident)
                mm.then_inc(turned, 1)
                pe.wait_ge(lkv_ready, 1)
                for t in range(QT):
                    mm = nc.tensor.transpose(core.ps[5][:, t * P:(t + 1) * P], V[:, t, :], core.ident)
                mm.then_inc(turned, 1)

            @st.block.scalar
            def _(act):
                for t in range(QT):
                    act.wait_ge(product_ready, t + 1)
                    nc.scalar.copy(qk[:, t, :, :].rearrange("p a f -> p (a f)"), core.ps[t][:, 0:2 * D])\
                      .then_inc(evac, 1)
                act.wait_ge(turned, 1)
                masks = core.c("head_scale")
                for j in range(4):
                    nc.scalar.mul(QM[:, j, LAT:S], core.ps[4][:, 0:S - LAT], masks[:, j:j + 1]).then_inc(evac, 1)
                    nc.scalar.mul(QM[:, j, 0:LAT], core.ps[4][:, S - LAT:S], masks[:, j:j + 1]).then_inc(evac, 1)
                act.wait_ge(eps_ready, 1)
                act.wait_ge(var_ready, 1)
                nc.scalar.activation(std[:, :], mean[:, :], ACT.Sqrt, bias=eps[:, 0:1], scale=1.0 / SH)\
                  .then_inc(std_ready, 1)
                act.wait_ge(turned, 2)
                nc.scalar.copy(K[:, :], core.ps[5][:, :]).then_inc(evac, 1)

            @st.block.vector
            def _(dve):
                link = Chain(dve, step)
                cos = core.c("rot_cos").rearrange("p (t d) -> p t d", d=SH)
                sin = core.c("rot_sin").rearrange("p (t d) -> p t d", d=SH)
                N = 2 * HEADS

                def heads_view(x):
                    return x[:, :, :, :].rearrange("p t a (h d) -> p t (a h) d", d=SH)
                dve.wait_ge(evac, QT)
                link(nc.vector.tensor_tensor(heads_view(rot), heads_view(qk),
                                             cos.unsqueeze(2).broadcast_to([P, QT, N, SH]), ALU.mult))
                link(nc.vector.tensor_tensor(heads_view(part)[:, :, :, 0:H4], heads_view(qk)[:, :, :, H4:SH],
                                             sin[:, :, 0:H4].unsqueeze(2).broadcast_to([P, QT, N, H4]), ALU.mult))
                link(nc.vector.tensor_tensor(heads_view(part)[:, :, :, H4:SH], heads_view(qk)[:, :, :, 0:H4],
                                             sin[:, :, H4:SH].unsqueeze(2).broadcast_to([P, QT, N, H4]), ALU.mult))
                nc.vector.tensor_tensor(rot[:, :, :, :], rot[:, :, :, :], part[:, :, :, :], ALU.add)\
                  .then_inc(q_ready, 1)
                dve.wait_ge(q_ready, 1)
                kv = rot[:, :, 1, :].rearrange("p t (h d) -> p t h d", d=SH)
                out = V[:, :, :].rearrange("p t (h d) -> p (t h) d", d=SH)
                out4 = V[:, :, :].rearrange("p t (h d) -> p t h d", d=SH)
                mean4 = mean[:, :].rearrange("p (t h) -> p t h", t=QT)
                link(nc.vector.tensor_reduce(mean4, kv, AX_X, ALU.add))
                link(nc.vector.tensor_scalar(mean[:, :], mean[:, :], 1.0 / SH, None, ALU.mult))
                link(nc.vector.tensor_tensor(out4, kv, mean4.unsqueeze(3).broadcast_to([P, QT, HEADS, SH]),
                                             ALU.subtract))
                link(nc.vector.tensor_tensor(sq[:, :, :], V[:, :, :], V[:, :, :], ALU.mult))
                nc.vector.tensor_reduce(mean4, sq[:, :, :].rearrange("p t (h d) -> p t h d", d=SH), AX_X, ALU.add)\
                  .then_inc(var_ready, 1)
                dve.wait_ge(std_ready, 1)
                link(nc.vector.reciprocal(std[:, :], std[:, :]))
                link(nc.vector.tensor_tensor(out, out, std[:, :].unsqueeze(2).broadcast_to([P, QT * HEADS, SH]),
                                             ALU.mult))
                link(nc.vector.tensor_tensor(out, out, w("ln_g").unsqueeze(1).broadcast_to([P, QT * HEADS, SH]),
                                             ALU.mult))
                nc.vector.tensor_tensor(out, out, w("ln_b").unsqueeze(1).broadcast_to([P, QT * HEADS, SH]),
                                        ALU.add).then_inc(lkv_ready, 1)

        latent_mask = core.c("latent_mask").rearrange("p (t k) -> p t k", t=QT)
        narrow_tiles(core, QM, q_tile, K, lambda h, i: V[:, i, h * SH:(h + 1) * SH], FOUR_PARTS,
                     bias_of=lambda qt: latent_mask[:, bass.ds(qt, 1), :].rearrange("p a k -> p (a k)"),
                     bias_cols=(S - LAT, S), w_out=lambda c: w("Wo"), out_bias=w("bo"))
    residual_norm(core)



def projected_attention(core, b, arena):
    nc = core.nc
    w = core.weights("L3a", arena)
    with ExitStack() as mem:
        def tmp(name, shape):
            return mem.enter_context(nc.sbuf_tensor(f"l3a_{name}_{nc.next_id()}", shape, F32))
        first, second = tmp("first", [P, 2, S]), tmp("second", [P, 2, S])
        V, QM, q_tile = tmp("V", [P, QT, D]), tmp("QM", [P, 4, S]), tmp("q_tile", [P, 4, TILE])
        dense(core, 2, lambda k, m: w("Wq" if m == 0 else "Wk"), lambda k: core.X, lambda m: first[:, m, :],
              bias=lambda m: w("bq" if m == 0 else "bk"))
        values_by_token(core, w("Wv"), V)
        for m in range(2):
            dense(core, 1, lambda k, _: w("Wp"), lambda k: first[:, m, :], lambda _: second[:, m, :])
        spread_heads(core, second[:, 0, :], QM)
        narrow_tiles(core, QM, q_tile, second[:, 1, :], lambda h, i: V[:, i, h * SH:(h + 1) * SH], FOUR_PARTS,
                     out_bias=w("bv"))
    residual_norm(core)


def cross_narrow(core, b, arena):
    nc = core.nc
    w = core.weights("L3x", arena)
    part = CTX_LEN // 2
    with ExitStack() as mem:
        def tmp(name, shape):
            return mem.enter_context(nc.sbuf_tensor(f"l3x_{name}_{nc.next_id()}", shape, F32))
        Q, K, V = tmp("Q", [P, S]), tmp("K", [P, CTX_LEN]), tmp("V", [part, 2, D])
        QM, q_tile = tmp("QM", [P, 4, S]), tmp("q_tile", [P, 4, TILE])
        dense(core, 1, lambda k, m: w("Wq"), lambda k: core.X, lambda m: Q[:, :], bias=lambda m: w("bq"))
        dense(core, 1, lambda k, m: w("Wk")[0:CTX_D, :], lambda k: core.ctxT[:, :], lambda m: K[:, :],
              bias=lambda m: w("bk"), n=CTX_LEN)
        with core.stage() as st:
            product_ready, evac = st.sem("product_ready"), st.sem("evac")

            @st.block.sync
            def _(sp):
                sp.sem_clear(st.stale)

            @st.block.tensor
            def _(pe):
                for i in range(2):
                    mm = nc.tensor.matmul(core.ps[0][0:part, i * D:(i + 1) * D],
                                          core.ctxT[:, i * part:(i + 1) * part], w("Wv")[0:CTX_D, :],
                                          start=True, stop=True)
                mm.then_inc(product_ready, 1)

            @st.block.scalar
            def _(act):
                act.wait_ge(product_ready, 1)
                nc.scalar.copy(V[:, :, :].rearrange("p i f -> p (i f)"), core.ps[0][0:part, 0:2 * D])\
                  .then_inc(evac, 1)
        spread_heads(core, Q[:, :], QM)
        narrow_tiles(core, QM, q_tile, K[:, :], lambda h, i: V[:, i, h * SH:(h + 1) * SH],
                     [(0, part), (part, part)], mid_bias=w("bv"), w_out=lambda c: w("Wo"), out_bias=w("bo"))
    residual_norm(core)



def shifted_tokens(core, xs):
    nc = core.nc
    half = D // 2
    with core.stage() as st:
        copied = st.sem("copied")

        @st.block.sync
        def _(sp):
            sp.sem_clear(st.stale)

        @st.block.vector
        def _(dve):
            nc.vector.tensor_copy(xs[0:half, :], core.X[0:half, :]).then_inc(copied, 1)

        @st.block.scalar
        def _(act):
            nc.scalar.copy(xs[half:D, :], core.XP[half:D, PAD - 1:PAD - 1 + S]).then_inc(copied, 1)


def local_attention(core, arena):
    nc = core.nc
    w = core.weights("L1f_a", arena)
    QK_SCALE = 8.0
    with ExitStack() as mem:
        def tmp(name, shape):
            return mem.enter_context(nc.sbuf_tensor(f"local_{name}_{nc.next_id()}", shape, F32))
        xs, x_tile = tmp("xs", [P, S]), tmp("x_tile", [P, TILE])
        qk, rot, swapped = (tmp(n, [P, 2, HEADS, DH]) for n in ("qk", "rot", "swapped"))
        cos, sin = tmp("cos", [P, 2, DH]), tmp("sin", [P, 2, DH])
        norm = tmp("norm", [P, 2 * HEADS])
        q_tile, K = tmp("q_tile", [P, CHUNKS, TILE]), tmp("K", [P, CHUNKS, LOCAL_KEYS])
        V, V_before = tmp("V", [P, INNER]), tmp("V_before", [WINDOW, INNER])
        shifted_tokens(core, xs)
        with core.stage() as st:
            cleared = st.sem("cleared")

            @st.block.sync
            def _(sp):
                sp.sem_clear(st.stale)

            @st.block.vector
            def _(dve):
                nc.vector.memset(K[:, :, TILE:LOCAL_KEYS], 0.0).then_inc(cleared, 1)

            @st.block.gpsimd
            def _(pool):
                nc.gpsimd.memset(V[P - WINDOW:P, :], 0.0).then_inc(cleared, 1)

        with nc.Fori(0, QT) as qt:
            project_local_tile(core, w, qt, xs, x_tile, qk, rot, swapped, cos, sin, norm, q_tile, K, V, V_before,
                               QK_SCALE)
            mask = core.c("local_mask").rearrange("p (t k) -> p t k", t=QT)
            attention_tile(core, qt, DH,
                           lambda h: q_tile[DH * (h % 2):DH * (h % 2) + DH, h // 2, :],
                           lambda h: K[DH * (h % 2):DH * (h % 2) + DH, h // 2, :],
                           lambda h, i: (V_before if i == 0 else V)[:, h * DH:(h + 1) * DH],
                           [(0, WINDOW), (WINDOW, TILE)],
                           bias=mask[:, bass.ds(qt, 1), :].rearrange("p a k -> p (a k)"),
                           bias_cols=(0, LOCAL_KEYS), w_out=lambda c: w("Wo", c * P, (c + 1) * P))
    add_residual(core, core.X)


def project_local_tile(core, w, qt, xs, x_tile, qk, rot, swapped, cos, sin, norm, q_tile, K, V, V_before, qk_scale):
    nc = core.nc
    HALF = DH // 2
    with core.stage() as st:
        x_ready, product_ready, before_kept, evac, squares_ready, sums_ready, norm_ready, tables_ready, swapped_ready, \
            step, rotated, turned, turned_copied, k_before_kept = (
                st.sem(n) for n in ("x_ready", "product_ready", "before_kept", "evac", "squares_ready",
                                    "sums_ready", "norm_ready", "tables_ready", "swapped_ready", "step", "rotated",
                                    "turned", "turned_copied", "k_before_kept"))

        @st.block.sync
        def _(sp):
            sp.sem_clear(st.stale)

        @st.block.tensor
        def _(pe):
            pe.wait_ge(x_ready, 1)
            for g in range(6):
                nc.tensor.matmul(core.ps[g][:, :], x_tile[:, :], w("Wqkv", g * 512, (g + 1) * 512),
                                 start=True, stop=True).then_inc(product_ready, 1)
            pe.wait_ge(rotated, 1)
            flat = rot[:, :, :, :].rearrange("p a h d -> p (a h d)")
            for c in range(2 * CHUNKS):
                bank = core.ps[(6, 7, 4, 5)[c // 4]]
                if c == CHUNKS:
                    pe.wait_ge(evac, 6)
                mm = nc.tensor.transpose(bank[:, (c % 4) * P:(c % 4 + 1) * P], flat[:, c * P:(c + 1) * P],
                                         core.ident)
                if c % 4 == 3:
                    mm.then_inc(turned, 1)

        @st.block.scalar
        def _(act):
            flat = qk[:, :, :, :].rearrange("p a h d -> p (a h d)")
            sq = rot[:, :, :, :].rearrange("p a h d -> p (a h d)")
            for g in range(4):
                act.wait_ge(product_ready, g + 1)
                nc.scalar.copy(flat[:, g * 512:(g + 1) * 512], core.ps[g][:, :]).then_inc(evac, 1)
                nc.scalar.activation(sq[:, g * 512:(g + 1) * 512], core.ps[g][:, :], ACT.Square)\
                  .then_inc(squares_ready, 1)
            act.wait_ge(before_kept, 1)
            for g in range(4, 6):
                act.wait_ge(product_ready, g + 1)
                nc.scalar.copy(V[:, (g - 4) * 512:(g - 3) * 512], core.ps[g][:, :]).then_inc(evac, 1)
            act.wait_ge(sums_ready, 1)
            nc.scalar.activation(norm[:, :], norm[:, :], ACT.Sqrt).then_inc(norm_ready, 1)
            for i in range(2):
                act.wait_ge(turned, i + 1)
                nc.scalar.mul(q_tile[:, 4 * i:4 * i + 4, :],
                              core.ps[6 + i][:, :].rearrange("p (c q) -> p c q", q=P), qk_scale)\
                  .then_inc(turned_copied, 1)

        @st.block.gpsimd
        def _(pool):
            nc.gpsimd.tensor_tensor(cos[:, :, :].rearrange("p a d -> p (a d)"),
                                    core.c("local_cos").rearrange("p (t k) -> p t k", t=QT)[:, bass.ds(qt, 1), :]
                                    .rearrange("p a k -> p (a k)"), w("qk_scale"), ALU.mult).then_inc(tables_ready, 1)
            nc.gpsimd.tensor_tensor(sin[:, :, :].rearrange("p a d -> p (a d)"),
                                    core.c("local_sin").rearrange("p (t k) -> p t k", t=QT)[:, bass.ds(qt, 1), :]
                                    .rearrange("p a k -> p (a k)"), w("qk_scale_swapped"), ALU.mult)\
              .then_inc(tables_ready, 1)
            pool.wait_ge(tables_ready, 2)
            pool.wait_ge(evac, 4)
            for lo, hi in ((0, HALF), (HALF, DH)):
                other = HALF - lo
                for a in range(2):
                    nc.gpsimd.tensor_tensor(swapped[:, a, :, lo:hi], qk[:, a, :, other:other + HALF],
                                            sin[:, a, lo:hi].unsqueeze(1).broadcast_to([P, HEADS, HALF]), ALU.mult)\
                      .then_inc(swapped_ready, 1)

        @st.block.vector
        def _(dve):
            link = Chain(dve, step)
            nc.vector.tensor_copy(x_tile[:, :], xs[:, bass.ds(qt * TILE, TILE)]).then_inc(x_ready, 1)
            nc.vector.tensor_copy(V_before[:, :], V[P - WINDOW:P, :]).then_inc(before_kept, 1)
            nc.vector.tensor_copy(K[:, :, 0:WINDOW], K[:, :, TILE:LOCAL_KEYS]).then_inc(k_before_kept, 1)
            dve.wait_ge(squares_ready, 4)
            nc.vector.tensor_reduce(norm[:, :], rot[:, :, :, :].rearrange("p a h d -> p (a h) d"), AX_X, ALU.add)\
              .then_inc(sums_ready, 1)
            dve.wait_ge(sums_ready, 1)
            dve.wait_ge(tables_ready, 2)
            link(nc.vector.tensor_tensor(rot[:, :, :, :], qk[:, :, :, :],
                                         cos[:, :, :].unsqueeze(2).broadcast_to([P, 2, HEADS, DH]), ALU.mult))
            dve.wait_ge(norm_ready, 1)
            link(nc.vector.tensor_scalar(norm[:, :], norm[:, :], 1e-12, None, ALU.max))
            link(nc.vector.reciprocal(norm[:, :], norm[:, :]))
            dve.wait_ge(swapped_ready, 4)
            link(nc.vector.tensor_tensor(rot[:, :, :, :], rot[:, :, :, :], swapped[:, :, :, :], ALU.add))
            nc.vector.tensor_tensor(rot[:, :, :, :].rearrange("p a h d -> p (a h) d"),
                                    rot[:, :, :, :].rearrange("p a h d -> p (a h) d"),
                                    norm[:, :].unsqueeze(2).broadcast_to([P, 2 * HEADS, DH]), ALU.mult)\
              .then_inc(rotated, 1)
            dve.wait_ge(k_before_kept, 1)
            for i in range(2):
                dve.wait_ge(turned, 3 + i)
                nc.vector.tensor_copy(K[:, 4 * i:4 * i + 4, WINDOW:LOCAL_KEYS],
                                      core.ps[4 + i][:, :].rearrange("p (c q) -> p c q", q=P))\
                  .then_inc(turned_copied, 1)


def gelu_ffn(core, arena):
    nc = core.nc
    w = core.weights("L1f_f", arena)
    M = (FFN_INNER + P - 1) // P
    rows = [min(P, FFN_INNER - m * P) for m in range(M)]
    with nc.sbuf_tensor(f"l1f_xs{nc.next_id()}", [P, S], F32) as xs, \
            nc.sbuf_tensor(f"l1f_h{nc.next_id()}", [P, M, S], F32) as h:
        shifted_tokens(core, xs)
        normalize(core, xs[:, :], xs[:, :], gain=w("ln_g"), shift=w("ln_b"))
        gated(core, M, lambda m: w("W1_gate", m * P, m * P + rows[m]), lambda m: w("W1_lin", m * P, m * P + rows[m]),
              xs[:, :], lambda m: h[0:rows[m], m, :], ACT.Gelu,
              act_bias=lambda m: w("b1_gate", m, m + 1)[0:rows[m], :],
              lin_op=ALU.add, lin=lambda m: w("b1_lin", m, m + 1)[0:rows[m], :])
        dense(core, 1, lambda k, m: w("W2", k * P, (k + 1) * P)[0:rows[k], :], lambda k: h[0:rows[k], k, :],
              lambda m: core.Y[:, :], kcount=M, bias=lambda m: w("b2"))
    add_residual(core, core.X)


def local_transformer(core, b, arena):
    nc = core.nc
    with nc.sbuf_tensor(f"l1f_input{nc.next_id()}", [P, S], F32) as kept:
        with core.stage() as st:
            copied = st.sem("copied")

            @st.block.sync
            def _(sp):
                sp.sem_clear(st.stale)

            @st.block.vector
            def _(dve):
                nc.vector.tensor_copy(kept[:, :], core.X).then_inc(copied, 1)

        with nc.Fori(0, DEPTH) as i:
            turn(core, arena, core.dram["L1f_f"][i, :, :])
            local_attention(core, arena)
            turn(core, 1 - arena, core.dram["L1f_a"][i + 1, :, :])
            gelu_ffn(core, 1 - arena)
        normalize(core, core.X, core.X, add=kept[:, :])



SEG = 10
SEGS = 9
SSM_CHUNK = SEG * SEGS
SSM_CHUNKS = 6
LEAD = SEG - 1
SSM_T = SSM_CHUNK * SSM_CHUNKS
DN = 2 * SSM_N


def soft_clamp_const(lo, hi):
    return (hi + lo) / 2.0, (hi - lo) / 2.0


def state_space(core, b, arena):
    nc = core.nc
    w = core.weights("L2a", arena)
    with ExitStack() as mem:
        def tmp(name, shape):
            return mem.enter_context(nc.sbuf_tensor(f"ssm_{name}_{nc.next_id()}", shape, F32))
        XC, G = tmp("XC", [P, 2, S]), tmp("G", [P, 2, S])
        dt, u, y = tmp("dt", [P, 2, SSM_T]), tmp("u", [P, 2, SSM_T]), tmp("y", [P, 2, SSM_T])
        BC = tmp("BC", [SSM_N, 2, SSM_T])
        rate = tmp("rate", [P, DN])
        real = slice(LEAD, LEAD + S)
        with nc.sbuf_tensor(f"ssm_xn{nc.next_id()}", [P, S], F32) as xn, \
                nc.sbuf_tensor(f"ssm_xb{nc.next_id()}", [P, 2, CONV - 1 + S], F32) as xb, \
                nc.sbuf_tensor(f"ssm_sp{nc.next_id()}", [P, 2, S], F32) as sp_, \
                nc.sbuf_tensor(f"ssm_z{nc.next_id()}", [P, 2, S], F32) as z:
            normalize(core, core.X, xn[:, :], gain=w("norm_w"), centred=False, eps=1e-6)
            dense(core, 2, lambda k, m: w("W_in", m * P, (m + 1) * P), lambda k: xn[:, :],
                  lambda m: xb[:, m, CONV - 1:])
            dense(core, 2, lambda k, m: w("W_in", (m + 2) * P, (m + 3) * P), lambda k: xn[:, :],
                  lambda m: G[:, m, :], func=ACT.Silu)
            with core.stage() as st:
                step, conv_ready, xc_ready, zeroed = (st.sem(n) for n in ("step", "conv_ready", "xc_ready", "zeroed"))

                @st.block.sync
                def _(sp):
                    sp.sem_clear(st.stale)

                @st.block.gpsimd
                def _(pool):
                    for a in (dt, u, BC):
                        nc.gpsimd.memset(a[:, :, 0:LEAD], 0.0).then_inc(zeroed, 1)
                        nc.gpsimd.memset(a[:, :, LEAD + S:SSM_T], 0.0).then_inc(zeroed, 1)

                @st.block.vector
                def _(dve):
                    link = Chain(dve, step)
                    link(nc.vector.memset(xb[:, :, 0:CONV - 1], 0.0))
                    for c in range(2):
                        link(nc.vector.tensor_scalar(z[:, c, :], xb[:, c, 0:S], w("conv_w", 4 * c, 4 * c + 1),
                                                     w("conv_b", c, c + 1), ALU.mult, ALU.add))
                        for j in range(1, CONV):
                            ins = nc.vector.scalar_tensor_tensor(
                                out=z[:, c, :], in0=xb[:, c, j:j + S], scalar=w("conv_w", 4 * c + j, 4 * c + j + 1),
                                in1=z[:, c, :], op0=ALU.mult, op1=ALU.add)
                            if j < CONV - 1:
                                link(ins)
                            else:
                                ins.then_inc(conv_ready, 1)

                @st.block.scalar
                def _(act):
                    for c in range(2):
                        act.wait_ge(conv_ready, c + 1)
                        nc.scalar.activation(XC[:, c, :], z[:, c, :], ACT.Silu).then_inc(xc_ready, 1)

            dense(core, 2, lambda k, m: w("W_dt", k * SSM_D + m * P, k * SSM_D + (m + 1) * P),
                  lambda k: XC[:, k, :], lambda m: z[:, m, :], kcount=2, bias=lambda m: w("b_dt", m, m + 1))
            dense(core, 2, lambda k, m: w("W_BC", (2 * k + m) * SSM_N, (2 * k + m + 1) * SSM_N),
                  lambda k: XC[:, k, :], lambda m: BC[:, m, real], kcount=2)
            mid, half = soft_clamp_const(0.001, 0.1)
            with core.stage() as st:
                step, act_step, log_ready, arg_ready, tanh_ready, rate_ready = (
                    st.sem(n) for n in ("step", "act_step", "log_ready", "arg_ready", "tanh_ready", "rate_ready"))

                @st.block.sync
                def _(sp):
                    sp.sem_clear(st.stale)

                @st.block.scalar
                def _(act):
                    link = Chain(act, act_step)
                    link(nc.scalar.activation(sp_[:, :, :], z[:, :, :], ACT.Abs))
                    link(nc.scalar.activation(sp_[:, :, :], sp_[:, :, :], ACT.Exp, scale=-1.0))
                    nc.scalar.activation(sp_[:, :, :], sp_[:, :, :], ACT.Ln, bias=1.0).then_inc(log_ready, 1)
                    link(nc.scalar.activation(rate[:, :], w("A_log"), ACT.Tanh, scale=0.5 / (5.0 + 1e-8)))
                    nc.scalar.activation(rate[:, :], rate[:, :], ACT.Exp, scale=5.0 / 0.5).then_inc(rate_ready, 1)
                    act.wait_ge(arg_ready, 1)
                    nc.scalar.activation(sp_[:, :, :], sp_[:, :, :], ACT.Tanh).then_inc(tanh_ready, 1)

                @st.block.vector
                def _(dve):
                    link = Chain(dve, step)
                    dve.wait_ge(log_ready, 1)
                    link(nc.vector.scalar_tensor_tensor(out=sp_[:, :, :], in0=z[:, :, :], scalar=0.0,
                                                        in1=sp_[:, :, :], op0=ALU.max, op1=ALU.add))
                    nc.vector.tensor_scalar(sp_[:, :, :], sp_[:, :, :], mid, 0.5 / (half + 1e-8),
                                            ALU.subtract, ALU.mult).then_inc(arg_ready, 1)
                    dve.wait_ge(rate_ready, 1)
                    link(nc.vector.tensor_scalar(rate[:, :], rate[:, :], -0.5 / (8.0 + 1e-8), None, ALU.mult))
                    dve.wait_ge(tanh_ready, 1)
                    link(nc.vector.tensor_scalar(dt[:, :, real], sp_[:, :, :], half / 0.5, mid, ALU.mult, ALU.add))
                    link(nc.vector.tensor_tensor(u[:, :, real], dt[:, :, real], XC[:, :, :], ALU.mult))

        dA, H = tmp("dA", [P, SEGS, DN, SEG]), tmp("H", [P, SEGS, DN, SEG])
        first, carry = tmp("first", [P, SEGS, DN]), tmp("carry", [P, DN])
        scratch, sums, fac = tmp("scratch", [P, DN]), tmp("sums", [P, 1]), tmp("fac", [P, 1])
        with core.stage() as st:
            zeroed = st.sem("zeroed")

            @st.block.sync
            def _(sp):
                sp.sem_clear(st.stale)

            @st.block.vector
            def _(dve):
                nc.vector.memset(carry[:, :], 0.0).then_inc(zeroed, 1)

        with nc.Fori(0, SSM_CHUNKS) as k:
            ssm_chunk(core, bass.ds(k * SSM_CHUNK, SSM_CHUNK), dt, u, y, BC, rate, dA, H, first, carry, scratch,
                      sums, fac)

        with core.stage() as st:
            step = st.sem("step")

            @st.block.sync
            def _(sp):
                sp.sem_clear(st.stale)

            @st.block.vector
            def _(dve):
                link = Chain(dve, step)
                for c in range(2):
                    link(nc.vector.scalar_tensor_tensor(out=XC[:, c, :], in0=XC[:, c, :], scalar=w("D", c, c + 1),
                                                        in1=y[:, c, real], op0=ALU.mult, op1=ALU.add))
                link(nc.vector.tensor_tensor(G[:, :, :], G[:, :, :], XC[:, :, :], ALU.mult))

            @st.block.scalar
            def _(act):
                nc.scalar.activation(fac[:, :], w("residual"), ACT.Sigmoid).then_inc(st.sem("sigmoid"), 1)
        with core.stage() as st:
            step = st.sem("step")

            @st.block.sync
            def _(sp):
                sp.sem_clear(st.stale)

            @st.block.vector
            def _(dve):
                nc.vector.tensor_scalar(fac[:, :], fac[:, :], 0.5, None, ALU.mult).then_inc(step, 1)
        dense(core, 1, lambda k, m: w("W_out", k * P, (k + 1) * P), lambda k: G[:, k, :], lambda m: core.Y[:, :],
              kcount=2, scale=lambda m: fac[:, 0:1])
    add_residual(core, core.Y[:, :])
    residual_norm(core)


def ssm_chunk(core, cols, dt, u, y, BC, rate, dA, H, first, carry, scratch, sums, fac):
    nc = core.nc
    PER_BANK = 5
    groups = [(n, min(PER_BANK, SSM_N - n)) for n in range(0, SSM_N, PER_BANK)]

    def steps(a, n):
        return a.unsqueeze(1).broadcast_to([P, n, SSM_CHUNK]).rearrange("p n (s j) -> p n s j", j=SEG)

    def states(a, c, n0, n):
        return a[:, :, c * SSM_N + n0:c * SSM_N + n0 + n, :].rearrange("p s n j -> p n s j")

    def rows(bank, n):
        return core.ps[bank][:, 0:n * SSM_CHUNK].rearrange("p (n s j) -> p n s j", n=n, j=SEG)

    with core.stage() as st:
        spread, args_ready, tanh_ready, decay_ready, step = (
            st.sem(n) for n in ("spread", "args_ready", "tanh_ready", "decay_ready", "step"))

        @st.block.sync
        def _(sp):
            sp.sem_clear(st.stale)

        @st.block.tensor
        def _(pe):
            for m in range(2):
                for g, (n0, n) in enumerate(groups):
                    for i in range(n):
                        mm = nc.tensor.matmul(core.ps[4 * m + g][:, i * SSM_CHUNK:(i + 1) * SSM_CHUNK],
                                              core.ident[0:SSM_N, n0 + i:n0 + i + 1].broadcast_to([SSM_N, P]),
                                              BC[:, m, cols], start=True, stop=True)
                    mm.then_inc(spread, 1)

        @st.block.gpsimd
        def _(pool):
            for c in range(2):
                nc.gpsimd.tensor_tensor(
                    states(dA, c, 0, SSM_N), steps(dt[:, c, cols], SSM_N),
                    rate[:, c * SSM_N:(c + 1) * SSM_N].unsqueeze(2).broadcast_to([P, SSM_N, SSM_CHUNK])
                    .rearrange("p n (s j) -> p n s j", j=SEG), ALU.mult).then_inc(args_ready, 1)

        @st.block.scalar
        def _(act):
            flat = dA[:, :, :, :].rearrange("p s n j -> p (s n j)")
            act.wait_ge(args_ready, 2)
            nc.scalar.activation(flat, flat, ACT.Tanh).then_inc(tanh_ready, 1)
            act.wait_ge(tanh_ready, 1)
            nc.scalar.activation(flat, flat, ACT.Exp, scale=8.0 / 0.5).then_inc(decay_ready, 1)

        @st.block.vector
        def _(dve):
            link = Chain(dve, step)
            for g, (n0, n) in enumerate(groups):
                dve.wait_ge(spread, g + 1)
                for c in range(2):
                    link(nc.vector.tensor_tensor(states(H, c, n0, n), steps(u[:, c, cols], n), rows(g, n), ALU.mult))
            dve.wait_ge(decay_ready, 1)
            link(nc.vector.tensor_copy(first[:, :, :], dA[:, :, :, 0]))
            link(nc.vector.memset(dA[:, :, :, 0], 0.0))

    with core.stage() as st:
        step, sums_ready, total_ready, norm_ready = (
            st.sem(n) for n in ("step", "sums_ready", "total_ready", "norm_ready"))

        @st.block.sync
        def _(sp):
            sp.sem_clear(st.stale)

        @st.block.tensor
        def _(pe):
            for s in range(SEGS):
                pe.wait_ge(sums_ready, s + 1)
                nc.tensor.matmul(core.ps[0][:, 0:1], core.c("ones"), sums[:, :], start=True, stop=True)\
                  .then_inc(total_ready, 1)

        @st.block.scalar
        def _(act):
            for s in range(SEGS):
                act.wait_ge(total_ready, s + 1)
                nc.scalar.activation(fac[:, :], core.ps[0][:, 0:1], ACT.Sqrt).then_inc(norm_ready, 1)

        @st.block.vector
        def _(dve):
            link = Chain(dve, step)
            for s in range(SEGS):
                before = carry[:, :] if s == 0 else H[:, s - 1, :, SEG - 1]
                last = H[:, s, :, SEG - 1]
                link(nc.vector.tensor_tensor(scratch[:, :], first[:, s, :], before, ALU.mult))
                link(nc.vector.tensor_tensor(H[:, s, :, 0], H[:, s, :, 0], scratch[:, :], ALU.add))
                segment = H[:, s, :, :].rearrange("p n j -> p (n j)")
                link(nc.vector.tensor_tensor_scan(segment, dA[:, s, :, :].rearrange("p n j -> p (n j)"), segment,
                                                  0.0, ALU.mult, ALU.add))
                nc.vector.scalar_tensor_tensor(out=scratch[:, :], in0=last, scalar=1.0, in1=last, op0=ALU.mult,
                                               op1=ALU.mult, accum_out=sums[:, :]).then_inc(sums_ready, 1)
                dve.wait_ge(norm_ready, s + 1)
                link(nc.vector.tensor_scalar(fac[:, :], fac[:, :], 1e-8, None, ALU.add))
                link(nc.vector.reciprocal(fac[:, :], fac[:, :]))
                link(nc.vector.tensor_scalar(fac[:, :], fac[:, :], 20.0, 1.0, ALU.mult, ALU.min))
                link(nc.vector.tensor_scalar(last, last, fac[:, 0:1], None, ALU.mult))
            link(nc.vector.tensor_copy(carry[:, :], H[:, SEGS - 1, :, SEG - 1]))
            for g, (n0, n) in enumerate(groups):
                for c in range(2):
                    link(nc.vector.tensor_tensor(states(dA, c, n0, n), states(H, c, n0, n), rows(4 + g, n), ALU.mult))
            for c in range(2):
                link(nc.vector.tensor_reduce(
                    y[:, c, cols].rearrange("p (s j) -> p s j", j=SEG),
                    dA[:, :, c * SSM_N:(c + 1) * SSM_N, :].rearrange("p s n j -> p s j n"), AX_X, ALU.add))



ROUND = 1.5 * 2.0 ** 23


def quantize_weights(core, raw, out):
    nc = core.nc
    with core.stage() as st, nc.sbuf_tensor(f"wq_abs{nc.next_id()}", [P, 2, 512], F32) as mag, \
            nc.sbuf_tensor(f"wq_sum{nc.next_id()}", [P, 2], F32) as sums, \
            nc.sbuf_tensor(f"wq_mean{nc.next_id()}", [P, 2], F32) as mean, \
            nc.sbuf_tensor(f"wq_inv{nc.next_id()}", [P, 2], F32) as inv:
        sums_ready, total_ready, step = st.sem("sums_ready"), st.sem("total_ready"), st.sem("step")

        @st.block.sync
        def _(sp):
            sp.sem_clear(st.stale)

        @st.block.scalar
        def _(act):
            for i in range(2):
                nc.scalar.activation(mag[:, i, :], raw[i], ACT.Abs, accum_out=sums[:, i:i + 1]).then_inc(sums_ready, 1)

        @st.block.tensor
        def _(pe):
            pe.wait_ge(sums_ready, 2)
            nc.tensor.matmul(core.ps[0][:, 0:2], core.c("ones"), sums[:, :], start=True, stop=True)\
              .then_inc(total_ready, 1)

        @st.block.vector
        def _(dve):
            link = Chain(dve, step)
            dve.wait_ge(total_ready, 1)
            link(nc.vector.tensor_scalar(mean[:, :], core.ps[0][:, 0:2], 1.0 / (P * 512), 1e-5, ALU.mult, ALU.max))
            link(nc.vector.reciprocal(inv[:, :], mean[:, :]))
            for i in range(2):
                link(nc.vector.tensor_scalar(out[i], raw[i], inv[:, i:i + 1], ROUND, ALU.mult, ALU.add))
                link(nc.vector.tensor_scalar(out[i], out[i], ROUND, 1.0, ALU.subtract, ALU.min))
                link(nc.vector.tensor_scalar(out[i], out[i], -1.0, mean[:, i:i + 1], ALU.max, ALU.mult))


def quantize_tokens(core, src, dst, chunks):
    nc = core.nc
    width = chunks * P
    with core.stage() as st, nc.sbuf_tensor(f"tq{nc.next_id()}", [P, QT, width], F32) as q, \
            nc.sbuf_tensor(f"tq_max{nc.next_id()}", [P, QT], F32) as top, \
            nc.sbuf_tensor(f"tq_scale{nc.next_id()}", [P, QT], F32) as scale:
        turned, step, quantized, back, evac = (st.sem(n) for n in ("turned", "step", "quantized", "back", "evac"))

        @st.block.sync
        def _(sp):
            sp.sem_clear(st.stale)

        @st.block.tensor
        def _(pe):
            for t in range(QT):
                for c in range(chunks):
                    mm = nc.tensor.transpose(core.ps[t][:, c * P:(c + 1) * P], src[:, c, t * P:(t + 1) * P],
                                             core.ident)
                mm.then_inc(turned, 1)
            pe.wait_ge(quantized, QT)
            for c in range(chunks):
                for t in range(QT):
                    mm = nc.tensor.transpose(core.ps[4 + c][:, t * P:(t + 1) * P], q[:, t, c * P:(c + 1) * P],
                                             core.ident)
                mm.then_inc(back, 1)

        @st.block.vector
        def _(dve):
            link = Chain(dve, step)
            for t in range(QT):
                dve.wait_ge(turned, t + 1)
                one = slice(t, t + 1)
                link(nc.vector.tensor_reduce(top[:, one], core.ps[t][:, 0:width], AX_X, ALU.max,
                                             apply_absolute_value=True))
                link(nc.vector.tensor_scalar(top[:, one], top[:, one], 1e-5, None, ALU.max))
                link(nc.vector.reciprocal(scale[:, one], top[:, one]))
                link(nc.vector.tensor_scalar(scale[:, one], scale[:, one], 127.0, None, ALU.mult))
                link(nc.vector.tensor_scalar(top[:, one], top[:, one], 1.0 / 127.0, None, ALU.mult))
                link(nc.vector.tensor_scalar(q[:, t, :], core.ps[t][:, 0:width], scale[:, one], ROUND,
                                             ALU.mult, ALU.add))
                link(nc.vector.tensor_scalar(q[:, t, :], q[:, t, :], ROUND, 127.0, ALU.subtract, ALU.min))
                nc.vector.tensor_scalar(q[:, t, :], q[:, t, :], -128.0, top[:, one], ALU.max, ALU.mult)\
                  .then_inc(quantized, 1)

        @st.block.scalar
        def _(act):
            for c in range(chunks):
                act.wait_ge(back, c + 1)
                nc.scalar.copy(dst[:, c, :], core.ps[4 + c][:, :]).then_inc(evac, 1)


def bit_ffn(core, b, arena):
    nc = core.nc
    w = core.weights("L2f", arena)
    M = 4
    with ExitStack() as mem:
        def tmp(name, shape):
            return mem.enter_context(nc.sbuf_tensor(f"l2f_{name}_{nc.next_id()}", shape, F32))
        W, xq = tmp("W", [P, 2, 512]), tmp("xq", [P, 1, S])
        h, z, hq = tmp("h", [P, M, S + 2]), tmp("z", [P, M, S]), tmp("hq", [P, M, S])
        quantize_weights(core, [w("w1"), w("w2")], [W[:, i, :] for i in range(2)])
        quantize_tokens(core, core.X.unsqueeze(1), xq, 1)
        dense(core, M, lambda k, m: W[:, 0, m * P:(m + 1) * P], lambda k: xq[:, 0, :], lambda m: h[:, m, 1:S + 1])
        with core.stage() as st:
            step, conv_ready, silu_ready = (st.sem(n) for n in ("step", "conv_ready", "silu_ready"))

            @st.block.sync
            def _(sp):
                sp.sem_clear(st.stale)

            @st.block.vector
            def _(dve):
                link = Chain(dve, step)
                link(nc.vector.memset(h[:, :, 0:1], 0.0))
                link(nc.vector.memset(h[:, :, S + 1:S + 2], 0.0))
                for m in range(M):
                    link(nc.vector.tensor_scalar(z[:, m, :], h[:, m, 0:S], w("conv_w", 3 * m, 3 * m + 1),
                                                 w("conv_b", m, m + 1), ALU.mult, ALU.add))
                    for j in (1, 2):
                        ins = nc.vector.scalar_tensor_tensor(
                            out=z[:, m, :], in0=h[:, m, j:j + S], scalar=w("conv_w", 3 * m + j, 3 * m + j + 1),
                            in1=z[:, m, :], op0=ALU.mult, op1=ALU.add)
                        if j == 1:
                            link(ins)
                        else:
                            ins.then_inc(conv_ready, 1)

            @st.block.scalar
            def _(act):
                for m in range(M):
                    act.wait_ge(conv_ready, m + 1)
                    nc.scalar.activation(z[:, m, :], z[:, m, :], ACT.Silu).then_inc(silu_ready, 1)

        quantize_tokens(core, z, hq, M)
        dense(core, 1, lambda k, m: W[:, 1, k * P:(k + 1) * P], lambda k: hq[:, k, :], lambda m: core.Y[:, :],
              kcount=M)
    residual_norm(core)



def experts(core, b, arena):
    nc = core.nc
    w = core.weights("L3f", arena)
    M = (EXPERTS + 1) * EXPERT_H // P
    with ExitStack() as mem:
        def tmp(name, shape, dt=F32):
            return mem.enter_context(nc.sbuf_tensor(f"l3f_{name}_{nc.next_id()}", shape, dt))
        h = tmp("h", [P, M, S])
        logits, best, index = tmp("logits", [P, QT, 8]), tmp("best", [P, QT, 8]), tmp("index", [P, QT, 8], U32)
        indexf, chosen, share = tmp("indexf", [P, QT, 8]), tmp("chosen", [P, QT, 8]), tmp("share", [P, QT, 8])
        total, shareT = tmp("total", [P, QT]), tmp("shareT", [EXPERTS, S])
        gated(core, M, lambda m: w("W1", m * P, (m + 1) * P), lambda m: w("W3", m * P, (m + 1) * P), core.X,
              lambda m: h[:, m, :], ACT.Silu)
        with core.stage() as st:
            product_ready, step, arg_ready, exp_ready, share_ready, turned, evac, spread, weighted = (
                st.sem(n) for n in ("product_ready", "step", "arg_ready", "exp_ready", "share_ready", "turned",
                                    "evac", "spread", "weighted"))

            @st.block.sync
            def _(sp):
                sp.sem_clear(st.stale)

            @st.block.tensor
            def _(pe):
                for t in range(QT):
                    mm = nc.tensor.matmul(core.ps[0][:, t * 8:(t + 1) * 8], core.X[:, t * P:(t + 1) * P], w("Wg"),
                                          start=True, stop=True)
                mm.then_inc(product_ready, 1)
                pe.wait_ge(share_ready, 1)
                for t in range(QT):
                    mm = nc.tensor.transpose(core.ps[1][0:EXPERTS, t * P:(t + 1) * P], share[:, t, :], core.ident)
                mm.then_inc(turned, 1)
                pe.wait_ge(evac, 1)
                for e in range(EXPERTS):
                    if e >= 4:
                        pe.wait_ge(weighted, 2 * (e - 3))
                    nc.tensor.matmul(core.ps[2 + e % 4][:, :],
                                     core.ident[0:EXPERTS, e:e + 1].broadcast_to([EXPERTS, P]), shareT[:, :],
                                     start=True, stop=True).then_inc(spread, 1)

            @st.block.scalar
            def _(act):
                act.wait_ge(arg_ready, 1)
                nc.scalar.activation(share[:, :, :], share[:, :, :], ACT.Exp).then_inc(exp_ready, 1)
                act.wait_ge(turned, 1)
                nc.scalar.copy(shareT[:, :], core.ps[1][0:EXPERTS, :]).then_inc(evac, 1)

            @st.block.vector
            def _(dve):
                link = Chain(dve, step)
                dve.wait_ge(product_ready, 1)
                link(nc.vector.tensor_copy(logits[:, :, :].rearrange("p t e -> p (t e)"), core.ps[0][:, 0:QT * 8]))
                for t in range(QT):
                    link(nc.vector.max(best[:, t, :], logits[:, t, :]))
                    link(nc.vector.max_index(index[:, t, :], best[:, t, :], logits[:, t, :]))
                nc.vector.tensor_tensor(share[:, :, :], logits[:, :, :], best[:, :, 0:1].broadcast_to([P, QT, 8]),
                                        ALU.subtract).then_inc(arg_ready, 1)
                link(nc.vector.tensor_copy(indexf[:, :, :], index[:, :, :]))
                number = core.c("number").unsqueeze(1).broadcast_to([P, QT, 8])
                link(nc.vector.tensor_tensor(chosen[:, :, :], number, indexf[:, :, 0:1].broadcast_to([P, QT, 8]),
                                             ALU.is_equal))
                link(nc.vector.tensor_tensor(logits[:, :, :], number, indexf[:, :, 1:2].broadcast_to([P, QT, 8]),
                                             ALU.is_equal))
                link(nc.vector.tensor_tensor(chosen[:, :, :], chosen[:, :, :], logits[:, :, :], ALU.add))
                dve.wait_ge(exp_ready, 1)
                link(nc.vector.tensor_tensor(share[:, :, :], share[:, :, :], chosen[:, :, :], ALU.mult))
                link(nc.vector.tensor_reduce(total[:, :], share[:, :, :], AX_X, ALU.add))
                link(nc.vector.reciprocal(total[:, :], total[:, :]))
                nc.vector.tensor_tensor(share[:, :, :], share[:, :, :], total[:, :].unsqueeze(2)
                                        .broadcast_to([P, QT, 8]), ALU.mult).then_inc(share_ready, 1)
                for e in range(EXPERTS):
                    dve.wait_ge(spread, e + 1)
                    for i in range(2):
                        nc.vector.tensor_tensor(h[:, 2 * e + i, :], h[:, 2 * e + i, :], core.ps[2 + e % 4][:, :],
                                                ALU.mult).then_inc(weighted, 1)
        dense(core, 1, lambda k, m: w("W2", k * P, (k + 1) * P), lambda k: h[:, k, :], lambda m: core.Y[:, :],
              kcount=M)
    residual_norm(core)


def run_sublayers(core, b, order):
    arena = 0
    for i, (name, f) in enumerate(order):
        if name == "L1f_a":
            f(core, b, arena)
            continue
        nxt = order[(i + 1) % len(order)][0]
        turn(core, arena, core.dram[nxt][0, :, :])
        f(core, b, arena)
        arena = 1 - arena


SUBLAYERS = [("L0x", cross_null), ("L0f", ternary_ffn), ("L1a", latent_attention), ("L1x", cross_plain),
             ("L1f_a", local_transformer), ("L2a", state_space), ("L2x", cross_masked), ("L2f", bit_ffn),
             ("L3a", projected_attention), ("L3x", cross_narrow), ("L3f", experts)]
WITH_RWKV = True


def build(nc, dram, cols):
    with ExitStack() as ctx:
        core = Core(nc, ctx, dram, cols)
        with nc.Block() as block:
            zeroed = core.banks[0][0]

            @block.sync
            def _(sp):
                first = dram[SUBLAYERS[0][0]] if SUBLAYERS else None
                if first is not None:
                    sp.dma_start(core.arenas[0][:, 0:first.shape[-1]], first[0, :, :]).then_inc(core.loaded[0], 16)
                sp.dma_start(core.const[:, :], dram["const"][0, :, :]).then_inc(core.resident_loaded, 16)
                sp.dma_start(core.rwkv[:, :], dram["L0a"][0, :, :]).then_inc(core.resident_loaded, 16)
                sp.wait_ge(core.resident_loaded, 32)

            @block.vector
            def _(dve):
                nc.vector.memset(core.XP[:, 0:PAD], 0.0).then_inc(zeroed, 1)

        with nc.Fori(0, B) as b:
            with nc.Block() as block:
                @block.sync
                def _(sp):
                    for span in core.spans:
                        sp.sem_clear(span)
                    sp.dma_start(core.X, dram["x"][b, :, :]).then_inc(core.tokens_loaded, 16)
                    sp.dma_start(core.ctxT[:, :], dram["ctx"][b, :, :]).then_inc(core.tokens_loaded, 16)
                    sp.wait_ge(core.tokens_loaded, 32)
                    sp.sem_clear(core.tokens_loaded)
            if WITH_RWKV:
                rwkv(core)
            run_sublayers(core, b, SUBLAYERS)
            with nc.Block() as block:
                @block.sync
                def _(sp):
                    sp.dma_start(dram["out"][b, :, :], core.X).then_inc(core.stored, 16)
                    sp.wait_ge(core.stored, 16)
                    sp.sem_clear(core.stored)
        with nc.Block() as block:
            @block.sync
            def _(sp):
                if SUBLAYERS:
                    sp.wait_ge(core.loaded[0], 16)



class Pack:

    def __init__(self):
        self.parts, self.cols, self.width = [], {}, 0

    def add(self, name, a):
        a = np.asarray(a)
        if a.ndim == 1:
            a = a[:, None]
        a = np.concatenate([a, np.zeros((P - a.shape[0], a.shape[1]), a.dtype)], 0)
        self.cols[name] = (self.width, self.width + a.shape[1])
        self.width += a.shape[1]
        self.parts.append(a)

    def array(self, width=None):
        width = width or self.width
        pad = np.zeros((P, width - self.width), np.float32)
        return np.ascontiguousarray(np.concatenate(self.parts + [pad], 1))


def by_chunk(a):
    k = a.shape[0] // P
    return a.reshape(k, P, -1).transpose(1, 0, 2).reshape(P, -1)


def cols_of(v):
    return v.reshape(-1, P).T


def constants():
    c = Pack()
    c.add("ident", np.eye(P, dtype=np.float32))
    c.add("average", np.full((P, P), 1.0 / P, np.float32))
    c.add("ones", np.ones((P, P), np.float32))
    heads = np.arange(P) // SH
    c.add("head_scale", (heads[:, None] % 4 == np.arange(4)[None, :]).astype(np.float32) * np.float32(SH ** -0.5))
    c.add("number", np.tile(np.arange(8, dtype=np.float32), (P, 1)))

    def by_tile(a):
        return a.reshape(QT, P, -1).transpose(1, 0, 2).reshape(P, -1).astype(np.float32)
    pos = np.arange(S, dtype=np.float32)
    inv = (1.0 / np.float32(10000.0) ** (np.arange(0, SH, 2, dtype=np.float32) / SH)).astype(np.float32)
    ang = pos[:, None] * inv[None, :]
    c.add("rot_cos", by_tile(np.concatenate([np.cos(ang), np.cos(ang)], 1)))
    c.add("rot_sin", by_tile(np.concatenate([-np.sin(ang), np.sin(ang)], 1)))
    at = np.arange(S)[:, None]
    c.add("latent_mask", by_tile(np.where((at < LAT) & (np.arange(LAT)[None, :] <= at), 0.0, MASKED)))
    half = np.arange(0, DH, 2, dtype=np.float32)
    inv = (1.0 / np.float32(10000.0) ** (half / DH)).astype(np.float32)
    ang = pos[:, None] * inv[None, :]
    base = (half + np.float32(0.4 * DH)) / np.float32(1.4 * DH)
    length = base[None, :] ** ((pos - S // 2) / np.float32(WINDOW // 2))[:, None]
    cos, sin = np.cos(ang), np.sin(ang)
    c.add("local_cos", by_tile(np.concatenate([cos * length] * 2 + [cos / length] * 2, 1)))
    c.add("local_sin", by_tile(np.concatenate([-sin * length, sin * length, -sin / length, sin / length], 1)))
    i, j = np.arange(TILE)[:, None], np.arange(LOCAL_KEYS)[None, :] - WINDOW
    seen = np.stack([(j <= i) & (j >= i - WINDOW) & (t * TILE + j >= 0) for t in range(QT)])
    c.add("local_mask", by_tile(np.where(seen, 0.0, MASKED).reshape(S, LOCAL_KEYS)))
    return c


def packs(x):
    out = {}
    p = out["L0a"] = Pack()
    for n in ("Wk", "Wv", "Wr", "Wo"):
        p.add(n, x["L0_attn_" + n].T)
    for n in ("W", "U"):
        p.add(n, x["L0_attn_" + n])
    for n in "kvr":
        p.add("mix_" + n, x["L0_attn_time_mix_" + n].reshape(-1))
    p = out["L0x"] = Pack()
    p.add("Wq", x["L0_xattn_Wq"])
    p.add("Wk", x["L0_xattn_Wkv"][:, :INNER])
    p.add("Wv", x["L0_xattn_Wkv"][:, INNER:])
    p.add("Wo", by_chunk(x["L0_xattn_Wout"]))
    p.add("g_norm", x["L0_xattn_g_norm"])
    p.add("g_out", x["L0_xattn_g_out"])
    p.add("null_k", np.concatenate([x["L0_xattn_null_kv"][0]] * 2))
    p = out["L0f"] = Pack()
    p.add("w1", x["L0_ffn_w1_w"].T)
    p.add("w2", x["L0_ffn_w2_w"].T)
    p.add("h1", by_chunk(x["L0_ffn_h1_w"].T))
    p.add("h2", by_chunk(x["L0_ffn_h2_w"].T))
    p.add("w3", by_chunk(x["L0_ffn_w3_w"].T))
    for n, k in (("s1", "w1_s"), ("s2", "w2_s"), ("sh1", "h1_s"), ("sh2", "h2_s"), ("s3", "w3_s")):
        p.add(n, cols_of(x["L0_ffn_" + k]))
    p = out["L1x"] = Pack()
    for n in ("Wq", "Wk", "Wv"):
        p.add(n, x["L1_xattn_" + n])
    p.add("Wo", by_chunk(x["L1_xattn_Wo"]))
    p.add("bo", x["L1_xattn_bo"])
    p = out["L2x"] = Pack()
    p.add("Wq", x["L2_xattn_Wq"])
    p.add("Wk", x["L2_xattn_Wkv"][:, :INNER])
    p.add("Wv", x["L2_xattn_Wkv"][:, INNER:])
    p.add("Wo", by_chunk(x["L2_xattn_Wo"]))
    p.add("gamma", x["L2_xattn_ln_gamma"])
    p.add("beta", x["L2_xattn_ln_beta"])
    p.add("bo", x["L2_xattn_bo"])
    def rows_of(v):
        return np.tile(v[None, :], (P, 1))

    p = out["L1a"] = Pack()
    p.add("Wqkv", np.concatenate([x["L1_attn_Wq"].T, x["L1_attn_Wkv"].T], 1))
    p.add("Wo", x["L1_attn_Wo"].T)
    p.add("bo", x["L1_attn_bo"])
    p.add("ln_g", rows_of(x["L1_attn_ln_g"]))
    p.add("ln_b", rows_of(x["L1_attn_ln_b"]))
    p = out["L3a"] = Pack()
    for n in ("Wq", "Wk", "Wv"):
        p.add(n, x["L3_attn_" + n])
    for n in ("bq", "bk", "bv"):
        p.add(n, x["L3_attn_" + n])
    block = np.zeros((P, P), np.float32)
    for h in range(HEADS):
        block[h * SH:(h + 1) * SH, h * SH:(h + 1) * SH] = x["L3_attn_Wp"]
    p.add("Wp", block)
    p = out["L3x"] = Pack()
    p.add("Wq", x["L3_xattn_q_w"])
    p.add("Wk", x["L3_xattn_kv_w"][:, :D])
    p.add("Wv", x["L3_xattn_kv_w"][:, D:])
    p.add("Wo", x["L3_xattn_proj_w"])
    p.add("bq", x["L3_xattn_q_b"])
    p.add("bk", x["L3_xattn_kv_b"][:D])
    p.add("bv", x["L3_xattn_kv_b"][D:])
    p.add("bo", x["L3_xattn_proj_b"])
    p = out["L2a"] = Pack()
    p.add("W_in", x["L2_attn_W_in"].T)
    p.add("W_dt", by_chunk(x["L2_attn_W_dt"].T))
    p.add("W_BC", by_chunk(np.concatenate([x["L2_attn_W_B"].T, x["L2_attn_W_C"].T], 1)))
    p.add("W_out", by_chunk(x["L2_attn_W_out"].T))
    p.add("norm_w", x["L2_attn_norm_w"])
    p.add("conv_w", by_chunk(x["L2_attn_conv_w"][:, 0, :]))
    p.add("conv_b", cols_of(x["L2_attn_conv_b"]))
    p.add("b_dt", cols_of(x["L2_attn_b_dt"]))
    p.add("D", cols_of(x["L2_attn_D_param"]))
    p.add("A_log", by_chunk(x["L2_attn_A_log"]))
    p.add("residual", rows_of(x["L2_attn_residual_scale"].reshape(1)))
    p = out["L2f"] = Pack()
    p.add("w1", x["L2_ffn_w1"].T)
    p.add("w2", by_chunk(x["L2_ffn_w2"].T))
    p.add("conv_w", by_chunk(x["L2_ffn_conv_w"][:, 0, :]))
    p.add("conv_b", cols_of(x["L2_ffn_conv_b"]))
    p = out["L3f"] = Pack()
    p.add("Wg", x["L3_ffn_Wg"].T)
    for n in ("1", "3"):
        p.add("W" + n, np.concatenate([a.T for a in x["L3_ffn_W" + n]] + [x["L3_ffn_sw" + n].T], 1))
    p.add("W2", np.concatenate([by_chunk(a.T) for a in x["L3_ffn_W2"]] + [by_chunk(x["L3_ffn_sw2"].T)], 1))

    out = {k: [p] for k, p in out.items()}
    out["L1f_a"], out["L1f_f"] = [], []
    for i in range(DEPTH):
        p = Pack()
        out["L1f_a"].append(p)
        p.add("Wqkv", x["L1_ffn_Wqkv"][i])
        p.add("Wo", by_chunk(x["L1_ffn_Wo"][i]))
        q, k = x["L1_ffn_q_scale"][i], x["L1_ffn_k_scale"][i]
        p.add("qk_scale", rows_of(np.concatenate([q, k])))
        p.add("qk_scale_swapped", rows_of(np.concatenate([a[s] for a in (q, k) for s in
                                                          (slice(DH // 2, DH), slice(0, DH // 2))])))
        p = Pack()
        out["L1f_f"].append(p)
        W1, b1 = x["L1_ffn_W1"][i], x["L1_ffn_b1"][i]

        def chunk_pad(a):
            more = -a.shape[0] % P
            return np.concatenate([a, np.zeros((more,) + a.shape[1:], a.dtype)], 0)
        p.add("W1_lin", W1[:, :FFN_INNER])
        p.add("W1_gate", W1[:, FFN_INNER:])
        p.add("W2", by_chunk(chunk_pad(x["L1_ffn_W2"][i])))
        p.add("ln_g", x["L1_ffn_ln_g"][i])
        p.add("ln_b", x["L1_ffn_ln_b"][i])
        p.add("b1_lin", cols_of(chunk_pad(b1[:FFN_INNER])))
        p.add("b1_gate", cols_of(chunk_pad(b1[FFN_INNER:])))
        p.add("b2", x["L1_ffn_b2"][i])
    return out


def kernel(**inputs):
    import concourse.bacc as _bacc
    from concourse.bass_utils import run_bass_kernel_spmd as _run

    x = {k: np.asarray(v) for k, v in inputs.items()}
    null_v = np.tile(x["L0_xattn_null_kv"][1], HEADS)
    arrays = {
        "x": x["x"].transpose(0, 2, 1),
        "ctx": x["ctx_768"].transpose(0, 2, 1),
        "mask_b": x["mask_BxS2_bf1"].view(np.uint8),
        "mask_q": np.ascontiguousarray(x["mask_1x1xSxS2_bk0"].reshape(QT, P, CTX_LEN).transpose(1, 0, 2))
        .reshape(P, QT * CTX_LEN).view(np.uint32),
        "null_v": np.stack([null_v, np.zeros_like(null_v)]),
    }
    cols = {}
    packed = dict(packs(x), const=[constants()])
    names = [name for name, _ in SUBLAYERS]
    if "L1f_a" in names:
        packed["L1f_a"] = packed["L1f_a"] + packed[names[(names.index("L1f_a") + 1) % len(names)]][:1]
    for name, rounds in packed.items():
        width = max(p.width for p in rounds)
        arrays[name] = np.stack([p.array(width) for p in rounds])
        cols[name] = dict(rounds[0].cols, width=width)
    arrays = {k: np.ascontiguousarray(a) for k, a in arrays.items()}

    nc = _bacc.Bacc("TRN2", target_bir_lowering=False, num_devices=1)
    dram = {k: nc.dram_tensor("in_" + k, a.shape, mybir.dt.from_np(a.dtype), kind="ExternalInput").ap()
            for k, a in arrays.items()}
    dram["out"] = nc.dram_tensor("out", (B, D, S), F32, kind="ExternalOutput").ap()
    build(nc, dram, cols)
    r = _run(nc, [{"in_" + k: a for k, a in arrays.items()}], core_ids=[0])
    return r.results[0]["out"].transpose(0, 2, 1)
```

```python
from contextlib import ExitStack, contextmanager
import math

import numpy as np

import concourse.bass as bass
from concourse import mybir

P = 128
B, S, D = 4, 512, 128
TILE = 128
QT = S // TILE
CTX_LEN, CTX_D = 154, 96
HEADS = 16
DH = 64
INNER = HEADS * DH
CHUNKS = INNER // P
SH = D // HEADS
LAT = S - (256 - 64)
DEPTH = 6
WINDOW = 32
LOCAL_KEYS = WINDOW + TILE
FFN_INNER = int(D * 4 * 2 / 3)
SSM_D, SSM_N, CONV = 256, 16, 4
EXPERTS, EXPERT_H = 8, 256
LN_EPS = 1e-5
MASKED = -1e30
PAD = 4

F32 = mybir.dt.float32
U8 = mybir.dt.uint8
U32 = mybir.dt.uint32
ALU = mybir.AluOpType
ACT = mybir.ActivationFunctionType
AX_X = mybir.AxisListType.X


class Chain:

    def __init__(self, eng, sem):
        self.eng, self.sem, self.steps = eng, sem, 0

    def __call__(self, ins):
        self.steps += 1
        ins.then_inc(self.sem, 1)
        self.eng.wait_ge(self.sem, self.steps)


class Stage:

    def __init__(self, block, bank, stale):
        self.block, self.bank, self.stale, self.used = block, bank, stale, 0

    def sem(self, name):
        self.used += 1
        return self.bank[self.used - 1]


class Core:

    BANK = 30

    def __init__(self, nc, ctx, dram, cols):
        self.nc, self.ctx, self.dram, self.cols = nc, ctx, dram, cols
        self.parity = 0
        self.banks = [[ctx.enter_context(nc.semaphore(f"bank{i}_{j}")) for j in range(self.BANK)]
                      for i in range(2)]
        self.spans = [range(bank[0].num, bank[-1].num + 1) for bank in self.banks]
        self.loaded = [ctx.enter_context(nc.semaphore(f"weights_loaded{i}")) for i in range(2)]
        self.resident_loaded = ctx.enter_context(nc.semaphore("resident_loaded"))
        self.tokens_loaded = ctx.enter_context(nc.semaphore("tokens_loaded"))
        self.stored = ctx.enter_context(nc.semaphore("stored"))
        self.ps = [ctx.enter_context(nc.psum_tensor(f"ps{i}", [P, 512], F32)) for i in range(8)]
        self.XP = self.buf("XP", [P, PAD + S])
        self.X = self.XP[:, PAD:PAD + S]
        self.Y = self.buf("Y", [P, S])
        self.ctxT = self.buf("ctxT", [CTX_D, CTX_LEN])
        self.const = self.buf("const", [P, cols["const"]["width"]])
        self.rwkv = self.buf("rwkv", [P, cols["L0a"]["width"]])
        self.arena_width = max(v["width"] for k, v in cols.items() if k not in ("const", "L0a"))
        self.arenas = [self.buf(f"arena{i}", [P, self.arena_width]) for i in range(2)]
        self.ident = self.c("ident")
        self.average = self.c("average")

    def buf(self, name, shape, dt=F32):
        return self.ctx.enter_context(self.nc.sbuf_tensor(name, shape, dt))

    def c(self, name):
        lo, hi = self.cols["const"][name]
        return self.const[:, lo:hi]

    def weights(self, pack, arena):
        mem = self.rwkv if arena is None else self.arenas[arena]

        def view(name, a=0, b=None):
            lo, hi = self.cols[pack][name]
            return mem[:, lo + a:(hi if b is None else lo + b)]
        return view

    @contextmanager
    def stage(self):
        self.parity ^= 1
        with self.nc.Block() as block:
            yield Stage(block, self.banks[self.parity], self.spans[1 - self.parity])


def turn(core, arena, prefetch):
    with core.nc.Block() as block:
        @block.sync
        def _(sp):
            for span in core.spans:
                sp.sem_clear(span)
            sp.wait_ge(core.loaded[arena], 16)
            sp.sem_clear(core.loaded[arena])
            if prefetch is not None:
                width = prefetch.shape[-1]
                sp.dma_start(core.arenas[1 - arena][:, 0:width], prefetch).then_inc(core.loaded[1 - arena], 16)


def normalize(core, src, dst, add=None, gain=None, shift=None, centred=True, eps=LN_EPS):
    nc = core.nc
    with core.stage() as st, ExitStack() as mem:
        def tmp(name, shape):
            return mem.enter_context(nc.sbuf_tensor(f"norm_{name}_{nc.next_id()}", shape, F32))
        z, d, sq, std = tmp("z", [P, S]), tmp("d", [P, S]), tmp("sq", [P, S]), tmp("std", [P, QT])
        epsc, warm = tmp("eps", [P, 1]), tmp("warm", [P, 1])
        z_ready, mean_ready, d_ready, sq_ready, var_ready, std_ready, inv_ready, spread, done, eps_ready, warmed = (
            st.sem(n) for n in ("z_ready", "mean_ready", "d_ready", "sq_ready", "var_ready", "std_ready",
                                "inv_ready", "spread", "done", "eps_ready", "warmed"))
        mean, var, inv = core.ps[0:2], core.ps[2:4], core.ps[4:6]
        summed = z[:, :] if add is not None else src
        centre = d[:, :] if centred else summed
        HALF = S // 2
        halves = [slice(0, HALF), slice(HALF, S)]

        @st.block.sync
        def _(sp):
            sp.sem_clear(st.stale)

        @st.block.gpsimd
        def _(pool):
            nc.gpsimd.memset(epsc[:, :], eps).then_inc(eps_ready, 1)

        @st.block.vector
        def _(dve):
            if add is not None:
                for cols in halves:
                    nc.vector.tensor_tensor(summed[:, cols], src[:, cols], add[:, cols], ALU.add).then_inc(z_ready, 1)
                dve.wait_ge(z_ready, 2)
            if centred:
                for i, cols in enumerate(halves):
                    dve.wait_ge(mean_ready, i + 1)
                    nc.vector.tensor_tensor(centre[:, cols], summed[:, cols], mean[i][:, 0:HALF], ALU.subtract)\
                      .then_inc(d_ready, 1)
                dve.wait_ge(d_ready, 2)
            for i in range(2):
                dve.wait_ge(std_ready, i + 1)
                nc.vector.reciprocal(std[:, 2 * i:2 * i + 2], std[:, 2 * i:2 * i + 2]).then_inc(inv_ready, 1)
            for i, cols in enumerate(halves):
                dve.wait_ge(spread, i + 1)
                nc.vector.scalar_tensor_tensor(out=dst[:, cols], in0=centre[:, cols], scalar=1.0 if gain is None else gain,
                                               in1=inv[i][:, 0:HALF], op0=ALU.mult, op1=ALU.mult).then_inc(done, 1)
            if shift is not None:
                dve.wait_ge(done, 2)
                nc.vector.tensor_scalar(dst, dst, shift, None, ALU.add).then_inc(done, 1)

        @st.block.tensor
        def _(pe):
            if centred:
                for i, cols in enumerate(halves):
                    if add is not None:
                        pe.wait_ge(z_ready, i + 1)
                    nc.tensor.matmul(mean[i][:, 0:HALF], core.average, summed[:, cols], start=True, stop=True)\
                      .then_inc(mean_ready, 1)
            for i in range(2):
                pe.wait_ge(sq_ready, i + 1)
                for t in (0, 1):
                    mm = nc.tensor.matmul(var[i][:, t:t + 1], sq[:, (2 * i + t) * P:(2 * i + t + 1) * P],
                                          core.average[:, 0:1], start=True, stop=True)
                mm.then_inc(var_ready, 1)
            for i in range(2):
                pe.wait_ge(inv_ready, i + 1)
                for t in (0, 1):
                    mm = nc.tensor.matmul(inv[i][:, t * P:(t + 1) * P],
                                          std[:, 2 * i + t:2 * i + t + 1].broadcast_to([P, P]), core.ident,
                                          start=True, stop=True)
                mm.then_inc(spread, 1)

        @st.block.scalar
        def _(act):
            act.wait_ge(eps_ready, 1)
            nc.scalar.activation(warm[:, :], epsc[:, :], ACT.Sqrt).then_inc(warmed, 1)
            for i, cols in enumerate(halves):
                if centred:
                    act.wait_ge(d_ready, i + 1)
                elif add is not None:
                    act.wait_ge(z_ready, i + 1)
                nc.scalar.activation(sq[:, cols], centre[:, cols], ACT.Square).then_inc(sq_ready, 1)
            for i in range(2):
                act.wait_ge(var_ready, i + 1)
                nc.scalar.activation(std[:, 2 * i:2 * i + 2], var[i][:, 0:2], ACT.Sqrt, bias=epsc[:, 0:1])\
                  .then_inc(std_ready, 1)


def dense(core, count, w, rhs, dst, kcount=1, func=None, scale=None, bias=None, n=S, also=None):
    nc = core.nc
    with core.stage() as st:
        product_ready = st.sem("product_ready")
        act_done, dve_done = st.sem("act_done"), st.sem("dve_done")
        BANKS = 6

        def on_scalar(m):
            return func is not None or m % 2 == 0

        @st.block.sync
        def _(sp):
            sp.sem_clear(st.stale)

        @st.block.tensor
        def _(pe):
            for m in range(count):
                if m >= BANKS:
                    if func is not None:
                        pe.wait_ge(act_done, m - BANKS + 1)
                    else:
                        pe.wait_ge(act_done if m % 2 == 0 else dve_done, (m - BANKS) // 2 + 1)
                for k in range(kcount):
                    lhs = w(k, m)
                    mm = nc.tensor.matmul(core.ps[m % BANKS][0:lhs.shape[-1], 0:n], lhs, rhs(k),
                                          start=(k == 0), stop=(k == kcount - 1))
                mm.then_inc(product_ready, 1)

        @st.block.scalar
        def _(act):
            for m in range(count):
                if on_scalar(m):
                    out = dst(m)
                    act.wait_ge(product_ready, m + 1)
                    nc.scalar.activation(out, core.ps[m % BANKS][0:out.shape[0], 0:n], func or ACT.Identity,
                                         bias=0.0 if bias is None else bias(m),
                                         scale=1.0 if scale is None else scale(m)).then_inc(act_done, 1)

        @st.block.vector
        def _(dve):
            for m in range(count):
                if not on_scalar(m):
                    out = dst(m)
                    dve.wait_ge(product_ready, m + 1)
                    nc.vector.tensor_scalar(out, core.ps[m % BANKS][0:out.shape[0], 0:n],
                                            1.0 if scale is None else scale(m),
                                            0.0 if bias is None else bias(m), ALU.mult, ALU.add).then_inc(dve_done, 1)


def gated(core, count, w_act, w_lin, rhs, dst, func, act_scale=None, act_bias=None, lin_op=ALU.mult, lin=None):
    nc = core.nc
    with core.stage() as st, nc.sbuf_tensor(f"gate_{nc.next_id()}", [P, 2, S], F32) as gate:
        products_ready, gate_ready, gated_ready = st.sem("products"), st.sem("gate"), st.sem("gated")

        @st.block.sync
        def _(sp):
            sp.sem_clear(st.stale)

        @st.block.tensor
        def _(pe):
            for m in range(count):
                if m >= 3:
                    pe.wait_ge(gated_ready, m - 2)
                for i, w in enumerate((w_act, w_lin)):
                    lhs = w(m)
                    mm = nc.tensor.matmul(core.ps[2 * (m % 3) + i][0:lhs.shape[-1], :], lhs, rhs,
                                          start=True, stop=True)
                mm.then_inc(products_ready, 1)

        @st.block.scalar
        def _(act):
            for m in range(count):
                rows = dst(m).shape[0]
                act.wait_ge(products_ready, m + 1)
                if m >= 2:
                    act.wait_ge(gated_ready, m - 1)
                nc.scalar.activation(gate[0:rows, m % 2, :], core.ps[2 * (m % 3)][0:rows, :], func,
                                     bias=0.0 if act_bias is None else act_bias(m),
                                     scale=1.0 if act_scale is None else act_scale(m)).then_inc(gate_ready, 1)

        @st.block.vector
        def _(dve):
            for m in range(count):
                out = dst(m)
                rows = out.shape[0]
                dve.wait_ge(gate_ready, m + 1)
                nc.vector.scalar_tensor_tensor(out=out, in0=core.ps[2 * (m % 3) + 1][0:rows, :],
                                               scalar=1.0 if lin is None else lin(m), in1=gate[0:rows, m % 2, :],
                                               op0=lin_op, op1=ALU.mult).then_inc(gated_ready, 1)


def residual_norm(core):
    normalize(core, core.X, core.X, add=core.Y[:, :])



def rwkv(core):
    nc = core.nc
    w = core.weights("L0a", None)
    X, Xs = core.X, core.XP[:, PAD - 1:PAD - 1 + S]
    with ExitStack() as mem:
        def tmp(name, width=S):
            return mem.enter_context(nc.sbuf_tensor(f"rwkv_{name}", [P, width], F32))
        diff, xk, xv, xr, k, v, r = (tmp(n) for n in ("diff", "xk", "xv", "xr", "k", "v", "r"))
        decay = tmp("decay", 2)
        with core.stage() as st:
            mixed, product_ready, dve_step, evac = (st.sem(n) for n in ("mixed", "product_ready", "dve_step", "evac"))

            @st.block.sync
            def _(sp):
                sp.sem_clear(st.stale)

            @st.block.vector
            def _(dve):
                link = Chain(dve, dve_step)
                link(nc.vector.tensor_tensor(diff[:, :], X, Xs, ALU.subtract))
                for out, mix in ((xk, "mix_k"), (xv, "mix_v"), (xr, "mix_r")):
                    nc.vector.scalar_tensor_tensor(out=out[:, :], in0=diff[:, :], scalar=w(mix), in1=Xs,
                                                   op0=ALU.mult, op1=ALU.add).then_inc(mixed, 1)
                dve.wait_ge(evac, 1)
                nc.vector.tensor_scalar(decay[:, 1:2], decay[:, 0:1], -1.0, None, ALU.mult).then_inc(dve_step, 1)

            @st.block.tensor
            def _(pe):
                for i, (src, name) in enumerate(((xk, "Wk"), (xv, "Wv"), (xr, "Wr"))):
                    pe.wait_ge(mixed, i + 1)
                    nc.tensor.matmul(core.ps[i][:, :], w(name), src[:, :], start=True, stop=True)\
                      .then_inc(product_ready, 1)

            @st.block.scalar
            def _(act):
                nc.scalar.activation(decay[:, 0:1], w("W"), ACT.Exp).then_inc(evac, 1)
                for i, (dst, f) in enumerate(((k, ACT.Copy), (v, ACT.Copy), (r, ACT.Sigmoid))):
                    act.wait_ge(product_ready, i + 1)
                    nc.scalar.activation(dst[:, :], core.ps[i][:, :], f).then_inc(evac, 1)

        PP, AA, BB = (tmp(n, S + 1) for n in ("PP", "AA", "BB"))
        e1b, e2b, e1, e2, kv, pmax, num = (tmp(n) for n in ("e1b", "e2b", "e1", "e2", "kv", "pmax", "num"))
        with core.stage() as st:
            args_ready, exp_ready, dve_step = (st.sem(n) for n in ("args_ready", "exp_ready", "dve_step"))
            before, now = slice(0, S), slice(1, S + 1)
            neg_decay = decay[:, 1:2]

            @st.block.sync
            def _(sp):
                sp.sem_clear(st.stale)

            @st.block.vector
            def _(dve):
                link = Chain(dve, dve_step)
                link(nc.vector.memset(PP[:, 0:1], -1e38))
                link(nc.vector.memset(AA[:, 0:1], 0.0))
                link(nc.vector.memset(BB[:, 0:1], 0.0))
                link(nc.vector.tensor_tensor_scan(PP[:, now], neg_decay.broadcast_to([P, S]), k[:, :], -1e38,
                                                  ALU.add, ALU.max))
                nc.vector.scalar_tensor_tensor(out=e1b[:, :], in0=PP[:, before], scalar=neg_decay, in1=PP[:, now],
                                               op0=ALU.add, op1=ALU.subtract).then_inc(args_ready, 1)
                nc.vector.tensor_tensor(e2b[:, :], k[:, :], PP[:, now], ALU.subtract).then_inc(args_ready, 1)
                link(nc.vector.scalar_tensor_tensor(out=pmax[:, :], in0=k[:, :], scalar=w("U"), in1=PP[:, before],
                                                    op0=ALU.add, op1=ALU.max))
                nc.vector.tensor_tensor(e1[:, :], PP[:, before], pmax[:, :], ALU.subtract).then_inc(args_ready, 1)
                nc.vector.scalar_tensor_tensor(out=e2[:, :], in0=k[:, :], scalar=w("U"), in1=pmax[:, :],
                                               op0=ALU.add, op1=ALU.subtract).then_inc(args_ready, 1)
                dve.wait_ge(exp_ready, 2)
                link(nc.vector.tensor_tensor(kv[:, :], e2b[:, :], v[:, :], ALU.mult))
                link(nc.vector.tensor_tensor_scan(AA[:, now], e1b[:, :], kv[:, :], 0.0, ALU.mult, ALU.add))
                link(nc.vector.tensor_tensor_scan(BB[:, now], e1b[:, :], e2b[:, :], 0.0, ALU.mult, ALU.add))
                dve.wait_ge(exp_ready, 4)
                link(nc.vector.tensor_tensor(num[:, :], e1[:, :], AA[:, before], ALU.mult))
                link(nc.vector.tensor_tensor(kv[:, :], e2[:, :], v[:, :], ALU.mult))
                link(nc.vector.tensor_tensor(num[:, :], num[:, :], kv[:, :], ALU.add))
                link(nc.vector.tensor_tensor(kv[:, :], e1[:, :], BB[:, before], ALU.mult))
                link(nc.vector.tensor_tensor(kv[:, :], kv[:, :], e2[:, :], ALU.add))
                link(nc.vector.reciprocal(kv[:, :], kv[:, :]))
                link(nc.vector.tensor_tensor(num[:, :], num[:, :], kv[:, :], ALU.mult))
                link(nc.vector.tensor_tensor(num[:, :], num[:, :], r[:, :], ALU.mult))

            @st.block.scalar
            def _(act):
                for i, e in enumerate((e1b, e2b, e1, e2)):
                    act.wait_ge(args_ready, i + 1)
                    nc.scalar.activation(e[:, :], e[:, :], ACT.Exp).then_inc(exp_ready, 1)

        dense(core, 1, lambda j, m: w("Wo"), lambda j: num[:, :], lambda m: core.Y[:, :])
    residual_norm(core)



class NoFeed:

    def pe(self, tile, piece):
        pass

    act = dve = pool = pe


def attention(core, dh, q_of, k_of, v_of, key_parts, bias_of=None, w_out=None, out_bias=None, mid_bias=None,
              make_feed=None):
    nc = core.nc
    keys = sum(n for _, n in key_parts)
    parts = len(key_parts)
    even_parts = len({n for _, n in key_parts}) == 1
    copies = 1 if even_parts else parts
    chunks = HEADS * dh // P
    G = QT * HEADS
    wide = dh == DH
    masked = bias_of is not None
    RING = 2 if make_feed else 3
    PR = 4
    with core.stage() as st, ExitStack() as mem:
        def tmp(name, shape):
            return mem.enter_context(nc.sbuf_tensor(f"attn_{name}_{nc.next_id()}", shape, F32))
        SC = core.ps[0:RING]
        PT = core.ps[RING:RING + 2]
        OUT = core.ps[RING + 2:RING + 4]
        FIN = core.ps[RING + 4]
        probs = tmp("probs", [P, PR, keys])
        shifted = tmp("shifted", [P, 3, keys]) if masked else None
        pts = tmp("pts", [P, 2, parts, P])
        negmax, total, recip = tmp("negmax", [P, G]), tmp("total", [P, G]), tmp("recip", [P, G])
        oT = tmp("oT", [P, chunks, P])
        scores_ready, max_ready, exp_ready, recip_ready, probs_ready = (
            st.sem(n) for n in ("scores_ready", "max_ready", "exp_ready", "recip_ready", "probs_ready"))
        turned, turned_act, turned_dve, heads_done, oT_ready, projected, y_ready = (
            st.sem(n) for n in ("turned", "turned_act", "turned_dve", "heads_done", "oT_ready", "projected",
                                "y_ready"))
        feed = make_feed(st, core.ps[7]) if make_feed else NoFeed()
        TURN, VALUE = 2, 3
        PROJECT = 2
        oT_copies = 2 if wide else 1
        last_step = G + VALUE + PROJECT + 2

        def out_place(t, h):
            if wide:
                return OUT[h // 8][DH * (h % 2):DH * (h % 2) + DH, (h // 2 % 4) * P:(h // 2 % 4 + 1) * P]
            return OUT[t % 2][32 * (h // 4):32 * (h // 4) + 32, 0:P]

        def copy_turned(op, g, sem):
            if even_parts:
                n = key_parts[0][1]
                op(pts[0:n, g % 2, :, :], PT[g % 2][0:n, 0:parts * P].rearrange("p (c q) -> p c q", q=P))\
                    .then_inc(sem, 1)
            else:
                for i, (_, n) in enumerate(key_parts):
                    op(pts[0:n, g % 2, i, :], PT[g % 2][0:n, i * P:(i + 1) * P]).then_inc(sem, 1)

        def finishing(s, offset):
            t, h = divmod(s - (HEADS - 1 + VALUE) - offset, HEADS)
            return t if h == 0 and 0 <= t < QT else None

        @st.block.sync
        def _(sp):
            sp.sem_clear(st.stale)

        @st.block.gpsimd
        def _(pool):
            for k in range(HEADS):
                feed.pool(0, k)
            for s in range(G + 1):
                g = s - 1
                if g >= 0:
                    pool.wait_ge(recip_ready, g + 1)
                    nc.gpsimd.tensor_scalar(probs[:, g % PR, :], probs[:, g % PR, :], recip[:, g:g + 1], None,
                                            ALU.mult).then_inc(probs_ready, 1)
                if s < G and s // HEADS + 1 < QT:
                    feed.pool(s // HEADS + 1, s % HEADS)

        @st.block.tensor
        def _(pe):
            for k in range(HEADS):
                feed.pe(0, k)
            for s in range(last_step):
                if s < G:
                    if s >= RING:
                        pe.wait_ge(max_ready if masked else exp_ready, s - RING + 1)
                    nc.tensor.matmul(SC[s % RING][:, 0:keys], q_of(*divmod(s, HEADS)), k_of(*divmod(s, HEADS)),
                                     start=True, stop=True).then_inc(scores_ready, 1)
                g = s - TURN
                if 0 <= g < G:
                    pe.wait_ge(probs_ready, g + 1)
                    if g >= 2:
                        pe.wait_ge(turned_act if g % 2 else turned_dve, copies * (g // 2))
                    for i, (first, n) in enumerate(key_parts):
                        mm = nc.tensor.transpose(PT[g % 2][0:n, i * P:(i + 1) * P],
                                                 probs[:, g % PR, first:first + n], core.ident)
                    mm.then_inc(turned, 1)
                if s < G and s // HEADS + 1 < QT:
                    feed.pe(s // HEADS + 1, s % HEADS)
                g = s - VALUE
                if 0 <= g < G:
                    t, h = divmod(g, HEADS)
                    pe.wait_ge(turned_act if g % 2 else turned_dve, copies * (g // 2 + 1))
                    if wide and t >= 1 and h in (0, HEADS // 2):
                        pe.wait_ge(oT_ready, 2 * (t - 1) + (1 if h == 0 else 2))
                    elif not wide and t >= 2 and h == 0:
                        pe.wait_ge(oT_ready, t - 1)
                    for i, (_, n) in enumerate(key_parts):
                        mm = nc.tensor.matmul(out_place(t, h), v_of(t, h, i), pts[0:n, g % 2, i, :],
                                              start=(i == 0 and (wide or h % 4 == 0)),
                                              stop=(i == parts - 1 and (wide or h % 4 == 3)))
                    mm.then_inc(heads_done, 1)
                t = finishing(s, PROJECT)
                if t is not None and w_out is not None:
                    pe.wait_ge(oT_ready, oT_copies * (t + 1))
                    if t > 0:
                        pe.wait_ge(y_ready, t)
                    for c in range(chunks):
                        mm = nc.tensor.matmul(FIN[:, 0:P], w_out(c), oT[:, c, :], start=(c == 0),
                                              stop=(c == chunks - 1))
                    mm.then_inc(projected, 1)

        @st.block.scalar
        def _(act):
            for k in range(HEADS):
                feed.act(0, k)
            for s in range(last_step):
                if s < G:
                    act.wait_ge(max_ready, s + 1)
                    if s >= PR:
                        act.wait_ge(turned, s - PR + 1)
                    nc.scalar.activation(probs[:, s % PR, :],
                                         shifted[:, s % 3, :] if masked else SC[s % RING][:, 0:keys],
                                         ACT.Exp, bias=negmax[:, s:s + 1], scale=-1.0 if masked else 1.0,
                                         accum_out=total[:, s:s + 1]).then_inc(exp_ready, 1)
                g = s - TURN
                if 0 <= g < G and g % 2 == 1:
                    act.wait_ge(turned, g + 1)
                    if g >= 2:
                        act.wait_ge(heads_done, g - 1)
                    copy_turned(nc.scalar.copy, g, turned_act)
                if s < G and s // HEADS + 1 < QT:
                    feed.act(s // HEADS + 1, s % HEADS)
                t = finishing(s, 0)
                if t is not None:
                    for j in range(oT_copies):
                        act.wait_ge(heads_done, t * HEADS + HEADS // oT_copies * (j + 1))
                        if w_out is None:
                            nc.scalar.activation(core.Y[:, t * TILE:(t + 1) * TILE], OUT[t % 2][:, 0:P],
                                                 ACT.Identity, bias=out_bias).then_inc(oT_ready, 1)
                            continue
                        if t > 0:
                            act.wait_ge(projected, t)
                        if wide:
                            src = OUT[j][:, :].rearrange("p (c q) -> p c q", q=P)
                        else:
                            src = OUT[t % 2][:, 0:P].unsqueeze(1)
                        nc.scalar.activation(oT[:, 4 * j:min(4 * j + 4, chunks), :], src, ACT.Identity,
                                             bias=0.0 if mid_bias is None else mid_bias).then_inc(oT_ready, 1)
                t = finishing(s, PROJECT + 1)
                if t is not None and w_out is not None:
                    act.wait_ge(projected, t + 1)
                    nc.scalar.activation(core.Y[:, t * TILE:(t + 1) * TILE], FIN[:, 0:P], ACT.Identity,
                                         bias=0.0 if out_bias is None else out_bias).then_inc(y_ready, 1)

        @st.block.vector
        def _(dve):
            for k in range(HEADS):
                feed.dve(0, k)
            for s in range(G + TURN):
                if s < G:
                    dve.wait_ge(scores_ready, s + 1)
                    if masked:
                        if s >= 3:
                            dve.wait_ge(exp_ready, s - 2)
                        nc.vector.tensor_tensor_reduce(shifted[:, s % 3, :], bias_of(s // HEADS),
                                                       SC[s % RING][:, 0:keys], -1.0, 3e38, ALU.add, ALU.min,
                                                       negmax[:, s:s + 1]).then_inc(max_ready, 1)
                    else:
                        nc.vector.tensor_reduce(negmax[:, s:s + 1], SC[s % RING][:, 0:keys], AX_X, ALU.max,
                                                negate=True).then_inc(max_ready, 1)
                g = s - TURN
                if 0 <= g < G and g % 2 == 0:
                    dve.wait_ge(turned, g + 1)
                    if g >= 2:
                        dve.wait_ge(heads_done, g - 1)
                    copy_turned(nc.vector.tensor_copy, g, turned_dve)
                g = s if s < G else None
                if g is not None:
                    dve.wait_ge(exp_ready, g + 1)
                    nc.vector.reciprocal(recip[:, g:g + 1], total[:, g:g + 1]).then_inc(recip_ready, 1)
                if s < G and s // HEADS + 1 < QT:
                    feed.dve(s // HEADS + 1, s % HEADS)



def cross_wide(core, b, w, src, has_null, scale, mask, out_bias, tag):
    nc = core.nc
    keys = CTX_LEN + 2 * has_null
    part = keys // 2
    with ExitStack() as mem:
        def tmp(name, shape, dt=F32):
            return mem.enter_context(nc.sbuf_tensor(f"{tag}_{name}_{nc.next_id()}", shape, dt))
        Q, K, V = tmp("Q", [P, CHUNKS, S]), tmp("K", [P, CHUNKS, keys]), tmp("V", [part, 2, INNER])
        dense(core, CHUNKS, lambda j, m: w("Wq", m * P, (m + 1) * P), lambda j: src, lambda m: Q[:, m, :],
              scale=lambda m: scale)
        dense(core, CHUNKS, lambda j, m: w("Wk", m * P, (m + 1) * P)[0:CTX_D, :], lambda j: core.ctxT[:, :],
              lambda m: K[:, m, 0:CTX_LEN], n=CTX_LEN)
        if mask is not None:
            rows = QT if mask == "per_query" else 1
            bias = tmp("bias", [P, rows, keys])
            mask_raw = tmp("mask_raw", [P, QT * CTX_LEN // 4], U32)
            mask_u8 = mask_raw[:, :].bitcast(U8)[:, 0:rows * CTX_LEN].rearrange("p (t k) -> p t k", t=rows)
        with core.stage() as st:
            product_ready, evac, mask_loaded, null_loaded, step = (
                st.sem(n) for n in ("product_ready", "evac", "mask_loaded", "null_loaded", "step"))

            @st.block.sync
            def _(sp):
                sp.sem_clear(st.stale)
                if mask == "per_query":
                    sp.dma_start(mask_raw[:, :], core.dram["mask_q"])\
                      .then_inc(mask_loaded, 16)
                elif mask == "per_batch":
                    sp.dma_start(mask_u8[:, 0, :], core.dram["mask_b"][b, :].partition_broadcast(P))\
                      .then_inc(mask_loaded, 16)

            @st.block.tensor
            def _(pe):
                for g in range(4):
                    i, half = g // 2, g % 2
                    n = min(part, CTX_LEN - i * part)
                    nc.tensor.matmul(core.ps[g][0:n, :], core.ctxT[:, i * part:i * part + n],
                                     w("Wv", half * 512, (half + 1) * 512)[0:CTX_D, :], start=True, stop=True)\
                      .then_inc(product_ready, 1)

            @st.block.vector
            def _(dve):
                link = Chain(dve, step)
                if has_null:
                    link(nc.vector.tensor_copy(K[:, :, CTX_LEN:CTX_LEN + 1],
                                               w("null_k").unsqueeze(1).broadcast_to([P, CHUNKS, 1])))
                    link(nc.vector.memset(K[:, :, CTX_LEN + 1:keys], 0.0))
                if mask is not None:
                    dve.wait_ge(mask_loaded, 16)
                    link(nc.vector.tensor_scalar(bias[:, :, 0:CTX_LEN], mask_u8[:, :, :], 1.0, -MASKED,
                                                 ALU.subtract, ALU.mult))
                    if has_null:
                        link(nc.vector.memset(bias[:, :, CTX_LEN:CTX_LEN + 1], 0.0))
                        link(nc.vector.memset(bias[:, :, CTX_LEN + 1:keys], MASKED))

            @st.block.scalar
            def _(act):
                for g in range(4):
                    i, half = g // 2, g % 2
                    n = min(part, CTX_LEN - i * part)
                    act.wait_ge(product_ready, g + 1)
                    nc.scalar.copy(V[0:n, i, half * 512:(half + 1) * 512], core.ps[g][0:n, :]).then_inc(evac, 1)
                if has_null:
                    act.dma_start(V[CTX_LEN - part:keys - part, 1, :], core.dram["null_v"]).then_inc(null_loaded, 16)
                    act.wait_ge(null_loaded, 16)

        attention(core, DH,
                  lambda t, h: Q[DH * (h % 2):DH * (h % 2) + DH, h // 2, t * TILE:(t + 1) * TILE],
                  lambda t, h: K[DH * (h % 2):DH * (h % 2) + DH, h // 2, :],
                  lambda t, h, i: V[:, i, h * DH:(h + 1) * DH],
                  [(0, part), (part, part)],
                  bias_of=None if mask is None else lambda t: bias[:, t if mask == "per_query" else 0, :],
                  w_out=lambda c: w("Wo", c * P, (c + 1) * P), out_bias=out_bias)


def cross_null(core, b, arena):
    w = core.weights("L0x", arena)
    with core.nc.sbuf_tensor(f"l0x_xn{core.nc.next_id()}", [P, S], F32) as xn:
        normalize(core, core.X, xn[:, :], gain=w("g_norm"))
        cross_wide(core, b, w, xn[:, :], True, DH ** -0.5, "per_batch", None, "l0x")
    normalize(core, core.Y[:, :], core.Y[:, :], gain=w("g_out"))
    residual_norm(core)


def cross_plain(core, b, arena):
    w = core.weights("L1x", arena)
    cross_wide(core, b, w, core.X, False, DH ** -0.5, None, w("bo"), "l1x")
    residual_norm(core)


def cross_masked(core, b, arena):
    w = core.weights("L2x", arena)
    with core.nc.sbuf_tensor(f"l2x_xn{core.nc.next_id()}", [P, S], F32) as xn:
        normalize(core, core.X, xn[:, :], gain=w("gamma"), shift=w("beta"))
        cross_wide(core, b, w, xn[:, :], False, DH ** -0.5, "per_query", w("bo"), "l2x")
    residual_norm(core)



def ternary_ffn(core, b, arena):
    nc = core.nc
    w = core.weights("L0f", arena)
    H = 512
    M = H // P
    with nc.sbuf_tensor(f"l0f_a{nc.next_id()}", [P, M, S], F32) as a, \
            nc.sbuf_tensor(f"l0f_b{nc.next_id()}", [P, M, S], F32) as h:
        gated(core, M, lambda m: w("w1", m * P, (m + 1) * P), lambda m: w("w2", m * P, (m + 1) * P), core.X,
              lambda m: a[:, m, :], ACT.Silu, act_scale=lambda m: w("s1", m, m + 1), lin=lambda m: w("s2", m, m + 1))
        dense(core, M, lambda k, m: w("h1", k * H + m * P, k * H + (m + 1) * P), lambda k: a[:, k, :],
              lambda m: h[:, m, :], kcount=M, func=ACT.Gelu, scale=lambda m: w("sh1", m, m + 1))
        dense(core, M, lambda k, m: w("h2", k * H + m * P, k * H + (m + 1) * P), lambda k: h[:, k, :],
              lambda m: a[:, m, :], kcount=M, func=ACT.Gelu, scale=lambda m: w("sh2", m, m + 1))
        dense(core, 1, lambda k, m: w("w3", k * P, (k + 1) * P), lambda k: a[:, k, :], lambda m: core.Y[:, :],
              kcount=M, scale=lambda m: w("s3"))
    residual_norm(core)



def add_residual(core, dst):
    nc = core.nc
    with core.stage() as st:
        added = st.sem("added")

        @st.block.sync
        def _(sp):
            sp.sem_clear(st.stale)

        @st.block.vector
        def _(dve):
            nc.vector.tensor_tensor(dst, core.X, core.Y[:, :], ALU.add).then_inc(added, 1)


def values_by_token(core, w, V):
    nc = core.nc
    with core.stage() as st:
        product_ready, evac = st.sem("product_ready"), st.sem("evac")

        @st.block.sync
        def _(sp):
            sp.sem_clear(st.stale)

        @st.block.tensor
        def _(pe):
            for t in range(QT):
                mm = nc.tensor.matmul(core.ps[0][:, t * D:(t + 1) * D], core.X[:, t * TILE:(t + 1) * TILE], w,
                                      start=True, stop=True)
            mm.then_inc(product_ready, 1)

        @st.block.scalar
        def _(act):
            act.wait_ge(product_ready, 1)
            nc.scalar.copy(V[:, :, :].rearrange("p t f -> p (t f)"), core.ps[0][:, :]).then_inc(evac, 1)


def spread_heads(core, src, QM):
    nc = core.nc
    masks = core.c("head_scale")
    with core.stage() as st:
        spread = st.sem("spread")

        @st.block.sync
        def _(sp):
            sp.sem_clear(st.stale)

        @st.block.vector
        def _(dve):
            for j in range(4):
                nc.vector.tensor_scalar(QM[:, j, :], src, masks[:, j:j + 1], None, ALU.mult).then_inc(spread, 1)


def narrow_attention(core, QM, K, V, key_parts, **kw):
    nc = core.nc
    parts, rows = len(key_parts), key_parts[0][1]
    with nc.sbuf_tensor(f"narrow_V{nc.next_id()}", [P, parts, 4, P], F32) as VM:
        with core.stage() as st:
            zeroed, filled = st.sem("zeroed"), st.sem("filled")

            @st.block.sync
            def _(sp):
                sp.sem_clear(st.stale)

            @st.block.gpsimd
            def _(pool):
                nc.gpsimd.memset(VM[:, :, :, :], 0.0).then_inc(zeroed, 1)

            @st.block.vector
            def _(dve):
                dve.wait_ge(zeroed, 1)
                for j in range(4):
                    for i in range(parts):
                        nc.vector.tensor_copy(
                            VM[0:rows, i, j, :].rearrange("p (g f) -> p g f", f=32)[:, :, j * SH:(j + 1) * SH],
                            V[0:rows, i, :].rearrange("p (g f) -> p g f", f=32)[:, :, j * SH:(j + 1) * SH])\
                          .then_inc(filled, 1)
        attention(core, SH,
                  lambda t, h: QM[32 * (h // 4):32 * (h // 4) + 32, h % 4, t * TILE:(t + 1) * TILE],
                  lambda t, h: K[32 * (h // 4):32 * (h // 4) + 32, :],
                  lambda t, h, i: VM[0:rows, i, h % 4, 32 * (h // 4):32 * (h // 4) + 32], key_parts, **kw)


FOUR_PARTS = [(i * P, P) for i in range(S // P)]



def latent_attention(core, b, arena):
    nc = core.nc
    w = core.weights("L1a", arena)
    with ExitStack() as mem:
        def tmp(name, shape):
            return mem.enter_context(nc.sbuf_tensor(f"l1a_{name}_{nc.next_id()}", shape, F32))
        qk, rot, part = tmp("qk", [P, QT, 2, D]), tmp("rot", [P, QT, 2, D]), tmp("part", [P, QT, 2, D])
        V = tmp("V", [P, QT, D])
        sq = tmp("sq", [P, QT, D])
        mean, std = tmp("mean", [P, QT * HEADS]), tmp("std", [P, QT * HEADS])
        eps = tmp("eps", [P, 1])
        K, QM = tmp("K", [P, S]), tmp("QM", [P, 4, S])
        H4 = SH // 2
        with core.stage() as st:
            product_ready, evac, step, var_ready, std_ready, lkv_ready, turned, keys_ready = (
                st.sem(n) for n in ("product_ready", "evac", "step", "var_ready", "std_ready", "lkv_ready",
                                    "turned", "keys_ready"))
            eps_ready, q_ready = st.sem("eps_ready"), st.sem("q_ready")

            @st.block.sync
            def _(sp):
                sp.sem_clear(st.stale)

            @st.block.gpsimd
            def _(pool):
                nc.gpsimd.memset(eps[:, :], LN_EPS).then_inc(eps_ready, 1)

            @st.block.tensor
            def _(pe):
                for t in range(QT):
                    nc.tensor.matmul(core.ps[t][:, 0:2 * D], core.X[:, t * TILE:(t + 1) * TILE], w("Wqkv"),
                                     start=True, stop=True).then_inc(product_ready, 1)
                pe.wait_ge(q_ready, 1)
                for t in range(QT):
                    mm = nc.tensor.transpose(core.ps[4][:, t * P:(t + 1) * P], rot[:, t, 0, :], core.ident)
                mm.then_inc(turned, 1)
                pe.wait_ge(lkv_ready, 1)
                for t in range(QT):
                    mm = nc.tensor.transpose(core.ps[5][:, t * P:(t + 1) * P], V[:, t, :], core.ident)
                mm.then_inc(turned, 1)

            @st.block.scalar
            def _(act):
                for t in range(QT):
                    act.wait_ge(product_ready, t + 1)
                    nc.scalar.copy(qk[:, t, :, :].rearrange("p a f -> p (a f)"), core.ps[t][:, 0:2 * D])\
                      .then_inc(evac, 1)
                act.wait_ge(turned, 1)
                masks = core.c("head_scale")
                for j in range(4):
                    nc.scalar.mul(QM[:, j, LAT:S], core.ps[4][:, 0:S - LAT], masks[:, j:j + 1]).then_inc(evac, 1)
                    nc.scalar.mul(QM[:, j, 0:LAT], core.ps[4][:, S - LAT:S], masks[:, j:j + 1]).then_inc(evac, 1)
                act.wait_ge(eps_ready, 1)
                act.wait_ge(var_ready, 1)
                nc.scalar.activation(std[:, :], mean[:, :], ACT.Sqrt, bias=eps[:, 0:1], scale=1.0 / SH)\
                  .then_inc(std_ready, 1)
                act.wait_ge(turned, 2)
                nc.scalar.copy(K[:, :], core.ps[5][:, :]).then_inc(evac, 1)

            @st.block.vector
            def _(dve):
                link = Chain(dve, step)
                cos = core.c("rot_cos").rearrange("p (t d) -> p t d", d=SH)
                sin = core.c("rot_sin").rearrange("p (t d) -> p t d", d=SH)
                N = 2 * HEADS

                def heads_view(x):
                    return x[:, :, :, :].rearrange("p t a (h d) -> p t (a h) d", d=SH)
                dve.wait_ge(evac, QT)
                link(nc.vector.tensor_tensor(heads_view(rot), heads_view(qk),
                                             cos.unsqueeze(2).broadcast_to([P, QT, N, SH]), ALU.mult))
                link(nc.vector.tensor_tensor(heads_view(part)[:, :, :, 0:H4], heads_view(qk)[:, :, :, H4:SH],
                                             sin[:, :, 0:H4].unsqueeze(2).broadcast_to([P, QT, N, H4]), ALU.mult))
                link(nc.vector.tensor_tensor(heads_view(part)[:, :, :, H4:SH], heads_view(qk)[:, :, :, 0:H4],
                                             sin[:, :, H4:SH].unsqueeze(2).broadcast_to([P, QT, N, H4]), ALU.mult))
                nc.vector.tensor_tensor(rot[:, :, :, :], rot[:, :, :, :], part[:, :, :, :], ALU.add)\
                  .then_inc(q_ready, 1)
                dve.wait_ge(q_ready, 1)
                kv = rot[:, :, 1, :].rearrange("p t (h d) -> p t h d", d=SH)
                out = V[:, :, :].rearrange("p t (h d) -> p (t h) d", d=SH)
                out4 = V[:, :, :].rearrange("p t (h d) -> p t h d", d=SH)
                mean4 = mean[:, :].rearrange("p (t h) -> p t h", t=QT)
                link(nc.vector.tensor_reduce(mean4, kv, AX_X, ALU.add))
                link(nc.vector.tensor_scalar(mean[:, :], mean[:, :], 1.0 / SH, None, ALU.mult))
                link(nc.vector.tensor_tensor(out4, kv, mean4.unsqueeze(3).broadcast_to([P, QT, HEADS, SH]),
                                             ALU.subtract))
                link(nc.vector.tensor_tensor(sq[:, :, :], V[:, :, :], V[:, :, :], ALU.mult))
                nc.vector.tensor_reduce(mean4, sq[:, :, :].rearrange("p t (h d) -> p t h d", d=SH), AX_X, ALU.add)\
                  .then_inc(var_ready, 1)
                dve.wait_ge(std_ready, 1)
                link(nc.vector.reciprocal(std[:, :], std[:, :]))
                link(nc.vector.tensor_tensor(out, out, std[:, :].unsqueeze(2).broadcast_to([P, QT * HEADS, SH]),
                                             ALU.mult))
                link(nc.vector.tensor_tensor(out, out, w("ln_g").unsqueeze(1).broadcast_to([P, QT * HEADS, SH]),
                                             ALU.mult))
                nc.vector.tensor_tensor(out, out, w("ln_b").unsqueeze(1).broadcast_to([P, QT * HEADS, SH]),
                                        ALU.add).then_inc(lkv_ready, 1)

        narrow_attention(core, QM, K, V, FOUR_PARTS,
                         bias_of=lambda t: w("latent_mask", t * S, (t + 1) * S),
                         w_out=lambda c: w("Wo"), out_bias=w("bo"))
    residual_norm(core)



def projected_attention(core, b, arena):
    nc = core.nc
    w = core.weights("L3a", arena)
    with ExitStack() as mem:
        def tmp(name, shape):
            return mem.enter_context(nc.sbuf_tensor(f"l3a_{name}_{nc.next_id()}", shape, F32))
        first, second = tmp("first", [P, 2, S]), tmp("second", [P, 2, S])
        V, QM = tmp("V", [P, QT, D]), tmp("QM", [P, 4, S])
        dense(core, 2, lambda k, m: w("Wq" if m == 0 else "Wk"), lambda k: core.X, lambda m: first[:, m, :],
              bias=lambda m: w("bq" if m == 0 else "bk"))
        values_by_token(core, w("Wv"), V)
        for m in range(2):
            dense(core, 1, lambda k, _: w("Wp"), lambda k: first[:, m, :], lambda _: second[:, m, :])
        spread_heads(core, second[:, 0, :], QM)
        narrow_attention(core, QM, second[:, 1, :], V, FOUR_PARTS,
                         out_bias=w("bv"))
    residual_norm(core)


def cross_narrow(core, b, arena):
    nc = core.nc
    w = core.weights("L3x", arena)
    part = CTX_LEN // 2
    with ExitStack() as mem:
        def tmp(name, shape):
            return mem.enter_context(nc.sbuf_tensor(f"l3x_{name}_{nc.next_id()}", shape, F32))
        Q, K, V = tmp("Q", [P, S]), tmp("K", [P, CTX_LEN]), tmp("V", [part, 2, D])
        QM = tmp("QM", [P, 4, S])
        dense(core, 1, lambda k, m: w("Wq"), lambda k: core.X, lambda m: Q[:, :], bias=lambda m: w("bq"))
        dense(core, 1, lambda k, m: w("Wk")[0:CTX_D, :], lambda k: core.ctxT[:, :], lambda m: K[:, :],
              bias=lambda m: w("bk"), n=CTX_LEN)
        with core.stage() as st:
            product_ready, evac = st.sem("product_ready"), st.sem("evac")

            @st.block.sync
            def _(sp):
                sp.sem_clear(st.stale)

            @st.block.tensor
            def _(pe):
                for i in range(2):
                    mm = nc.tensor.matmul(core.ps[0][0:part, i * D:(i + 1) * D],
                                          core.ctxT[:, i * part:(i + 1) * part], w("Wv")[0:CTX_D, :],
                                          start=True, stop=True)
                mm.then_inc(product_ready, 1)

            @st.block.scalar
            def _(act):
                act.wait_ge(product_ready, 1)
                nc.scalar.copy(V[:, :, :].rearrange("p i f -> p (i f)"), core.ps[0][0:part, 0:2 * D])\
                  .then_inc(evac, 1)
        spread_heads(core, Q[:, :], QM)
        narrow_attention(core, QM, K[:, :], V,
                             [(0, part), (part, part)], mid_bias=w("bv"), w_out=lambda c: w("Wo"), out_bias=w("bo"))
    residual_norm(core)



def shifted_tokens(core, xs):
    nc = core.nc
    half = D // 2
    with core.stage() as st:
        copied = st.sem("copied")

        @st.block.sync
        def _(sp):
            sp.sem_clear(st.stale)

        @st.block.vector
        def _(dve):
            nc.vector.tensor_copy(xs[0:half, :], core.X[0:half, :]).then_inc(copied, 1)

        @st.block.scalar
        def _(act):
            nc.scalar.copy(xs[half:D, :], core.XP[half:D, PAD - 1:PAD - 1 + S]).then_inc(copied, 1)


class LocalFeed:

    def __init__(self, core, st, bank, bufs, w, qk_scale):
        self.core, self.bank, self.w, self.qk_scale = core, bank, w, qk_scale
        (self.xs, self.qk, self.rot, self.swapped, self.squares, self.cos, self.sin, self.norm, self.q_tile, self.K,
         self.V, self.V_before) = bufs
        (self.product_ready, self.bank_read, self.raw_ready, self.squares_ready, self.sums_ready, self.norm_ready,
         self.tables_ready, self.pool_step, self.turns_ready, self.step, self.rotated, self.turned) = (
            st.sem(n) for n in ("product_ready", "bank_read", "raw_ready", "squares_ready", "sums_ready",
                                "norm_ready", "tables_ready", "pool_step", "turns_ready", "step", "rotated",
                                "turned"))
        self.links = 0

    USES = 10

    def group(self, a, g):
        return a[:, g * 512:(g + 1) * 512].rearrange("p (h d) -> p h d", d=DH)

    def pe(self, t, k):
        nc, pe = self.core.nc, self.core.nc.tensor
        if k < 6:
            use = self.USES * t + k
            if use > 0:
                pe.wait_ge(self.bank_read, use)
            nc.tensor.matmul(self.bank[:, :], self.xs[:, t * TILE:(t + 1) * TILE],
                             self.w("Wqkv", k * 512, (k + 1) * 512), start=True, stop=True)\
              .then_inc(self.product_ready, 1)
        if 10 <= k < 14:
            g = k - 10
            pe.wait_ge(self.rotated, 4 * t + g + 1)
            pe.wait_ge(self.bank_read, self.USES * t + 6 + g)
            for c in range(4):
                mm = nc.tensor.transpose(self.bank[:, c * P:(c + 1) * P],
                                         self.rot[:, g * 512 + c * P:g * 512 + (c + 1) * P], self.core.ident)
            mm.then_inc(self.turned, 1)

    def act(self, t, k):
        nc, act = self.core.nc, self.core.nc.scalar
        if k < 6:
            act.wait_ge(self.product_ready, 6 * t + k + 1)
            if k < 4:
                if t > 0:
                    act.wait_ge(self.turns_ready, 4 * (t - 1) + k + 1)
                nc.scalar.copy(self.qk[:, k * 512:(k + 1) * 512], self.bank[:, :]).then_inc(self.raw_ready, 1)
                if 4 * t + k >= 2:
                    act.wait_ge(self.sums_ready, 4 * t + k - 1)
                nc.scalar.activation(self.squares[:, (k % 2) * 512:(k % 2 + 1) * 512], self.bank[:, :], ACT.Square)\
                  .then_inc(self.squares_ready, 1)
                act.wait_ge(self.squares_ready, 4 * t + k + 1)
                act.wait_ge(self.raw_ready, 4 * t + k + 1)
                act.sem_inc(self.bank_read, 1)
            else:
                nc.scalar.copy(self.V[:, t, (k - 4) * 512:(k - 3) * 512], self.bank[:, :]).then_inc(self.bank_read, 1)
        if k == 7:
            act.wait_ge(self.sums_ready, 4 * t + 4)
            nc.scalar.activation(self.norm[:, t, :], self.norm[:, t, :], ACT.Sqrt).then_inc(self.norm_ready, 1)
        if 10 <= k < 14:
            g = k - 10
            act.wait_ge(self.turned, 4 * t + g + 1)
            src = self.bank[:, :].rearrange("p (c q) -> p c q", q=P)
            if g < 2:
                nc.scalar.mul(self.q_tile[:, t % 2, 4 * g:4 * g + 4, :], src, self.qk_scale)\
                  .then_inc(self.bank_read, 1)
            else:
                nc.scalar.copy(self.K[:, 4 * (g - 2):4 * (g - 2) + 4, WINDOW + t * TILE:WINDOW + (t + 1) * TILE], src)\
                  .then_inc(self.bank_read, 1)

    def dve(self, t, k):
        nc, dve = self.core.nc, self.core.nc.vector

        def link(ins):
            self.links += 1
            ins.then_inc(self.step, 1)
            dve.wait_ge(self.step, self.links)
        if k == 6:
            if t == 0:
                link(nc.vector.memset(self.K[:, :, 0:WINDOW], 0.0))
                link(nc.vector.memset(self.V_before[:, 0, :], 0.0))
            else:
                dve.wait_ge(self.bank_read, self.USES * (t - 1) + 6)
                link(nc.vector.tensor_copy(self.V_before[:, t % 2, :], self.V[P - WINDOW:P, t - 1, :]))
        if 2 <= k < 6:
            g = k - 2
            dve.wait_ge(self.squares_ready, 4 * t + g + 1)
            nc.vector.tensor_reduce(self.norm[:, t, 8 * g:8 * g + 8],
                                    self.squares[:, (g % 2) * 512:(g % 2 + 1) * 512]
                                    .rearrange("p (h d) -> p h d", d=DH), AX_X, ALU.add)\
              .then_inc(self.sums_ready, 1)
        if k == 8:
            dve.wait_ge(self.norm_ready, t + 1)
            link(nc.vector.tensor_scalar(self.norm[:, t, :], self.norm[:, t, :], 1e-12, None, ALU.max))
            link(nc.vector.reciprocal(self.norm[:, t, :], self.norm[:, t, :]))
        if 9 <= k < 13:
            g = k - 9
            dve.wait_ge(self.turns_ready, 4 * t + g + 1)
            group = self.group(self.rot, g)
            nc.vector.tensor_tensor(group, group, self.norm[:, t, 8 * g:8 * g + 8].unsqueeze(2)
                                    .broadcast_to([P, 8, DH]), ALU.mult).then_inc(self.rotated, 1)

    def pool(self, t, k):
        nc, pool = self.core.nc, self.core.nc.gpsimd
        HALF = DH // 2
        if k == 0:
            if t > 0:
                pool.wait_ge(self.turns_ready, 4 * t)
            for i, (table, const, scale) in enumerate(((self.cos, "local_cos", "qk_scale"),
                                                       (self.sin, "local_sin", "qk_scale_swapped"))):
                nc.gpsimd.tensor_tensor(table[:, :], self.core.c(const)[:, t * P:(t + 1) * P], self.w(scale),
                                        ALU.mult).then_inc(self.tables_ready, 1)
            pool.wait_ge(self.tables_ready, 2 * (t + 1))
        if 1 <= k < 9 and k % 2 == 1:
            g = k // 2
            a = g // 2
            pool.wait_ge(self.raw_ready, 4 * t + g + 1)
            if t > 0:
                pool.wait_ge(self.turned, 4 * (t - 1) + g + 1)
            raw, rot, other = self.group(self.qk, g), self.group(self.rot, g), self.group(self.swapped, 0)
            nc.gpsimd.tensor_tensor(rot, raw, self.cos[:, a * DH:(a + 1) * DH].unsqueeze(1)
                                    .broadcast_to([P, 8, DH]), ALU.mult).then_inc(self.pool_step, 1)
            for lo in (0, HALF):
                nc.gpsimd.tensor_tensor(other[:, :, lo:lo + HALF], raw[:, :, HALF - lo:2 * HALF - lo],
                                        self.sin[:, a * DH + lo:a * DH + lo + HALF].unsqueeze(1)
                                        .broadcast_to([P, 8, HALF]), ALU.mult).then_inc(self.pool_step, 1)
        if 2 <= k < 10 and k % 2 == 0:
            g = (k - 2) // 2
            rot, other = self.group(self.rot, g), self.group(self.swapped, 0)
            pool.wait_ge(self.pool_step, 3 * (4 * t + g + 1))
            nc.gpsimd.tensor_tensor(rot, rot, other, ALU.add).then_inc(self.turns_ready, 1)
            pool.wait_ge(self.turns_ready, 4 * t + g + 1)


def local_attention(core, arena):
    nc = core.nc
    w = core.weights("L1f_a", arena)
    QK_SCALE = 8.0
    with ExitStack() as mem:
        def tmp(name, shape):
            return mem.enter_context(nc.sbuf_tensor(f"local_{name}_{nc.next_id()}", shape, F32))
        xs = tmp("xs", [P, S])
        qk, rot = tmp("qk", [P, 4 * 512]), tmp("rot", [P, 4 * 512])
        swapped, squares = tmp("swapped", [P, 512]), tmp("squares", [P, 2 * 512])
        cos, sin = tmp("cos", [P, 2 * DH]), tmp("sin", [P, 2 * DH])
        norm = tmp("norm", [P, QT, 2 * HEADS])
        q_tile, K = tmp("q_tile", [P, 2, CHUNKS, TILE]), tmp("K", [P, CHUNKS, WINDOW + S])
        V, V_before = tmp("V", [P, QT, INNER]), tmp("V_before", [WINDOW, 2, INNER])
        shifted_tokens(core, xs)
        bufs = (xs, qk, rot, swapped, squares, cos, sin, norm, q_tile, K, V, V_before)
        attention(core, DH,
                  lambda t, h: q_tile[DH * (h % 2):DH * (h % 2) + DH, t % 2, h // 2, :],
                  lambda t, h: K[DH * (h % 2):DH * (h % 2) + DH, h // 2, t * TILE:t * TILE + LOCAL_KEYS],
                  lambda t, h, i: V_before[:, t % 2, h * DH:(h + 1) * DH] if i == 0 else V[:, t, h * DH:(h + 1) * DH],
                  [(0, WINDOW), (WINDOW, TILE)],
                  bias_of=lambda t: core.c("local_mask")[:, t * LOCAL_KEYS:(t + 1) * LOCAL_KEYS],
                  w_out=lambda c: w("Wo", c * P, (c + 1) * P),
                  make_feed=lambda st, bank: LocalFeed(core, st, bank, bufs, w, QK_SCALE))
    add_residual(core, core.X)


def gelu_ffn(core, arena):
    nc = core.nc
    w = core.weights("L1f_f", arena)
    M = (FFN_INNER + P - 1) // P
    rows = [min(P, FFN_INNER - m * P) for m in range(M)]
    with nc.sbuf_tensor(f"l1f_xs{nc.next_id()}", [P, S], F32) as xs, \
            nc.sbuf_tensor(f"l1f_h{nc.next_id()}", [P, M, S], F32) as h:
        shifted_tokens(core, xs)
        normalize(core, xs[:, :], xs[:, :], gain=w("ln_g"), shift=w("ln_b"))
        gated(core, M, lambda m: w("W1_gate", m * P, m * P + rows[m]), lambda m: w("W1_lin", m * P, m * P + rows[m]),
              xs[:, :], lambda m: h[0:rows[m], m, :], ACT.Gelu,
              act_bias=lambda m: w("b1_gate", m, m + 1)[0:rows[m], :],
              lin_op=ALU.add, lin=lambda m: w("b1_lin", m, m + 1)[0:rows[m], :])
        dense(core, 1, lambda k, m: w("W2", k * P, (k + 1) * P)[0:rows[k], :], lambda k: h[0:rows[k], k, :],
              lambda m: core.Y[:, :], kcount=M, bias=lambda m: w("b2"))
    add_residual(core, core.X)


def local_transformer(core, b, arena):
    nc = core.nc
    with nc.sbuf_tensor(f"l1f_input{nc.next_id()}", [P, S], F32) as kept:
        with core.stage() as st:
            copied = st.sem("copied")

            @st.block.sync
            def _(sp):
                sp.sem_clear(st.stale)

            @st.block.vector
            def _(dve):
                nc.vector.tensor_copy(kept[:, :], core.X).then_inc(copied, 1)

        with nc.Fori(0, DEPTH) as i:
            turn(core, arena, core.dram["L1f_f"][i, :, :])
            local_attention(core, arena)
            turn(core, 1 - arena, core.dram["L1f_a"][i + 1, :, :])
            gelu_ffn(core, 1 - arena)
        normalize(core, core.X, core.X, add=kept[:, :])



SEG = 10
SEGS = 9
SSM_CHUNK = SEG * SEGS
SSM_CHUNKS = 6
LEAD = SEG - 1
SSM_T = SSM_CHUNK * SSM_CHUNKS
DN = 2 * SSM_N


def soft_clamp_const(lo, hi):
    return (hi + lo) / 2.0, (hi - lo) / 2.0


def state_space(core, b, arena):
    nc = core.nc
    w = core.weights("L2a", arena)
    with ExitStack() as mem:
        def tmp(name, shape):
            return mem.enter_context(nc.sbuf_tensor(f"ssm_{name}_{nc.next_id()}", shape, F32))
        XC, G = tmp("XC", [P, 2, S]), tmp("G", [P, 2, S])
        dt, u, y = tmp("dt", [P, 2, SSM_T]), tmp("u", [P, 2, SSM_T]), tmp("y", [P, 2, SSM_T])
        BC = tmp("BC", [SSM_N, 2, SSM_T])
        rate = tmp("rate", [P, DN])
        real = slice(LEAD, LEAD + S)
        with nc.sbuf_tensor(f"ssm_xn{nc.next_id()}", [P, S], F32) as xn, \
                nc.sbuf_tensor(f"ssm_xb{nc.next_id()}", [P, 2, CONV - 1 + S], F32) as xb, \
                nc.sbuf_tensor(f"ssm_sp{nc.next_id()}", [P, 2, S], F32) as sp_, \
                nc.sbuf_tensor(f"ssm_z{nc.next_id()}", [P, 2, S], F32) as z:
            normalize(core, core.X, xn[:, :], gain=w("norm_w"), centred=False, eps=1e-6)
            dense(core, 2, lambda k, m: w("W_in", m * P, (m + 1) * P), lambda k: xn[:, :],
                  lambda m: xb[:, m, CONV - 1:])
            dense(core, 2, lambda k, m: w("W_in", (m + 2) * P, (m + 3) * P), lambda k: xn[:, :],
                  lambda m: G[:, m, :], func=ACT.Silu)
            with core.stage() as st:
                step, conv_ready, xc_ready, zeroed = (st.sem(n) for n in ("step", "conv_ready", "xc_ready", "zeroed"))

                @st.block.sync
                def _(sp):
                    sp.sem_clear(st.stale)

                @st.block.gpsimd
                def _(pool):
                    for a in (dt, u, BC):
                        nc.gpsimd.memset(a[:, :, 0:LEAD], 0.0).then_inc(zeroed, 1)
                        nc.gpsimd.memset(a[:, :, LEAD + S:SSM_T], 0.0).then_inc(zeroed, 1)

                @st.block.vector
                def _(dve):
                    link = Chain(dve, step)
                    link(nc.vector.memset(xb[:, :, 0:CONV - 1], 0.0))
                    for c in range(2):
                        link(nc.vector.tensor_scalar(z[:, c, :], xb[:, c, 0:S], w("conv_w", 4 * c, 4 * c + 1),
                                                     w("conv_b", c, c + 1), ALU.mult, ALU.add))
                        for j in range(1, CONV):
                            ins = nc.vector.scalar_tensor_tensor(
                                out=z[:, c, :], in0=xb[:, c, j:j + S], scalar=w("conv_w", 4 * c + j, 4 * c + j + 1),
                                in1=z[:, c, :], op0=ALU.mult, op1=ALU.add)
                            if j < CONV - 1:
                                link(ins)
                            else:
                                ins.then_inc(conv_ready, 1)

                @st.block.scalar
                def _(act):
                    for c in range(2):
                        act.wait_ge(conv_ready, c + 1)
                        nc.scalar.activation(XC[:, c, :], z[:, c, :], ACT.Silu).then_inc(xc_ready, 1)

            dense(core, 2, lambda k, m: w("W_dt", k * SSM_D + m * P, k * SSM_D + (m + 1) * P),
                  lambda k: XC[:, k, :], lambda m: z[:, m, :], kcount=2, bias=lambda m: w("b_dt", m, m + 1))
            dense(core, 2, lambda k, m: w("W_BC", (2 * k + m) * SSM_N, (2 * k + m + 1) * SSM_N),
                  lambda k: XC[:, k, :], lambda m: BC[:, m, real], kcount=2)
            mid, half = soft_clamp_const(0.001, 0.1)
            with core.stage() as st:
                step, act_step, log_ready, arg_ready, tanh_ready, rate_ready = (
                    st.sem(n) for n in ("step", "act_step", "log_ready", "arg_ready", "tanh_ready", "rate_ready"))

                @st.block.sync
                def _(sp):
                    sp.sem_clear(st.stale)

                @st.block.scalar
                def _(act):
                    link = Chain(act, act_step)
                    link(nc.scalar.activation(sp_[:, :, :], z[:, :, :], ACT.Abs))
                    link(nc.scalar.activation(sp_[:, :, :], sp_[:, :, :], ACT.Exp, scale=-1.0))
                    nc.scalar.activation(sp_[:, :, :], sp_[:, :, :], ACT.Ln, bias=1.0).then_inc(log_ready, 1)
                    link(nc.scalar.activation(rate[:, :], w("A_log"), ACT.Tanh, scale=0.5 / (5.0 + 1e-8)))
                    nc.scalar.activation(rate[:, :], rate[:, :], ACT.Exp, scale=5.0 / 0.5).then_inc(rate_ready, 1)
                    act.wait_ge(arg_ready, 1)
                    nc.scalar.activation(sp_[:, :, :], sp_[:, :, :], ACT.Tanh).then_inc(tanh_ready, 1)

                @st.block.vector
                def _(dve):
                    link = Chain(dve, step)
                    dve.wait_ge(log_ready, 1)
                    link(nc.vector.scalar_tensor_tensor(out=sp_[:, :, :], in0=z[:, :, :], scalar=0.0,
                                                        in1=sp_[:, :, :], op0=ALU.max, op1=ALU.add))
                    nc.vector.tensor_scalar(sp_[:, :, :], sp_[:, :, :], mid, 0.5 / (half + 1e-8),
                                            ALU.subtract, ALU.mult).then_inc(arg_ready, 1)
                    dve.wait_ge(rate_ready, 1)
                    link(nc.vector.tensor_scalar(rate[:, :], rate[:, :], -0.5 / (8.0 + 1e-8), None, ALU.mult))
                    dve.wait_ge(tanh_ready, 1)
                    link(nc.vector.tensor_scalar(dt[:, :, real], sp_[:, :, :], half / 0.5, mid, ALU.mult, ALU.add))
                    link(nc.vector.tensor_tensor(u[:, :, real], dt[:, :, real], XC[:, :, :], ALU.mult))

        dA, H = tmp("dA", [P, SEGS, DN, SEG]), tmp("H", [P, SEGS, DN, SEG])
        first, carry = tmp("first", [P, SEGS, DN]), tmp("carry", [P, DN])
        scratch, sums, fac = tmp("scratch", [P, DN]), tmp("sums", [P, 1]), tmp("fac", [P, 1])
        with core.stage() as st:
            zeroed = st.sem("zeroed")

            @st.block.sync
            def _(sp):
                sp.sem_clear(st.stale)

            @st.block.vector
            def _(dve):
                nc.vector.memset(carry[:, :], 0.0).then_inc(zeroed, 1)

        with nc.Fori(0, SSM_CHUNKS) as k:
            ssm_chunk(core, bass.ds(k * SSM_CHUNK, SSM_CHUNK), dt, u, y, BC, rate, dA, H, first, carry, scratch,
                      sums, fac)

        with core.stage() as st:
            step = st.sem("step")

            @st.block.sync
            def _(sp):
                sp.sem_clear(st.stale)

            @st.block.vector
            def _(dve):
                link = Chain(dve, step)
                for c in range(2):
                    link(nc.vector.scalar_tensor_tensor(out=XC[:, c, :], in0=XC[:, c, :], scalar=w("D", c, c + 1),
                                                        in1=y[:, c, real], op0=ALU.mult, op1=ALU.add))
                link(nc.vector.tensor_tensor(G[:, :, :], G[:, :, :], XC[:, :, :], ALU.mult))

            @st.block.scalar
            def _(act):
                nc.scalar.activation(fac[:, :], w("residual"), ACT.Sigmoid).then_inc(st.sem("sigmoid"), 1)
        with core.stage() as st:
            step = st.sem("step")

            @st.block.sync
            def _(sp):
                sp.sem_clear(st.stale)

            @st.block.vector
            def _(dve):
                nc.vector.tensor_scalar(fac[:, :], fac[:, :], 0.5, None, ALU.mult).then_inc(step, 1)
        dense(core, 1, lambda k, m: w("W_out", k * P, (k + 1) * P), lambda k: G[:, k, :], lambda m: core.Y[:, :],
              kcount=2, scale=lambda m: fac[:, 0:1])
    add_residual(core, core.Y[:, :])
    residual_norm(core)


def ssm_chunk(core, cols, dt, u, y, BC, rate, dA, H, first, carry, scratch, sums, fac):
    nc = core.nc
    PER_BANK = 5
    groups = [(n, min(PER_BANK, SSM_N - n)) for n in range(0, SSM_N, PER_BANK)]

    def steps(a, n):
        return a.unsqueeze(1).broadcast_to([P, n, SSM_CHUNK]).rearrange("p n (s j) -> p n s j", j=SEG)

    def states(a, c, n0, n):
        return a[:, :, c * SSM_N + n0:c * SSM_N + n0 + n, :].rearrange("p s n j -> p n s j")

    def rows(bank, n):
        return core.ps[bank][:, 0:n * SSM_CHUNK].rearrange("p (n s j) -> p n s j", n=n, j=SEG)

    with core.stage() as st:
        spread, args_ready, tanh_ready, decay_ready, step = (
            st.sem(n) for n in ("spread", "args_ready", "tanh_ready", "decay_ready", "step"))

        @st.block.sync
        def _(sp):
            sp.sem_clear(st.stale)

        @st.block.tensor
        def _(pe):
            for m in range(2):
                for g, (n0, n) in enumerate(groups):
                    for i in range(n):
                        mm = nc.tensor.matmul(core.ps[4 * m + g][:, i * SSM_CHUNK:(i + 1) * SSM_CHUNK],
                                              core.ident[0:SSM_N, n0 + i:n0 + i + 1].broadcast_to([SSM_N, P]),
                                              BC[:, m, cols], start=True, stop=True)
                    mm.then_inc(spread, 1)

        @st.block.gpsimd
        def _(pool):
            for c in range(2):
                nc.gpsimd.tensor_tensor(
                    states(dA, c, 0, SSM_N), steps(dt[:, c, cols], SSM_N),
                    rate[:, c * SSM_N:(c + 1) * SSM_N].unsqueeze(2).broadcast_to([P, SSM_N, SSM_CHUNK])
                    .rearrange("p n (s j) -> p n s j", j=SEG), ALU.mult).then_inc(args_ready, 1)

        @st.block.scalar
        def _(act):
            flat = dA[:, :, :, :].rearrange("p s n j -> p (s n j)")
            act.wait_ge(args_ready, 2)
            nc.scalar.activation(flat, flat, ACT.Tanh).then_inc(tanh_ready, 1)
            act.wait_ge(tanh_ready, 1)
            nc.scalar.activation(flat, flat, ACT.Exp, scale=8.0 / 0.5).then_inc(decay_ready, 1)

        @st.block.vector
        def _(dve):
            link = Chain(dve, step)
            for g, (n0, n) in enumerate(groups):
                dve.wait_ge(spread, g + 1)
                for c in range(2):
                    link(nc.vector.tensor_tensor(states(H, c, n0, n), steps(u[:, c, cols], n), rows(g, n), ALU.mult))
            dve.wait_ge(decay_ready, 1)
            link(nc.vector.tensor_copy(first[:, :, :], dA[:, :, :, 0]))
            link(nc.vector.memset(dA[:, :, :, 0], 0.0))

    with core.stage() as st:
        step, sums_ready, total_ready, norm_ready = (
            st.sem(n) for n in ("step", "sums_ready", "total_ready", "norm_ready"))

        @st.block.sync
        def _(sp):
            sp.sem_clear(st.stale)

        @st.block.tensor
        def _(pe):
            for s in range(SEGS):
                pe.wait_ge(sums_ready, s + 1)
                nc.tensor.matmul(core.ps[0][:, 0:1], core.c("ones"), sums[:, :], start=True, stop=True)\
                  .then_inc(total_ready, 1)

        @st.block.scalar
        def _(act):
            for s in range(SEGS):
                act.wait_ge(total_ready, s + 1)
                nc.scalar.activation(fac[:, :], core.ps[0][:, 0:1], ACT.Sqrt).then_inc(norm_ready, 1)

        @st.block.vector
        def _(dve):
            link = Chain(dve, step)
            for s in range(SEGS):
                before = carry[:, :] if s == 0 else H[:, s - 1, :, SEG - 1]
                last = H[:, s, :, SEG - 1]
                link(nc.vector.tensor_tensor(scratch[:, :], first[:, s, :], before, ALU.mult))
                link(nc.vector.tensor_tensor(H[:, s, :, 0], H[:, s, :, 0], scratch[:, :], ALU.add))
                segment = H[:, s, :, :].rearrange("p n j -> p (n j)")
                link(nc.vector.tensor_tensor_scan(segment, dA[:, s, :, :].rearrange("p n j -> p (n j)"), segment,
                                                  0.0, ALU.mult, ALU.add))
                nc.vector.scalar_tensor_tensor(out=scratch[:, :], in0=last, scalar=1.0, in1=last, op0=ALU.mult,
                                               op1=ALU.mult, accum_out=sums[:, :]).then_inc(sums_ready, 1)
                dve.wait_ge(norm_ready, s + 1)
                link(nc.vector.tensor_scalar(fac[:, :], fac[:, :], 1e-8, None, ALU.add))
                link(nc.vector.reciprocal(fac[:, :], fac[:, :]))
                link(nc.vector.tensor_scalar(fac[:, :], fac[:, :], 20.0, 1.0, ALU.mult, ALU.min))
                link(nc.vector.tensor_scalar(last, last, fac[:, 0:1], None, ALU.mult))
            link(nc.vector.tensor_copy(carry[:, :], H[:, SEGS - 1, :, SEG - 1]))
            for g, (n0, n) in enumerate(groups):
                for c in range(2):
                    link(nc.vector.tensor_tensor(states(dA, c, n0, n), states(H, c, n0, n), rows(4 + g, n), ALU.mult))
            for c in range(2):
                link(nc.vector.tensor_reduce(
                    y[:, c, cols].rearrange("p (s j) -> p s j", j=SEG),
                    dA[:, :, c * SSM_N:(c + 1) * SSM_N, :].rearrange("p s n j -> p s j n"), AX_X, ALU.add))



ROUND = 1.5 * 2.0 ** 23


def quantize_weights(core, raw, out):
    nc = core.nc
    with core.stage() as st, nc.sbuf_tensor(f"wq_abs{nc.next_id()}", [P, 2, 512], F32) as mag, \
            nc.sbuf_tensor(f"wq_sum{nc.next_id()}", [P, 2], F32) as sums, \
            nc.sbuf_tensor(f"wq_mean{nc.next_id()}", [P, 2], F32) as mean, \
            nc.sbuf_tensor(f"wq_inv{nc.next_id()}", [P, 2], F32) as inv:
        sums_ready, total_ready, step = st.sem("sums_ready"), st.sem("total_ready"), st.sem("step")

        @st.block.sync
        def _(sp):
            sp.sem_clear(st.stale)

        @st.block.scalar
        def _(act):
            for i in range(2):
                nc.scalar.activation(mag[:, i, :], raw[i], ACT.Abs, accum_out=sums[:, i:i + 1]).then_inc(sums_ready, 1)

        @st.block.tensor
        def _(pe):
            pe.wait_ge(sums_ready, 2)
            nc.tensor.matmul(core.ps[0][:, 0:2], core.c("ones"), sums[:, :], start=True, stop=True)\
              .then_inc(total_ready, 1)

        @st.block.vector
        def _(dve):
            link = Chain(dve, step)
            dve.wait_ge(total_ready, 1)
            link(nc.vector.tensor_scalar(mean[:, :], core.ps[0][:, 0:2], 1.0 / (P * 512), 1e-5, ALU.mult, ALU.max))
            link(nc.vector.reciprocal(inv[:, :], mean[:, :]))
            for i in range(2):
                link(nc.vector.tensor_scalar(out[i], raw[i], inv[:, i:i + 1], ROUND, ALU.mult, ALU.add))
                link(nc.vector.tensor_scalar(out[i], out[i], ROUND, 1.0, ALU.subtract, ALU.min))
                link(nc.vector.tensor_scalar(out[i], out[i], -1.0, mean[:, i:i + 1], ALU.max, ALU.mult))


def quantize_tokens(core, src, dst, chunks):
    nc = core.nc
    width = chunks * P
    with core.stage() as st, nc.sbuf_tensor(f"tq{nc.next_id()}", [P, QT, width], F32) as q, \
            nc.sbuf_tensor(f"tq_max{nc.next_id()}", [P, QT], F32) as top, \
            nc.sbuf_tensor(f"tq_scale{nc.next_id()}", [P, QT], F32) as scale:
        turned, step, quantized, back, evac = (st.sem(n) for n in ("turned", "step", "quantized", "back", "evac"))

        @st.block.sync
        def _(sp):
            sp.sem_clear(st.stale)

        @st.block.tensor
        def _(pe):
            for t in range(QT):
                for c in range(chunks):
                    mm = nc.tensor.transpose(core.ps[t][:, c * P:(c + 1) * P], src[:, c, t * P:(t + 1) * P],
                                             core.ident)
                mm.then_inc(turned, 1)
            pe.wait_ge(quantized, QT)
            for c in range(chunks):
                for t in range(QT):
                    mm = nc.tensor.transpose(core.ps[4 + c][:, t * P:(t + 1) * P], q[:, t, c * P:(c + 1) * P],
                                             core.ident)
                mm.then_inc(back, 1)

        @st.block.vector
        def _(dve):
            link = Chain(dve, step)
            for t in range(QT):
                dve.wait_ge(turned, t + 1)
                one = slice(t, t + 1)
                link(nc.vector.tensor_reduce(top[:, one], core.ps[t][:, 0:width], AX_X, ALU.max,
                                             apply_absolute_value=True))
                link(nc.vector.tensor_scalar(top[:, one], top[:, one], 1e-5, None, ALU.max))
                link(nc.vector.reciprocal(scale[:, one], top[:, one]))
                link(nc.vector.tensor_scalar(scale[:, one], scale[:, one], 127.0, None, ALU.mult))
                link(nc.vector.tensor_scalar(top[:, one], top[:, one], 1.0 / 127.0, None, ALU.mult))
                link(nc.vector.tensor_scalar(q[:, t, :], core.ps[t][:, 0:width], scale[:, one], ROUND,
                                             ALU.mult, ALU.add))
                link(nc.vector.tensor_scalar(q[:, t, :], q[:, t, :], ROUND, 127.0, ALU.subtract, ALU.min))
                nc.vector.tensor_scalar(q[:, t, :], q[:, t, :], -128.0, top[:, one], ALU.max, ALU.mult)\
                  .then_inc(quantized, 1)

        @st.block.scalar
        def _(act):
            for c in range(chunks):
                act.wait_ge(back, c + 1)
                nc.scalar.copy(dst[:, c, :], core.ps[4 + c][:, :]).then_inc(evac, 1)


def bit_ffn(core, b, arena):
    nc = core.nc
    w = core.weights("L2f", arena)
    M = 4
    with ExitStack() as mem:
        def tmp(name, shape):
            return mem.enter_context(nc.sbuf_tensor(f"l2f_{name}_{nc.next_id()}", shape, F32))
        W, xq = tmp("W", [P, 2, 512]), tmp("xq", [P, 1, S])
        h, z, hq = tmp("h", [P, M, S + 2]), tmp("z", [P, M, S]), tmp("hq", [P, M, S])
        quantize_weights(core, [w("w1"), w("w2")], [W[:, i, :] for i in range(2)])
        quantize_tokens(core, core.X.unsqueeze(1), xq, 1)
        dense(core, M, lambda k, m: W[:, 0, m * P:(m + 1) * P], lambda k: xq[:, 0, :], lambda m: h[:, m, 1:S + 1])
        with core.stage() as st:
            step, conv_ready, silu_ready = (st.sem(n) for n in ("step", "conv_ready", "silu_ready"))

            @st.block.sync
            def _(sp):
                sp.sem_clear(st.stale)

            @st.block.vector
            def _(dve):
                link = Chain(dve, step)
                link(nc.vector.memset(h[:, :, 0:1], 0.0))
                link(nc.vector.memset(h[:, :, S + 1:S + 2], 0.0))
                for m in range(M):
                    link(nc.vector.tensor_scalar(z[:, m, :], h[:, m, 0:S], w("conv_w", 3 * m, 3 * m + 1),
                                                 w("conv_b", m, m + 1), ALU.mult, ALU.add))
                    for j in (1, 2):
                        ins = nc.vector.scalar_tensor_tensor(
                            out=z[:, m, :], in0=h[:, m, j:j + S], scalar=w("conv_w", 3 * m + j, 3 * m + j + 1),
                            in1=z[:, m, :], op0=ALU.mult, op1=ALU.add)
                        if j == 1:
                            link(ins)
                        else:
                            ins.then_inc(conv_ready, 1)

            @st.block.scalar
            def _(act):
                for m in range(M):
                    act.wait_ge(conv_ready, m + 1)
                    nc.scalar.activation(z[:, m, :], z[:, m, :], ACT.Silu).then_inc(silu_ready, 1)

        quantize_tokens(core, z, hq, M)
        dense(core, 1, lambda k, m: W[:, 1, k * P:(k + 1) * P], lambda k: hq[:, k, :], lambda m: core.Y[:, :],
              kcount=M)
    residual_norm(core)



def experts(core, b, arena):
    nc = core.nc
    w = core.weights("L3f", arena)
    M = (EXPERTS + 1) * EXPERT_H // P
    with ExitStack() as mem:
        def tmp(name, shape, dt=F32):
            return mem.enter_context(nc.sbuf_tensor(f"l3f_{name}_{nc.next_id()}", shape, dt))
        h = tmp("h", [P, M, S])
        logits, best, index = tmp("logits", [P, QT, 8]), tmp("best", [P, QT, 8]), tmp("index", [P, QT, 8], U32)
        indexf, chosen, share = tmp("indexf", [P, QT, 8]), tmp("chosen", [P, QT, 8]), tmp("share", [P, QT, 8])
        total, shareT = tmp("total", [P, QT]), tmp("shareT", [EXPERTS, S])
        gated(core, M, lambda m: w("W1", m * P, (m + 1) * P), lambda m: w("W3", m * P, (m + 1) * P), core.X,
              lambda m: h[:, m, :], ACT.Silu)
        with core.stage() as st:
            product_ready, step, arg_ready, exp_ready, share_ready, turned, evac, spread, weighted = (
                st.sem(n) for n in ("product_ready", "step", "arg_ready", "exp_ready", "share_ready", "turned",
                                    "evac", "spread", "weighted"))

            @st.block.sync
            def _(sp):
                sp.sem_clear(st.stale)

            @st.block.tensor
            def _(pe):
                for t in range(QT):
                    mm = nc.tensor.matmul(core.ps[0][:, t * 8:(t + 1) * 8], core.X[:, t * P:(t + 1) * P], w("Wg"),
                                          start=True, stop=True)
                mm.then_inc(product_ready, 1)
                pe.wait_ge(share_ready, 1)
                for t in range(QT):
                    mm = nc.tensor.transpose(core.ps[1][0:EXPERTS, t * P:(t + 1) * P], share[:, t, :], core.ident)
                mm.then_inc(turned, 1)
                pe.wait_ge(evac, 1)
                for e in range(EXPERTS):
                    if e >= 4:
                        pe.wait_ge(weighted, 2 * (e - 3))
                    nc.tensor.matmul(core.ps[2 + e % 4][:, :],
                                     core.ident[0:EXPERTS, e:e + 1].broadcast_to([EXPERTS, P]), shareT[:, :],
                                     start=True, stop=True).then_inc(spread, 1)

            @st.block.scalar
            def _(act):
                act.wait_ge(arg_ready, 1)
                nc.scalar.activation(share[:, :, :], share[:, :, :], ACT.Exp).then_inc(exp_ready, 1)
                act.wait_ge(turned, 1)
                nc.scalar.copy(shareT[:, :], core.ps[1][0:EXPERTS, :]).then_inc(evac, 1)

            @st.block.vector
            def _(dve):
                link = Chain(dve, step)
                dve.wait_ge(product_ready, 1)
                link(nc.vector.tensor_copy(logits[:, :, :].rearrange("p t e -> p (t e)"), core.ps[0][:, 0:QT * 8]))
                for t in range(QT):
                    link(nc.vector.max(best[:, t, :], logits[:, t, :]))
                    link(nc.vector.max_index(index[:, t, :], best[:, t, :], logits[:, t, :]))
                nc.vector.tensor_tensor(share[:, :, :], logits[:, :, :], best[:, :, 0:1].broadcast_to([P, QT, 8]),
                                        ALU.subtract).then_inc(arg_ready, 1)
                link(nc.vector.tensor_copy(indexf[:, :, :], index[:, :, :]))
                number = core.c("number").unsqueeze(1).broadcast_to([P, QT, 8])
                link(nc.vector.tensor_tensor(chosen[:, :, :], number, indexf[:, :, 0:1].broadcast_to([P, QT, 8]),
                                             ALU.is_equal))
                link(nc.vector.tensor_tensor(logits[:, :, :], number, indexf[:, :, 1:2].broadcast_to([P, QT, 8]),
                                             ALU.is_equal))
                link(nc.vector.tensor_tensor(chosen[:, :, :], chosen[:, :, :], logits[:, :, :], ALU.add))
                dve.wait_ge(exp_ready, 1)
                link(nc.vector.tensor_tensor(share[:, :, :], share[:, :, :], chosen[:, :, :], ALU.mult))
                link(nc.vector.tensor_reduce(total[:, :], share[:, :, :], AX_X, ALU.add))
                link(nc.vector.reciprocal(total[:, :], total[:, :]))
                nc.vector.tensor_tensor(share[:, :, :], share[:, :, :], total[:, :].unsqueeze(2)
                                        .broadcast_to([P, QT, 8]), ALU.mult).then_inc(share_ready, 1)
                for e in range(EXPERTS):
                    dve.wait_ge(spread, e + 1)
                    for i in range(2):
                        nc.vector.tensor_tensor(h[:, 2 * e + i, :], h[:, 2 * e + i, :], core.ps[2 + e % 4][:, :],
                                                ALU.mult).then_inc(weighted, 1)
        dense(core, 1, lambda k, m: w("W2", k * P, (k + 1) * P), lambda k: h[:, k, :], lambda m: core.Y[:, :],
              kcount=M)
    residual_norm(core)


def run_sublayers(core, b, order):
    arena = 0
    for i, (name, f) in enumerate(order):
        if name == "L1f_a":
            f(core, b, arena)
            continue
        nxt = order[(i + 1) % len(order)][0]
        turn(core, arena, core.dram[nxt][0, :, :])
        f(core, b, arena)
        arena = 1 - arena


SUBLAYERS = [("L0x", cross_null), ("L0f", ternary_ffn), ("L1a", latent_attention), ("L1x", cross_plain),
             ("L1f_a", local_transformer), ("L2a", state_space), ("L2x", cross_masked), ("L2f", bit_ffn),
             ("L3a", projected_attention), ("L3x", cross_narrow), ("L3f", experts)]
WITH_RWKV = True


def build(nc, dram, cols):
    with ExitStack() as ctx:
        core = Core(nc, ctx, dram, cols)
        with nc.Block() as block:
            zeroed = core.banks[0][0]

            @block.sync
            def _(sp):
                first = dram[SUBLAYERS[0][0]] if SUBLAYERS else None
                if first is not None:
                    sp.dma_start(core.arenas[0][:, 0:first.shape[-1]], first[0, :, :]).then_inc(core.loaded[0], 16)
                sp.dma_start(core.const[:, :], dram["const"][0, :, :]).then_inc(core.resident_loaded, 16)
                sp.dma_start(core.rwkv[:, :], dram["L0a"][0, :, :]).then_inc(core.resident_loaded, 16)
                sp.wait_ge(core.resident_loaded, 32)

            @block.vector
            def _(dve):
                nc.vector.memset(core.XP[:, 0:PAD], 0.0).then_inc(zeroed, 1)

        with nc.Fori(0, B) as b:
            with nc.Block() as block:
                @block.sync
                def _(sp):
                    for span in core.spans:
                        sp.sem_clear(span)
                    sp.dma_start(core.X, dram["x"][b, :, :]).then_inc(core.tokens_loaded, 16)
                    sp.dma_start(core.ctxT[:, :], dram["ctx"][b, :, :]).then_inc(core.tokens_loaded, 16)
                    sp.wait_ge(core.tokens_loaded, 32)
                    sp.sem_clear(core.tokens_loaded)
            if WITH_RWKV:
                rwkv(core)
            run_sublayers(core, b, SUBLAYERS)
            with nc.Block() as block:
                @block.sync
                def _(sp):
                    sp.dma_start(dram["out"][b, :, :], core.X).then_inc(core.stored, 16)
                    sp.wait_ge(core.stored, 16)
                    sp.sem_clear(core.stored)
        with nc.Block() as block:
            @block.sync
            def _(sp):
                if SUBLAYERS:
                    sp.wait_ge(core.loaded[0], 16)



class Pack:

    def __init__(self):
        self.parts, self.cols, self.width = [], {}, 0

    def add(self, name, a):
        a = np.asarray(a)
        if a.ndim == 1:
            a = a[:, None]
        a = np.concatenate([a, np.zeros((P - a.shape[0], a.shape[1]), a.dtype)], 0)
        self.cols[name] = (self.width, self.width + a.shape[1])
        self.width += a.shape[1]
        self.parts.append(a)

    def array(self, width=None):
        width = width or self.width
        pad = np.zeros((P, width - self.width), np.float32)
        return np.ascontiguousarray(np.concatenate(self.parts + [pad], 1))


def by_chunk(a):
    k = a.shape[0] // P
    return a.reshape(k, P, -1).transpose(1, 0, 2).reshape(P, -1)


def cols_of(v):
    return v.reshape(-1, P).T


def by_tile(a):
    return a.reshape(QT, P, -1).transpose(1, 0, 2).reshape(P, -1).astype(np.float32)


def constants():
    c = Pack()
    c.add("ident", np.eye(P, dtype=np.float32))
    c.add("average", np.full((P, P), 1.0 / P, np.float32))
    c.add("ones", np.ones((P, P), np.float32))
    heads = np.arange(P) // SH
    c.add("head_scale", (heads[:, None] % 4 == np.arange(4)[None, :]).astype(np.float32) * np.float32(SH ** -0.5))
    c.add("number", np.tile(np.arange(8, dtype=np.float32), (P, 1)))
    pos = np.arange(S, dtype=np.float32)
    inv = (1.0 / np.float32(10000.0) ** (np.arange(0, SH, 2, dtype=np.float32) / SH)).astype(np.float32)
    ang = pos[:, None] * inv[None, :]
    c.add("rot_cos", by_tile(np.concatenate([np.cos(ang), np.cos(ang)], 1)))
    c.add("rot_sin", by_tile(np.concatenate([-np.sin(ang), np.sin(ang)], 1)))
    half = np.arange(0, DH, 2, dtype=np.float32)
    inv = (1.0 / np.float32(10000.0) ** (half / DH)).astype(np.float32)
    ang = pos[:, None] * inv[None, :]
    base = (half + np.float32(0.4 * DH)) / np.float32(1.4 * DH)
    length = base[None, :] ** ((pos - S // 2) / np.float32(WINDOW // 2))[:, None]
    cos, sin = np.cos(ang), np.sin(ang)
    c.add("local_cos", by_tile(np.concatenate([cos * length] * 2 + [cos / length] * 2, 1)))
    c.add("local_sin", by_tile(np.concatenate([-sin * length, sin * length, -sin / length, sin / length], 1)))
    i, j = np.arange(TILE)[:, None], np.arange(LOCAL_KEYS)[None, :] - WINDOW
    seen = np.stack([(j <= i) & (j >= i - WINDOW) & (t * TILE + j >= 0) for t in range(QT)])
    c.add("local_mask", by_tile(np.where(seen, 0.0, MASKED).reshape(S, LOCAL_KEYS)))
    return c


def packs(x):
    out = {}
    p = out["L0a"] = Pack()
    for n in ("Wk", "Wv", "Wr", "Wo"):
        p.add(n, x["L0_attn_" + n].T)
    for n in ("W", "U"):
        p.add(n, x["L0_attn_" + n])
    for n in "kvr":
        p.add("mix_" + n, x["L0_attn_time_mix_" + n].reshape(-1))
    p = out["L0x"] = Pack()
    p.add("Wq", x["L0_xattn_Wq"])
    p.add("Wk", x["L0_xattn_Wkv"][:, :INNER])
    p.add("Wv", x["L0_xattn_Wkv"][:, INNER:])
    p.add("Wo", by_chunk(x["L0_xattn_Wout"]))
    p.add("g_norm", x["L0_xattn_g_norm"])
    p.add("g_out", x["L0_xattn_g_out"])
    p.add("null_k", np.concatenate([x["L0_xattn_null_kv"][0]] * 2))
    p = out["L0f"] = Pack()
    p.add("w1", x["L0_ffn_w1_w"].T)
    p.add("w2", x["L0_ffn_w2_w"].T)
    p.add("h1", by_chunk(x["L0_ffn_h1_w"].T))
    p.add("h2", by_chunk(x["L0_ffn_h2_w"].T))
    p.add("w3", by_chunk(x["L0_ffn_w3_w"].T))
    for n, k in (("s1", "w1_s"), ("s2", "w2_s"), ("sh1", "h1_s"), ("sh2", "h2_s"), ("s3", "w3_s")):
        p.add(n, cols_of(x["L0_ffn_" + k]))
    p = out["L1x"] = Pack()
    for n in ("Wq", "Wk", "Wv"):
        p.add(n, x["L1_xattn_" + n])
    p.add("Wo", by_chunk(x["L1_xattn_Wo"]))
    p.add("bo", x["L1_xattn_bo"])
    p = out["L2x"] = Pack()
    p.add("Wq", x["L2_xattn_Wq"])
    p.add("Wk", x["L2_xattn_Wkv"][:, :INNER])
    p.add("Wv", x["L2_xattn_Wkv"][:, INNER:])
    p.add("Wo", by_chunk(x["L2_xattn_Wo"]))
    p.add("gamma", x["L2_xattn_ln_gamma"])
    p.add("beta", x["L2_xattn_ln_beta"])
    p.add("bo", x["L2_xattn_bo"])
    def rows_of(v):
        return np.tile(v[None, :], (P, 1))

    p = out["L1a"] = Pack()
    p.add("Wqkv", np.concatenate([x["L1_attn_Wq"].T, x["L1_attn_Wkv"].T], 1))
    p.add("Wo", x["L1_attn_Wo"].T)
    p.add("bo", x["L1_attn_bo"])
    p.add("ln_g", rows_of(x["L1_attn_ln_g"]))
    p.add("ln_b", rows_of(x["L1_attn_ln_b"]))
    at, key = np.arange(S)[:, None], np.arange(S)[None, :] - (S - LAT)
    p.add("latent_mask", by_tile(np.where((key < 0) | ((at < LAT) & (key <= at)), 0.0, MASKED)))
    p = out["L3a"] = Pack()
    for n in ("Wq", "Wk", "Wv"):
        p.add(n, x["L3_attn_" + n])
    for n in ("bq", "bk", "bv"):
        p.add(n, x["L3_attn_" + n])
    block = np.zeros((P, P), np.float32)
    for h in range(HEADS):
        block[h * SH:(h + 1) * SH, h * SH:(h + 1) * SH] = x["L3_attn_Wp"]
    p.add("Wp", block)
    p = out["L3x"] = Pack()
    p.add("Wq", x["L3_xattn_q_w"])
    p.add("Wk", x["L3_xattn_kv_w"][:, :D])
    p.add("Wv", x["L3_xattn_kv_w"][:, D:])
    p.add("Wo", x["L3_xattn_proj_w"])
    p.add("bq", x["L3_xattn_q_b"])
    p.add("bk", x["L3_xattn_kv_b"][:D])
    p.add("bv", x["L3_xattn_kv_b"][D:])
    p.add("bo", x["L3_xattn_proj_b"])
    p = out["L2a"] = Pack()
    p.add("W_in", x["L2_attn_W_in"].T)
    p.add("W_dt", by_chunk(x["L2_attn_W_dt"].T))
    p.add("W_BC", by_chunk(np.concatenate([x["L2_attn_W_B"].T, x["L2_attn_W_C"].T], 1)))
    p.add("W_out", by_chunk(x["L2_attn_W_out"].T))
    p.add("norm_w", x["L2_attn_norm_w"])
    p.add("conv_w", by_chunk(x["L2_attn_conv_w"][:, 0, :]))
    p.add("conv_b", cols_of(x["L2_attn_conv_b"]))
    p.add("b_dt", cols_of(x["L2_attn_b_dt"]))
    p.add("D", cols_of(x["L2_attn_D_param"]))
    p.add("A_log", by_chunk(x["L2_attn_A_log"]))
    p.add("residual", rows_of(x["L2_attn_residual_scale"].reshape(1)))
    p = out["L2f"] = Pack()
    p.add("w1", x["L2_ffn_w1"].T)
    p.add("w2", by_chunk(x["L2_ffn_w2"].T))
    p.add("conv_w", by_chunk(x["L2_ffn_conv_w"][:, 0, :]))
    p.add("conv_b", cols_of(x["L2_ffn_conv_b"]))
    p = out["L3f"] = Pack()
    p.add("Wg", x["L3_ffn_Wg"].T)
    for n in ("1", "3"):
        p.add("W" + n, np.concatenate([a.T for a in x["L3_ffn_W" + n]] + [x["L3_ffn_sw" + n].T], 1))
    p.add("W2", np.concatenate([by_chunk(a.T) for a in x["L3_ffn_W2"]] + [by_chunk(x["L3_ffn_sw2"].T)], 1))

    out = {k: [p] for k, p in out.items()}
    out["L1f_a"], out["L1f_f"] = [], []
    for i in range(DEPTH):
        p = Pack()
        out["L1f_a"].append(p)
        p.add("Wqkv", x["L1_ffn_Wqkv"][i])
        p.add("Wo", by_chunk(x["L1_ffn_Wo"][i]))
        q, k = x["L1_ffn_q_scale"][i], x["L1_ffn_k_scale"][i]
        p.add("qk_scale", rows_of(np.concatenate([q, k])))
        p.add("qk_scale_swapped", rows_of(np.concatenate([a[s] for a in (q, k) for s in
                                                          (slice(DH // 2, DH), slice(0, DH // 2))])))
        p = Pack()
        out["L1f_f"].append(p)
        W1, b1 = x["L1_ffn_W1"][i], x["L1_ffn_b1"][i]

        def chunk_pad(a):
            more = -a.shape[0] % P
            return np.concatenate([a, np.zeros((more,) + a.shape[1:], a.dtype)], 0)
        p.add("W1_lin", W1[:, :FFN_INNER])
        p.add("W1_gate", W1[:, FFN_INNER:])
        p.add("W2", by_chunk(chunk_pad(x["L1_ffn_W2"][i])))
        p.add("ln_g", x["L1_ffn_ln_g"][i])
        p.add("ln_b", x["L1_ffn_ln_b"][i])
        p.add("b1_lin", cols_of(chunk_pad(b1[:FFN_INNER])))
        p.add("b1_gate", cols_of(chunk_pad(b1[FFN_INNER:])))
        p.add("b2", x["L1_ffn_b2"][i])
    return out


def kernel(**inputs):
    import concourse.bacc as _bacc
    from concourse.bass_utils import run_bass_kernel_spmd as _run

    x = {k: np.asarray(v) for k, v in inputs.items()}
    null_v = np.tile(x["L0_xattn_null_kv"][1], HEADS)
    arrays = {
        "x": x["x"].transpose(0, 2, 1),
        "ctx": x["ctx_768"].transpose(0, 2, 1),
        "mask_b": x["mask_BxS2_bf1"].view(np.uint8),
        "mask_q": np.ascontiguousarray(x["mask_1x1xSxS2_bk0"].reshape(QT, P, CTX_LEN).transpose(1, 0, 2))
        .reshape(P, QT * CTX_LEN).view(np.uint32),
        "null_v": np.stack([null_v, np.zeros_like(null_v)]),
    }
    cols = {}
    packed = dict(packs(x), const=[constants()])
    names = [name for name, _ in SUBLAYERS]
    if "L1f_a" in names:
        packed["L1f_a"] = packed["L1f_a"] + packed[names[(names.index("L1f_a") + 1) % len(names)]][:1]
    for name, rounds in packed.items():
        width = max(p.width for p in rounds)
        arrays[name] = np.stack([p.array(width) for p in rounds])
        cols[name] = dict(rounds[0].cols, width=width)
    arrays = {k: np.ascontiguousarray(a) for k, a in arrays.items()}

    nc = _bacc.Bacc("TRN2", target_bir_lowering=False, num_devices=1)
    dram = {k: nc.dram_tensor("in_" + k, a.shape, mybir.dt.from_np(a.dtype), kind="ExternalInput").ap()
            for k, a in arrays.items()}
    dram["out"] = nc.dram_tensor("out", (B, D, S), F32, kind="ExternalOutput").ap()
    build(nc, dram, cols)
    r = _run(nc, [{"in_" + k: a for k, a in arrays.items()}], core_ids=[0])
    return r.results[0]["out"].transpose(0, 2, 1)
```

```python
from contextlib import ExitStack, contextmanager
import math

import numpy as np

import concourse.bass as bass
from concourse import mybir

P = 128
B, S, D = 4, 512, 128
TILE = 128
QT = S // TILE
CTX_LEN, CTX_D = 154, 96
HEADS = 16
DH = 64
INNER = HEADS * DH
CHUNKS = INNER // P
SH = D // HEADS
LAT = S - (256 - 64)
DEPTH = 6
WINDOW = 32
LOCAL_KEYS = WINDOW + TILE
FFN_INNER = int(D * 4 * 2 / 3)
SSM_D, SSM_N, CONV = 256, 16, 4
EXPERTS, EXPERT_H = 8, 256
LN_EPS = 1e-5
MASKED = -1e30
PAD = 4

F32 = mybir.dt.float32
U8 = mybir.dt.uint8
U32 = mybir.dt.uint32
I32 = mybir.dt.int32
ALU = mybir.AluOpType
ACT = mybir.ActivationFunctionType
AX_X = mybir.AxisListType.X


class Chain:

    def __init__(self, eng, sem):
        self.eng, self.sem, self.steps = eng, sem, 0

    def __call__(self, ins):
        self.steps += 1
        ins.then_inc(self.sem, 1)
        self.eng.wait_ge(self.sem, self.steps)


ROOT_STEPS = 13


def inverse_root(eng, link, x, y, u):
    MAGIC = 0x5F3759DF
    link(eng.tensor_scalar(y.bitcast(I32), x.bitcast(I32), -0.5, float(MAGIC), ALU.mult, ALU.add))
    for _ in range(3):
        link(eng.tensor_tensor(u, y, y, ALU.mult))
        link(eng.tensor_tensor(u, u, x, ALU.mult))
        link(eng.tensor_scalar(u, u, -0.5, 1.5, ALU.mult, ALU.add))
        link(eng.tensor_tensor(y, y, u, ALU.mult))


class Stage:

    def __init__(self, block, bank, stale):
        self.block, self.bank, self.stale, self.used = block, bank, stale, 0

    def sem(self, name):
        self.used += 1
        return self.bank[self.used - 1]


class Core:

    BANK = 30

    def __init__(self, nc, ctx, dram, cols):
        self.nc, self.ctx, self.dram, self.cols = nc, ctx, dram, cols
        self.parity = 0
        self.banks = [[ctx.enter_context(nc.semaphore(f"bank{i}_{j}")) for j in range(self.BANK)]
                      for i in range(2)]
        self.spans = [range(bank[0].num, bank[-1].num + 1) for bank in self.banks]
        self.loaded = [ctx.enter_context(nc.semaphore(f"weights_loaded{i}")) for i in range(2)]
        self.resident_loaded = ctx.enter_context(nc.semaphore("resident_loaded"))
        self.tokens_loaded = ctx.enter_context(nc.semaphore("tokens_loaded"))
        self.stored = ctx.enter_context(nc.semaphore("stored"))
        self.ps = [ctx.enter_context(nc.psum_tensor(f"ps{i}", [P, 512], F32)) for i in range(8)]
        self.XP = self.buf("XP", [P, PAD + S])
        self.X = self.XP[:, PAD:PAD + S]
        self.Y = self.buf("Y", [P, S])
        self.ctxT = self.buf("ctxT", [CTX_D, CTX_LEN])
        self.const = self.buf("const", [P, cols["const"]["width"]])
        self.rwkv = self.buf("rwkv", [P, cols["L0a"]["width"]])
        self.arena_width = max(v["width"] for k, v in cols.items() if k not in ("const", "L0a"))
        self.arenas = [self.buf(f"arena{i}", [P, self.arena_width]) for i in range(2)]
        self.ident = self.c("ident")
        self.average = self.c("average")

    def buf(self, name, shape, dt=F32):
        return self.ctx.enter_context(self.nc.sbuf_tensor(name, shape, dt))

    def c(self, name):
        lo, hi = self.cols["const"][name]
        return self.const[:, lo:hi]

    def weights(self, pack, arena):
        mem = self.rwkv if arena is None else self.arenas[arena]

        def view(name, a=0, b=None):
            lo, hi = self.cols[pack][name]
            return mem[:, lo + a:(hi if b is None else lo + b)]
        return view

    @contextmanager
    def stage(self):
        self.parity ^= 1
        with self.nc.Block() as block:
            yield Stage(block, self.banks[self.parity], self.spans[1 - self.parity])


def turn(core, arena, prefetch):
    with core.nc.Block() as block:
        @block.sync
        def _(sp):
            for span in core.spans:
                sp.sem_clear(span)
            sp.wait_ge(core.loaded[arena], 16)
            sp.sem_clear(core.loaded[arena])
            if prefetch is not None:
                width = prefetch.shape[-1]
                sp.dma_start(core.arenas[1 - arena][:, 0:width], prefetch).then_inc(core.loaded[1 - arena], 16)


def normalize(core, src, dst, add=None, gain=None, shift=None, centred=True, eps=LN_EPS):
    nc = core.nc
    with core.stage() as st, ExitStack() as mem:
        def tmp(name, shape):
            return mem.enter_context(nc.sbuf_tensor(f"norm_{name}_{nc.next_id()}", shape, F32))
        z, d, sq, std = tmp("z", [P, S]), tmp("d", [P, S]), tmp("sq", [P, S]), tmp("std", [P, QT])
        epsc, warm = tmp("eps", [P, 1]), tmp("warm", [P, 1])
        z_ready, mean_ready, d_ready, sq_ready, var_ready, std_ready, inv_ready, spread, done, eps_ready, warmed = (
            st.sem(n) for n in ("z_ready", "mean_ready", "d_ready", "sq_ready", "var_ready", "std_ready",
                                "inv_ready", "spread", "done", "eps_ready", "warmed"))
        mean, var, inv = core.ps[0:2], core.ps[2:4], core.ps[4:6]
        summed = z[:, :] if add is not None else src
        centre = d[:, :] if centred else summed
        HALF = S // 2
        halves = [slice(0, HALF), slice(HALF, S)]

        @st.block.sync
        def _(sp):
            sp.sem_clear(st.stale)

        @st.block.gpsimd
        def _(pool):
            nc.gpsimd.memset(epsc[:, :], eps).then_inc(eps_ready, 1)

        @st.block.vector
        def _(dve):
            if add is not None:
                for cols in halves:
                    nc.vector.tensor_tensor(summed[:, cols], src[:, cols], add[:, cols], ALU.add).then_inc(z_ready, 1)
                dve.wait_ge(z_ready, 2)
            if centred:
                for i, cols in enumerate(halves):
                    dve.wait_ge(mean_ready, i + 1)
                    nc.vector.tensor_tensor(centre[:, cols], summed[:, cols], mean[i][:, 0:HALF], ALU.subtract)\
                      .then_inc(d_ready, 1)
                dve.wait_ge(d_ready, 2)
            for i in range(2):
                dve.wait_ge(std_ready, i + 1)
                nc.vector.reciprocal(std[:, 2 * i:2 * i + 2], std[:, 2 * i:2 * i + 2]).then_inc(inv_ready, 1)
            for i, cols in enumerate(halves):
                dve.wait_ge(spread, i + 1)
                nc.vector.scalar_tensor_tensor(out=dst[:, cols], in0=centre[:, cols], scalar=1.0 if gain is None else gain,
                                               in1=inv[i][:, 0:HALF], op0=ALU.mult, op1=ALU.mult).then_inc(done, 1)
            if shift is not None:
                dve.wait_ge(done, 2)
                nc.vector.tensor_scalar(dst, dst, shift, None, ALU.add).then_inc(done, 1)

        @st.block.tensor
        def _(pe):
            if centred:
                for i, cols in enumerate(halves):
                    if add is not None:
                        pe.wait_ge(z_ready, i + 1)
                    nc.tensor.matmul(mean[i][:, 0:HALF], core.average, summed[:, cols], start=True, stop=True)\
                      .then_inc(mean_ready, 1)
            for i in range(2):
                pe.wait_ge(sq_ready, i + 1)
                for t in (0, 1):
                    mm = nc.tensor.matmul(var[i][:, t:t + 1], sq[:, (2 * i + t) * P:(2 * i + t + 1) * P],
                                          core.average[:, 0:1], start=True, stop=True)
                mm.then_inc(var_ready, 1)
            for i in range(2):
                pe.wait_ge(inv_ready, i + 1)
                for t in (0, 1):
                    mm = nc.tensor.matmul(inv[i][:, t * P:(t + 1) * P],
                                          std[:, 2 * i + t:2 * i + t + 1].broadcast_to([P, P]), core.ident,
                                          start=True, stop=True)
                mm.then_inc(spread, 1)

        @st.block.scalar
        def _(act):
            act.wait_ge(eps_ready, 1)
            nc.scalar.activation(warm[:, :], epsc[:, :], ACT.Sqrt).then_inc(warmed, 1)
            for i, cols in enumerate(halves):
                if centred:
                    act.wait_ge(d_ready, i + 1)
                elif add is not None:
                    act.wait_ge(z_ready, i + 1)
                nc.scalar.activation(sq[:, cols], centre[:, cols], ACT.Square).then_inc(sq_ready, 1)
            for i in range(2):
                act.wait_ge(var_ready, i + 1)
                nc.scalar.activation(std[:, 2 * i:2 * i + 2], var[i][:, 0:2], ACT.Sqrt, bias=epsc[:, 0:1])\
                  .then_inc(std_ready, 1)


def dense(core, count, w, rhs, dst, kcount=1, func=None, scale=None, bias=None, n=S, also=None):
    nc = core.nc
    with core.stage() as st:
        product_ready = st.sem("product_ready")
        act_done, dve_done = st.sem("act_done"), st.sem("dve_done")
        BANKS = 6

        def on_scalar(m):
            return func is not None or m % 2 == 0

        @st.block.sync
        def _(sp):
            sp.sem_clear(st.stale)

        @st.block.tensor
        def _(pe):
            for m in range(count):
                if m >= BANKS:
                    if func is not None:
                        pe.wait_ge(act_done, m - BANKS + 1)
                    else:
                        pe.wait_ge(act_done if m % 2 == 0 else dve_done, (m - BANKS) // 2 + 1)
                for k in range(kcount):
                    lhs = w(k, m)
                    mm = nc.tensor.matmul(core.ps[m % BANKS][0:lhs.shape[-1], 0:n], lhs, rhs(k),
                                          start=(k == 0), stop=(k == kcount - 1))
                mm.then_inc(product_ready, 1)

        @st.block.scalar
        def _(act):
            for m in range(count):
                if on_scalar(m):
                    out = dst(m)
                    act.wait_ge(product_ready, m + 1)
                    nc.scalar.activation(out, core.ps[m % BANKS][0:out.shape[0], 0:n], func or ACT.Identity,
                                         bias=0.0 if bias is None else bias(m),
                                         scale=1.0 if scale is None else scale(m)).then_inc(act_done, 1)

        @st.block.vector
        def _(dve):
            for m in range(count):
                if not on_scalar(m):
                    out = dst(m)
                    dve.wait_ge(product_ready, m + 1)
                    nc.vector.tensor_scalar(out, core.ps[m % BANKS][0:out.shape[0], 0:n],
                                            1.0 if scale is None else scale(m),
                                            0.0 if bias is None else bias(m), ALU.mult, ALU.add).then_inc(dve_done, 1)


def gated(core, count, w_act, w_lin, rhs, dst, func, act_scale=None, act_bias=None, lin_op=ALU.mult, lin=None):
    nc = core.nc
    with core.stage() as st, nc.sbuf_tensor(f"gate_{nc.next_id()}", [P, 2, S], F32) as gate:
        products_ready, gate_ready, gated_ready = st.sem("products"), st.sem("gate"), st.sem("gated")

        @st.block.sync
        def _(sp):
            sp.sem_clear(st.stale)

        @st.block.tensor
        def _(pe):
            for m in range(count):
                if m >= 3:
                    pe.wait_ge(gated_ready, m - 2)
                for i, w in enumerate((w_act, w_lin)):
                    lhs = w(m)
                    mm = nc.tensor.matmul(core.ps[2 * (m % 3) + i][0:lhs.shape[-1], :], lhs, rhs,
                                          start=True, stop=True)
                mm.then_inc(products_ready, 1)

        @st.block.scalar
        def _(act):
            for m in range(count):
                rows = dst(m).shape[0]
                act.wait_ge(products_ready, m + 1)
                if m >= 2:
                    act.wait_ge(gated_ready, m - 1)
                nc.scalar.activation(gate[0:rows, m % 2, :], core.ps[2 * (m % 3)][0:rows, :], func,
                                     bias=0.0 if act_bias is None else act_bias(m),
                                     scale=1.0 if act_scale is None else act_scale(m)).then_inc(gate_ready, 1)

        @st.block.vector
        def _(dve):
            for m in range(count):
                out = dst(m)
                rows = out.shape[0]
                dve.wait_ge(gate_ready, m + 1)
                nc.vector.scalar_tensor_tensor(out=out, in0=core.ps[2 * (m % 3) + 1][0:rows, :],
                                               scalar=1.0 if lin is None else lin(m), in1=gate[0:rows, m % 2, :],
                                               op0=lin_op, op1=ALU.mult).then_inc(gated_ready, 1)


def residual_norm(core):
    normalize(core, core.X, core.X, add=core.Y[:, :])



def rwkv(core):
    nc = core.nc
    w = core.weights("L0a", None)
    X, Xs = core.X, core.XP[:, PAD - 1:PAD - 1 + S]
    with ExitStack() as mem:
        def tmp(name, width=S):
            return mem.enter_context(nc.sbuf_tensor(f"rwkv_{name}", [P, width], F32))
        diff, xk, xv, xr, k, v, r = (tmp(n) for n in ("diff", "xk", "xv", "xr", "k", "v", "r"))
        decay = tmp("decay", 2)
        with core.stage() as st:
            mixed, product_ready, dve_step, evac = (st.sem(n) for n in ("mixed", "product_ready", "dve_step", "evac"))

            @st.block.sync
            def _(sp):
                sp.sem_clear(st.stale)

            @st.block.vector
            def _(dve):
                link = Chain(dve, dve_step)
                link(nc.vector.tensor_tensor(diff[:, :], X, Xs, ALU.subtract))
                for out, mix in ((xk, "mix_k"), (xv, "mix_v"), (xr, "mix_r")):
                    nc.vector.scalar_tensor_tensor(out=out[:, :], in0=diff[:, :], scalar=w(mix), in1=Xs,
                                                   op0=ALU.mult, op1=ALU.add).then_inc(mixed, 1)
                dve.wait_ge(evac, 1)
                nc.vector.tensor_scalar(decay[:, 1:2], decay[:, 0:1], -1.0, None, ALU.mult).then_inc(dve_step, 1)

            @st.block.tensor
            def _(pe):
                for i, (src, name) in enumerate(((xk, "Wk"), (xv, "Wv"), (xr, "Wr"))):
                    pe.wait_ge(mixed, i + 1)
                    nc.tensor.matmul(core.ps[i][:, :], w(name), src[:, :], start=True, stop=True)\
                      .then_inc(product_ready, 1)

            @st.block.scalar
            def _(act):
                nc.scalar.activation(decay[:, 0:1], w("W"), ACT.Exp).then_inc(evac, 1)
                for i, (dst, f) in enumerate(((k, ACT.Copy), (v, ACT.Copy), (r, ACT.Sigmoid))):
                    act.wait_ge(product_ready, i + 1)
                    nc.scalar.activation(dst[:, :], core.ps[i][:, :], f).then_inc(evac, 1)

        PP, AA, BB = (tmp(n, S + 1) for n in ("PP", "AA", "BB"))
        e1b, e2b, e1, e2, kv, pmax, num = (tmp(n) for n in ("e1b", "e2b", "e1", "e2", "kv", "pmax", "num"))
        with core.stage() as st:
            args_ready, exp_ready, dve_step = (st.sem(n) for n in ("args_ready", "exp_ready", "dve_step"))
            before, now = slice(0, S), slice(1, S + 1)
            neg_decay = decay[:, 1:2]

            @st.block.sync
            def _(sp):
                sp.sem_clear(st.stale)

            @st.block.vector
            def _(dve):
                link = Chain(dve, dve_step)
                link(nc.vector.memset(PP[:, 0:1], -1e38))
                link(nc.vector.memset(AA[:, 0:1], 0.0))
                link(nc.vector.memset(BB[:, 0:1], 0.0))
                link(nc.vector.tensor_tensor_scan(PP[:, now], neg_decay.broadcast_to([P, S]), k[:, :], -1e38,
                                                  ALU.add, ALU.max))
                nc.vector.scalar_tensor_tensor(out=e1b[:, :], in0=PP[:, before], scalar=neg_decay, in1=PP[:, now],
                                               op0=ALU.add, op1=ALU.subtract).then_inc(args_ready, 1)
                nc.vector.tensor_tensor(e2b[:, :], k[:, :], PP[:, now], ALU.subtract).then_inc(args_ready, 1)
                link(nc.vector.scalar_tensor_tensor(out=pmax[:, :], in0=k[:, :], scalar=w("U"), in1=PP[:, before],
                                                    op0=ALU.add, op1=ALU.max))
                nc.vector.tensor_tensor(e1[:, :], PP[:, before], pmax[:, :], ALU.subtract).then_inc(args_ready, 1)
                nc.vector.scalar_tensor_tensor(out=e2[:, :], in0=k[:, :], scalar=w("U"), in1=pmax[:, :],
                                               op0=ALU.add, op1=ALU.subtract).then_inc(args_ready, 1)
                dve.wait_ge(exp_ready, 2)
                link(nc.vector.tensor_tensor(kv[:, :], e2b[:, :], v[:, :], ALU.mult))
                link(nc.vector.tensor_tensor_scan(AA[:, now], e1b[:, :], kv[:, :], 0.0, ALU.mult, ALU.add))
                link(nc.vector.tensor_tensor_scan(BB[:, now], e1b[:, :], e2b[:, :], 0.0, ALU.mult, ALU.add))
                dve.wait_ge(exp_ready, 4)
                link(nc.vector.tensor_tensor(num[:, :], e1[:, :], AA[:, before], ALU.mult))
                link(nc.vector.tensor_tensor(kv[:, :], e2[:, :], v[:, :], ALU.mult))
                link(nc.vector.tensor_tensor(num[:, :], num[:, :], kv[:, :], ALU.add))
                link(nc.vector.tensor_tensor(kv[:, :], e1[:, :], BB[:, before], ALU.mult))
                link(nc.vector.tensor_tensor(kv[:, :], kv[:, :], e2[:, :], ALU.add))
                link(nc.vector.reciprocal(kv[:, :], kv[:, :]))
                link(nc.vector.tensor_tensor(num[:, :], num[:, :], kv[:, :], ALU.mult))
                link(nc.vector.tensor_tensor(num[:, :], num[:, :], r[:, :], ALU.mult))

            @st.block.scalar
            def _(act):
                for i, e in enumerate((e1b, e2b, e1, e2)):
                    act.wait_ge(args_ready, i + 1)
                    nc.scalar.activation(e[:, :], e[:, :], ACT.Exp).then_inc(exp_ready, 1)

        dense(core, 1, lambda j, m: w("Wo"), lambda j: num[:, :], lambda m: core.Y[:, :])
    residual_norm(core)



class NoFeed:

    def pe(self, tile, piece):
        pass

    act = dve = pool = pe

    def before_projection(self, t):
        pass

    def before_scores(self, t, h):
        pass


ACT_COPIES = lambda g: g % 4 != 0
ACT_COPIES_LOCAL = lambda g: g % 2 == 1


def attention(core, dh, q_of, k_of, v_of, key_parts, bias_of=None, w_out=None, out_bias=None, mid_bias=None,
              make_feed=None):
    nc = core.nc
    keys = sum(n for _, n in key_parts)
    parts = len(key_parts)
    even_parts = len({n for _, n in key_parts}) == 1
    copies = 1 if even_parts else parts
    chunks = HEADS * dh // P
    G = QT * HEADS
    wide = dh == DH
    masked = bias_of is not None
    RING = 2 if make_feed else 3
    TURN, VALUE = 3, 5
    PR, TP = TURN + 2, 4
    on_act = ACT_COPIES if not make_feed else ACT_COPIES_LOCAL
    with core.stage() as st, ExitStack() as mem:
        def tmp(name, shape):
            return mem.enter_context(nc.sbuf_tensor(f"attn_{name}_{nc.next_id()}", shape, F32))
        SC = core.ps[0:RING]
        PT = core.ps[3:5]
        OUT = core.ps[5:7]
        FIN = core.ps[7]
        probs = tmp("probs", [P, PR, keys])
        shifted = tmp("shifted", [P, 3, keys]) if masked else None
        pts = tmp("pts", [P, TP, parts, P])
        negmax, total, recip = tmp("negmax", [P, G]), tmp("total", [P, G]), tmp("recip", [P, G])
        oT = tmp("oT", [P, chunks, P])
        scores_ready, max_ready, exp_ready, recip_ready, probs_ready = (
            st.sem(n) for n in ("scores_ready", "max_ready", "exp_ready", "recip_ready", "probs_ready"))
        turned, turned_act, turned_dve, heads_done, oT_ready, projected, y_ready = (
            st.sem(n) for n in ("turned", "turned_act", "turned_dve", "heads_done", "oT_ready", "projected",
                                "y_ready"))
        feed = make_feed(st, core.ps[2], FIN, y_ready) if make_feed else NoFeed()
        PROJECT = 2
        oT_copies = 2 if wide else 1
        last_step = G + VALUE + PROJECT + 2

        def out_place(t, h):
            if wide:
                return OUT[h // 8][DH * (h % 2):DH * (h % 2) + DH, (h // 2 % 4) * P:(h // 2 % 4 + 1) * P]
            return OUT[t % 2][32 * (h // 4):32 * (h // 4) + 32, 0:P]

        def copy_turned(op, g, sem):
            if even_parts:
                n = key_parts[0][1]
                op(pts[0:n, g % TP, :, :], PT[g % 2][0:n, 0:parts * P].rearrange("p (c q) -> p c q", q=P))\
                    .then_inc(sem, 1)
            else:
                for i, (_, n) in enumerate(key_parts):
                    op(pts[0:n, g % TP, i, :], PT[g % 2][0:n, i * P:(i + 1) * P]).then_inc(sem, 1)

        def copies_until(g):
            return copies * sum(on_act(i) == on_act(g) for i in range(g + 1))

        def copy_done(g):
            return (turned_act if on_act(g) else turned_dve), copies_until(g)

        def finishing(s, offset):
            t, h = divmod(s - (HEADS - 1 + VALUE) - offset, HEADS)
            return t if h == 0 and 0 <= t < QT else None

        @st.block.sync
        def _(sp):
            sp.sem_clear(st.stale)

        @st.block.gpsimd
        def _(pool):
            for k in range(HEADS):
                feed.pool(0, k)
            for s in range(G - HEADS):
                feed.pool(s // HEADS + 1, s % HEADS)

        @st.block.tensor
        def _(pe):
            for k in range(HEADS):
                feed.pe(0, k)
            for s in range(last_step):
                if s < G:
                    feed.before_scores(*divmod(s, HEADS))
                    if s >= RING:
                        pe.wait_ge(max_ready if masked else exp_ready, s - RING + 1)
                    nc.tensor.matmul(SC[s % RING][:, 0:keys], q_of(*divmod(s, HEADS)), k_of(*divmod(s, HEADS)),
                                     start=True, stop=True).then_inc(scores_ready, 1)
                g = s - TURN
                if 0 <= g < G:
                    pe.wait_ge(probs_ready, g + 1)
                    if g >= 2:
                        pe.wait_ge(*copy_done(g - 2))
                    for i, (first, n) in enumerate(key_parts):
                        mm = nc.tensor.transpose(PT[g % 2][0:n, i * P:(i + 1) * P],
                                                 probs[:, g % PR, first:first + n], core.ident)
                    mm.then_inc(turned, 1)
                if s < G and s // HEADS + 1 < QT:
                    feed.pe(s // HEADS + 1, s % HEADS)
                g = s - VALUE
                if 0 <= g < G:
                    t, h = divmod(g, HEADS)
                    pe.wait_ge(*copy_done(g))
                    if wide and t >= 1 and h in (0, HEADS // 2):
                        pe.wait_ge(oT_ready, 2 * (t - 1) + (1 if h == 0 else 2))
                    elif not wide and t >= 2 and h == 0:
                        pe.wait_ge(oT_ready, t - 1)
                    for i, (_, n) in enumerate(key_parts):
                        mm = nc.tensor.matmul(out_place(t, h), v_of(t, h, i), pts[0:n, g % TP, i, :],
                                              start=(i == 0 and (wide or h % 4 == 0)),
                                              stop=(i == parts - 1 and (wide or h % 4 == 3)))
                    mm.then_inc(heads_done, 1)
                t = finishing(s, PROJECT)
                if t is not None and w_out is not None:
                    pe.wait_ge(oT_ready, oT_copies * (t + 1))
                    feed.before_projection(t)
                    if t > 0:
                        pe.wait_ge(y_ready, t)
                    for c in range(chunks):
                        mm = nc.tensor.matmul(FIN[:, 0:P], w_out(c), oT[:, c, :], start=(c == 0),
                                              stop=(c == chunks - 1))
                    mm.then_inc(projected, 1)

        @st.block.scalar
        def _(act):
            for k in range(HEADS):
                feed.act(0, k)
            for s in range(last_step):
                if s < G:
                    act.wait_ge(max_ready, s + 1)
                    if s >= PR:
                        act.wait_ge(turned, s - PR + 1)
                    nc.scalar.activation(probs[:, s % PR, :],
                                         shifted[:, s % 3, :] if masked else SC[s % RING][:, 0:keys],
                                         ACT.Exp, bias=negmax[:, s:s + 1], scale=-1.0 if masked else 1.0,
                                         accum_out=total[:, s:s + 1]).then_inc(exp_ready, 1)
                g = s - TURN
                if 0 <= g < G and on_act(g):
                    act.wait_ge(turned, g + 1)
                    if g >= TP:
                        act.wait_ge(heads_done, g - TP + 1)
                    copy_turned(nc.scalar.copy, g, turned_act)
                if s < G and s // HEADS + 1 < QT:
                    feed.act(s // HEADS + 1, s % HEADS)
                for j in range(oT_copies):
                    t, late = divmod(s - VALUE + 1 - HEADS // oT_copies * (j + 1), HEADS)
                    if late or not 0 <= t < QT:
                        continue
                    act.wait_ge(heads_done, t * HEADS + HEADS // oT_copies * (j + 1))
                    if w_out is None:
                        nc.scalar.activation(core.Y[:, t * TILE:(t + 1) * TILE], OUT[t % 2][:, 0:P],
                                             ACT.Identity, bias=out_bias).then_inc(oT_ready, 1)
                        continue
                    if t > 0:
                        act.wait_ge(projected, t)
                    if wide:
                        src = OUT[j][:, :].rearrange("p (c q) -> p c q", q=P)
                    else:
                        src = OUT[t % 2][:, 0:P].unsqueeze(1)
                    nc.scalar.activation(oT[:, 4 * j:min(4 * j + 4, chunks), :], src, ACT.Identity,
                                         bias=0.0 if mid_bias is None else mid_bias).then_inc(oT_ready, 1)
                t = finishing(s, PROJECT + 1)
                if t is not None and w_out is not None:
                    act.wait_ge(projected, t + 1)
                    nc.scalar.activation(core.Y[:, t * TILE:(t + 1) * TILE], FIN[:, 0:P], ACT.Identity,
                                         bias=0.0 if out_bias is None else out_bias).then_inc(y_ready, 1)

        @st.block.vector
        def _(dve):
            for k in range(HEADS):
                feed.dve(0, k)
            for s in range(G + TURN):
                if s < G:
                    dve.wait_ge(scores_ready, s + 1)
                    if masked:
                        if s >= 3:
                            dve.wait_ge(exp_ready, s - 2)
                        nc.vector.tensor_tensor_reduce(shifted[:, s % 3, :], bias_of(s // HEADS),
                                                       SC[s % RING][:, 0:keys], -1.0, 3e38, ALU.add, ALU.min,
                                                       negmax[:, s:s + 1]).then_inc(max_ready, 1)
                    else:
                        nc.vector.tensor_reduce(negmax[:, s:s + 1], SC[s % RING][:, 0:keys], AX_X, ALU.max,
                                                negate=True).then_inc(max_ready, 1)
                g = s - 1
                if 0 <= g < G:
                    dve.wait_ge(exp_ready, g + 1)
                    nc.vector.reciprocal(recip[:, g:g + 1], total[:, g:g + 1]).then_inc(recip_ready, 1)
                    dve.wait_ge(recip_ready, g + 1)
                    nc.vector.tensor_scalar(probs[:, g % PR, :], probs[:, g % PR, :], recip[:, g:g + 1], None,
                                            ALU.mult).then_inc(probs_ready, 1)
                g = s - TURN
                if 0 <= g < G and not on_act(g):
                    dve.wait_ge(turned, g + 1)
                    if g >= TP:
                        dve.wait_ge(heads_done, g - TP + 1)
                    copy_turned(nc.vector.tensor_copy, g, turned_dve)
                if s < G and s // HEADS + 1 < QT:
                    feed.dve(s // HEADS + 1, s % HEADS)



def cross_wide(core, b, w, src, has_null, scale, mask, out_bias, tag):
    nc = core.nc
    keys = CTX_LEN + 2 * has_null
    part = keys // 2
    with ExitStack() as mem:
        def tmp(name, shape, dt=F32):
            return mem.enter_context(nc.sbuf_tensor(f"{tag}_{name}_{nc.next_id()}", shape, dt))
        Q, K, V = tmp("Q", [P, CHUNKS, S]), tmp("K", [P, CHUNKS, keys]), tmp("V", [part, 2, INNER])
        dense(core, CHUNKS, lambda j, m: w("Wq", m * P, (m + 1) * P), lambda j: src, lambda m: Q[:, m, :],
              scale=lambda m: scale)
        dense(core, CHUNKS, lambda j, m: w("Wk", m * P, (m + 1) * P)[0:CTX_D, :], lambda j: core.ctxT[:, :],
              lambda m: K[:, m, 0:CTX_LEN], n=CTX_LEN)
        if mask is not None:
            rows = QT if mask == "per_query" else 1
            bias = tmp("bias", [P, rows, keys])
            mask_raw = tmp("mask_raw", [P, QT * CTX_LEN // 4], U32)
            mask_u8 = mask_raw[:, :].bitcast(U8)[:, 0:rows * CTX_LEN].rearrange("p (t k) -> p t k", t=rows)
        with core.stage() as st:
            product_ready, evac, mask_loaded, null_loaded, step = (
                st.sem(n) for n in ("product_ready", "evac", "mask_loaded", "null_loaded", "step"))

            @st.block.sync
            def _(sp):
                sp.sem_clear(st.stale)
                if mask == "per_query":
                    sp.dma_start(mask_raw[:, :], core.dram["mask_q"])\
                      .then_inc(mask_loaded, 16)
                elif mask == "per_batch":
                    sp.dma_start(mask_u8[:, 0, :], core.dram["mask_b"][b, :].partition_broadcast(P))\
                      .then_inc(mask_loaded, 16)

            @st.block.tensor
            def _(pe):
                for g in range(4):
                    i, half = g // 2, g % 2
                    n = min(part, CTX_LEN - i * part)
                    nc.tensor.matmul(core.ps[g][0:n, :], core.ctxT[:, i * part:i * part + n],
                                     w("Wv", half * 512, (half + 1) * 512)[0:CTX_D, :], start=True, stop=True)\
                      .then_inc(product_ready, 1)

            @st.block.vector
            def _(dve):
                link = Chain(dve, step)
                if has_null:
                    link(nc.vector.tensor_copy(K[:, :, CTX_LEN:CTX_LEN + 1],
                                               w("null_k").unsqueeze(1).broadcast_to([P, CHUNKS, 1])))
                    link(nc.vector.memset(K[:, :, CTX_LEN + 1:keys], 0.0))
                if mask is not None:
                    dve.wait_ge(mask_loaded, 16)
                    link(nc.vector.tensor_scalar(bias[:, :, 0:CTX_LEN], mask_u8[:, :, :], 1.0, -MASKED,
                                                 ALU.subtract, ALU.mult))
                    if has_null:
                        link(nc.vector.memset(bias[:, :, CTX_LEN:CTX_LEN + 1], 0.0))
                        link(nc.vector.memset(bias[:, :, CTX_LEN + 1:keys], MASKED))

            @st.block.scalar
            def _(act):
                for g in range(4):
                    i, half = g // 2, g % 2
                    n = min(part, CTX_LEN - i * part)
                    act.wait_ge(product_ready, g + 1)
                    nc.scalar.copy(V[0:n, i, half * 512:(half + 1) * 512], core.ps[g][0:n, :]).then_inc(evac, 1)
                if has_null:
                    act.dma_start(V[CTX_LEN - part:keys - part, 1, :], core.dram["null_v"]).then_inc(null_loaded, 16)
                    act.wait_ge(null_loaded, 16)

        attention(core, DH,
                  lambda t, h: Q[DH * (h % 2):DH * (h % 2) + DH, h // 2, t * TILE:(t + 1) * TILE],
                  lambda t, h: K[DH * (h % 2):DH * (h % 2) + DH, h // 2, :],
                  lambda t, h, i: V[:, i, h * DH:(h + 1) * DH],
                  [(0, part), (part, part)],
                  bias_of=None if mask is None else lambda t: bias[:, t if mask == "per_query" else 0, :],
                  w_out=lambda c: w("Wo", c * P, (c + 1) * P), out_bias=out_bias)


def cross_null(core, b, arena):
    w = core.weights("L0x", arena)
    with core.nc.sbuf_tensor(f"l0x_xn{core.nc.next_id()}", [P, S], F32) as xn:
        normalize(core, core.X, xn[:, :], gain=w("g_norm"))
        cross_wide(core, b, w, xn[:, :], True, DH ** -0.5, "per_batch", None, "l0x")
    normalize(core, core.Y[:, :], core.Y[:, :], gain=w("g_out"))
    residual_norm(core)


def cross_plain(core, b, arena):
    w = core.weights("L1x", arena)
    cross_wide(core, b, w, core.X, False, DH ** -0.5, None, w("bo"), "l1x")
    residual_norm(core)


def cross_masked(core, b, arena):
    w = core.weights("L2x", arena)
    with core.nc.sbuf_tensor(f"l2x_xn{core.nc.next_id()}", [P, S], F32) as xn:
        normalize(core, core.X, xn[:, :], gain=w("gamma"), shift=w("beta"))
        cross_wide(core, b, w, xn[:, :], False, DH ** -0.5, "per_query", w("bo"), "l2x")
    residual_norm(core)



def ternary_ffn(core, b, arena):
    nc = core.nc
    w = core.weights("L0f", arena)
    H = 512
    M = H // P
    with nc.sbuf_tensor(f"l0f_a{nc.next_id()}", [P, M, S], F32) as a, \
            nc.sbuf_tensor(f"l0f_b{nc.next_id()}", [P, M, S], F32) as h:
        gated(core, M, lambda m: w("w1", m * P, (m + 1) * P), lambda m: w("w2", m * P, (m + 1) * P), core.X,
              lambda m: a[:, m, :], ACT.Silu, act_scale=lambda m: w("s1", m, m + 1), lin=lambda m: w("s2", m, m + 1))
        dense(core, M, lambda k, m: w("h1", k * H + m * P, k * H + (m + 1) * P), lambda k: a[:, k, :],
              lambda m: h[:, m, :], kcount=M, func=ACT.Gelu, scale=lambda m: w("sh1", m, m + 1))
        dense(core, M, lambda k, m: w("h2", k * H + m * P, k * H + (m + 1) * P), lambda k: h[:, k, :],
              lambda m: a[:, m, :], kcount=M, func=ACT.Gelu, scale=lambda m: w("sh2", m, m + 1))
        dense(core, 1, lambda k, m: w("w3", k * P, (k + 1) * P), lambda k: a[:, k, :], lambda m: core.Y[:, :],
              kcount=M, scale=lambda m: w("s3"))
    residual_norm(core)



def add_residual(core, dst):
    nc = core.nc
    with core.stage() as st:
        added = st.sem("added")

        @st.block.sync
        def _(sp):
            sp.sem_clear(st.stale)

        @st.block.vector
        def _(dve):
            nc.vector.tensor_tensor(dst, core.X, core.Y[:, :], ALU.add).then_inc(added, 1)


def values_by_token(core, w, V):
    nc = core.nc
    with core.stage() as st:
        product_ready, evac = st.sem("product_ready"), st.sem("evac")

        @st.block.sync
        def _(sp):
            sp.sem_clear(st.stale)

        @st.block.tensor
        def _(pe):
            for t in range(QT):
                mm = nc.tensor.matmul(core.ps[0][:, t * D:(t + 1) * D], core.X[:, t * TILE:(t + 1) * TILE], w,
                                      start=True, stop=True)
            mm.then_inc(product_ready, 1)

        @st.block.scalar
        def _(act):
            act.wait_ge(product_ready, 1)
            nc.scalar.copy(V[:, :, :].rearrange("p t f -> p (t f)"), core.ps[0][:, :]).then_inc(evac, 1)


def spread_heads(core, src, QM):
    nc = core.nc
    masks = core.c("head_scale")
    with core.stage() as st:
        spread = st.sem("spread")

        @st.block.sync
        def _(sp):
            sp.sem_clear(st.stale)

        @st.block.vector
        def _(dve):
            for j in range(4):
                nc.vector.tensor_scalar(QM[:, j, :], src, masks[:, j:j + 1], None, ALU.mult).then_inc(spread, 1)


def narrow_attention(core, QM, K, V, key_parts, **kw):
    nc = core.nc
    parts, rows = len(key_parts), key_parts[0][1]
    with nc.sbuf_tensor(f"narrow_V{nc.next_id()}", [P, parts, 4, P], F32) as VM:
        with core.stage() as st:
            zeroed, filled = st.sem("zeroed"), st.sem("filled")

            @st.block.sync
            def _(sp):
                sp.sem_clear(st.stale)

            @st.block.gpsimd
            def _(pool):
                nc.gpsimd.memset(VM[:, :, :, :], 0.0).then_inc(zeroed, 1)

            @st.block.vector
            def _(dve):
                dve.wait_ge(zeroed, 1)
                for j in range(4):
                    for i in range(parts):
                        nc.vector.tensor_copy(
                            VM[0:rows, i, j, :].rearrange("p (g f) -> p g f", f=32)[:, :, j * SH:(j + 1) * SH],
                            V[0:rows, i, :].rearrange("p (g f) -> p g f", f=32)[:, :, j * SH:(j + 1) * SH])\
                          .then_inc(filled, 1)
        attention(core, SH,
                  lambda t, h: QM[32 * (h // 4):32 * (h // 4) + 32, h % 4, t * TILE:(t + 1) * TILE],
                  lambda t, h: K[32 * (h // 4):32 * (h // 4) + 32, :],
                  lambda t, h, i: VM[0:rows, i, h % 4, 32 * (h // 4):32 * (h // 4) + 32], key_parts, **kw)


FOUR_PARTS = [(i * P, P) for i in range(S // P)]



def latent_attention(core, b, arena):
    nc = core.nc
    w = core.weights("L1a", arena)
    with ExitStack() as mem:
        def tmp(name, shape):
            return mem.enter_context(nc.sbuf_tensor(f"l1a_{name}_{nc.next_id()}", shape, F32))
        qk, rot, part = tmp("qk", [P, QT, 2, D]), tmp("rot", [P, QT, 2, D]), tmp("part", [P, QT, 2, D])
        V = tmp("V", [P, QT, D])
        sq = tmp("sq", [P, QT, D])
        mean, std = tmp("mean", [P, QT * HEADS]), tmp("std", [P, QT * HEADS])
        eps = tmp("eps", [P, 1])
        K, QM = tmp("K", [P, S]), tmp("QM", [P, 4, S])
        H4 = SH // 2
        with core.stage() as st:
            product_ready, evac, step, var_ready, std_ready, lkv_ready, turned, keys_ready = (
                st.sem(n) for n in ("product_ready", "evac", "step", "var_ready", "std_ready", "lkv_ready",
                                    "turned", "keys_ready"))
            eps_ready, q_ready = st.sem("eps_ready"), st.sem("q_ready")

            @st.block.sync
            def _(sp):
                sp.sem_clear(st.stale)

            @st.block.gpsimd
            def _(pool):
                nc.gpsimd.memset(eps[:, :], LN_EPS).then_inc(eps_ready, 1)

            @st.block.tensor
            def _(pe):
                for t in range(QT):
                    nc.tensor.matmul(core.ps[t][:, 0:2 * D], core.X[:, t * TILE:(t + 1) * TILE], w("Wqkv"),
                                     start=True, stop=True).then_inc(product_ready, 1)
                pe.wait_ge(q_ready, 1)
                for t in range(QT):
                    mm = nc.tensor.transpose(core.ps[4][:, t * P:(t + 1) * P], rot[:, t, 0, :], core.ident)
                mm.then_inc(turned, 1)
                pe.wait_ge(lkv_ready, 1)
                for t in range(QT):
                    mm = nc.tensor.transpose(core.ps[5][:, t * P:(t + 1) * P], V[:, t, :], core.ident)
                mm.then_inc(turned, 1)

            @st.block.scalar
            def _(act):
                for t in range(QT):
                    act.wait_ge(product_ready, t + 1)
                    nc.scalar.copy(qk[:, t, :, :].rearrange("p a f -> p (a f)"), core.ps[t][:, 0:2 * D])\
                      .then_inc(evac, 1)
                act.wait_ge(turned, 1)
                masks = core.c("head_scale")
                for j in range(4):
                    nc.scalar.mul(QM[:, j, LAT:S], core.ps[4][:, 0:S - LAT], masks[:, j:j + 1]).then_inc(evac, 1)
                    nc.scalar.mul(QM[:, j, 0:LAT], core.ps[4][:, S - LAT:S], masks[:, j:j + 1]).then_inc(evac, 1)
                act.wait_ge(eps_ready, 1)
                act.wait_ge(var_ready, 1)
                nc.scalar.activation(std[:, :], mean[:, :], ACT.Sqrt, bias=eps[:, 0:1], scale=1.0 / SH)\
                  .then_inc(std_ready, 1)
                act.wait_ge(turned, 2)
                nc.scalar.copy(K[:, :], core.ps[5][:, :]).then_inc(evac, 1)

            @st.block.vector
            def _(dve):
                link = Chain(dve, step)
                cos = core.c("rot_cos").rearrange("p (t d) -> p t d", d=SH)
                sin = core.c("rot_sin").rearrange("p (t d) -> p t d", d=SH)
                N = 2 * HEADS

                def heads_view(x):
                    return x[:, :, :, :].rearrange("p t a (h d) -> p t (a h) d", d=SH)
                dve.wait_ge(evac, QT)
                link(nc.vector.tensor_tensor(heads_view(rot), heads_view(qk),
                                             cos.unsqueeze(2).broadcast_to([P, QT, N, SH]), ALU.mult))
                link(nc.vector.tensor_tensor(heads_view(part)[:, :, :, 0:H4], heads_view(qk)[:, :, :, H4:SH],
                                             sin[:, :, 0:H4].unsqueeze(2).broadcast_to([P, QT, N, H4]), ALU.mult))
                link(nc.vector.tensor_tensor(heads_view(part)[:, :, :, H4:SH], heads_view(qk)[:, :, :, 0:H4],
                                             sin[:, :, H4:SH].unsqueeze(2).broadcast_to([P, QT, N, H4]), ALU.mult))
                nc.vector.tensor_tensor(rot[:, :, :, :], rot[:, :, :, :], part[:, :, :, :], ALU.add)\
                  .then_inc(q_ready, 1)
                dve.wait_ge(q_ready, 1)
                kv = rot[:, :, 1, :].rearrange("p t (h d) -> p t h d", d=SH)
                out = V[:, :, :].rearrange("p t (h d) -> p (t h) d", d=SH)
                out4 = V[:, :, :].rearrange("p t (h d) -> p t h d", d=SH)
                mean4 = mean[:, :].rearrange("p (t h) -> p t h", t=QT)
                link(nc.vector.tensor_reduce(mean4, kv, AX_X, ALU.add))
                link(nc.vector.tensor_scalar(mean[:, :], mean[:, :], 1.0 / SH, None, ALU.mult))
                link(nc.vector.tensor_tensor(out4, kv, mean4.unsqueeze(3).broadcast_to([P, QT, HEADS, SH]),
                                             ALU.subtract))
                link(nc.vector.tensor_tensor(sq[:, :, :], V[:, :, :], V[:, :, :], ALU.mult))
                nc.vector.tensor_reduce(mean4, sq[:, :, :].rearrange("p t (h d) -> p t h d", d=SH), AX_X, ALU.add)\
                  .then_inc(var_ready, 1)
                dve.wait_ge(std_ready, 1)
                link(nc.vector.reciprocal(std[:, :], std[:, :]))
                link(nc.vector.tensor_tensor(out, out, std[:, :].unsqueeze(2).broadcast_to([P, QT * HEADS, SH]),
                                             ALU.mult))
                link(nc.vector.tensor_tensor(out, out, w("ln_g").unsqueeze(1).broadcast_to([P, QT * HEADS, SH]),
                                             ALU.mult))
                nc.vector.tensor_tensor(out, out, w("ln_b").unsqueeze(1).broadcast_to([P, QT * HEADS, SH]),
                                        ALU.add).then_inc(lkv_ready, 1)

        narrow_attention(core, QM, K, V, FOUR_PARTS,
                         bias_of=lambda t: w("latent_mask", t * S, (t + 1) * S),
                         w_out=lambda c: w("Wo"), out_bias=w("bo"))
    residual_norm(core)



def projected_attention(core, b, arena):
    nc = core.nc
    w = core.weights("L3a", arena)
    with ExitStack() as mem:
        def tmp(name, shape):
            return mem.enter_context(nc.sbuf_tensor(f"l3a_{name}_{nc.next_id()}", shape, F32))
        first, second = tmp("first", [P, 2, S]), tmp("second", [P, 2, S])
        V, QM = tmp("V", [P, QT, D]), tmp("QM", [P, 4, S])
        dense(core, 2, lambda k, m: w("Wq" if m == 0 else "Wk"), lambda k: core.X, lambda m: first[:, m, :],
              bias=lambda m: w("bq" if m == 0 else "bk"))
        values_by_token(core, w("Wv"), V)
        for m in range(2):
            dense(core, 1, lambda k, _: w("Wp"), lambda k: first[:, m, :], lambda _: second[:, m, :])
        spread_heads(core, second[:, 0, :], QM)
        narrow_attention(core, QM, second[:, 1, :], V, FOUR_PARTS,
                         out_bias=w("bv"))
    residual_norm(core)


def cross_narrow(core, b, arena):
    nc = core.nc
    w = core.weights("L3x", arena)
    part = CTX_LEN // 2
    with ExitStack() as mem:
        def tmp(name, shape):
            return mem.enter_context(nc.sbuf_tensor(f"l3x_{name}_{nc.next_id()}", shape, F32))
        Q, K, V = tmp("Q", [P, S]), tmp("K", [P, CTX_LEN]), tmp("V", [part, 2, D])
        QM = tmp("QM", [P, 4, S])
        dense(core, 1, lambda k, m: w("Wq"), lambda k: core.X, lambda m: Q[:, :], bias=lambda m: w("bq"))
        dense(core, 1, lambda k, m: w("Wk")[0:CTX_D, :], lambda k: core.ctxT[:, :], lambda m: K[:, :],
              bias=lambda m: w("bk"), n=CTX_LEN)
        with core.stage() as st:
            product_ready, evac = st.sem("product_ready"), st.sem("evac")

            @st.block.sync
            def _(sp):
                sp.sem_clear(st.stale)

            @st.block.tensor
            def _(pe):
                for i in range(2):
                    mm = nc.tensor.matmul(core.ps[0][0:part, i * D:(i + 1) * D],
                                          core.ctxT[:, i * part:(i + 1) * part], w("Wv")[0:CTX_D, :],
                                          start=True, stop=True)
                mm.then_inc(product_ready, 1)

            @st.block.scalar
            def _(act):
                act.wait_ge(product_ready, 1)
                nc.scalar.copy(V[:, :, :].rearrange("p i f -> p (i f)"), core.ps[0][0:part, 0:2 * D])\
                  .then_inc(evac, 1)
        spread_heads(core, Q[:, :], QM)
        narrow_attention(core, QM, K[:, :], V,
                             [(0, part), (part, part)], mid_bias=w("bv"), w_out=lambda c: w("Wo"), out_bias=w("bo"))
    residual_norm(core)



def shifted_tokens(core, xs):
    nc = core.nc
    half = D // 2
    with core.stage() as st:
        copied = st.sem("copied")

        @st.block.sync
        def _(sp):
            sp.sem_clear(st.stale)

        @st.block.vector
        def _(dve):
            nc.vector.tensor_copy(xs[0:half, :], core.X[0:half, :]).then_inc(copied, 1)

        @st.block.scalar
        def _(act):
            nc.scalar.copy(xs[half:D, :], core.XP[half:D, PAD - 1:PAD - 1 + S]).then_inc(copied, 1)


class LocalFeed:

    GROUPS = (0, 2, 1, 3)
    PRODUCT = {0: 0, 1: 1, 2: 2, 3: 3, 5: 4, 7: 5}
    SQUARE = {1: 0, 2: 1, 3: 2, 4: 3}
    SUM = {2: 0, 3: 1, 4: 2, 5: 3}
    ROOT = 6
    SCALE = {10: 0, 11: 1, 12: 2, 13: 3}
    TURN = {11: 0, 12: 1, 14: 2, 15: 3}

    def __init__(self, core, st, bank, turn_bank, y_ready, bufs, w, qk_scale):
        self.core, self.w, self.qk_scale = core, w, qk_scale
        self.y_ready = y_ready
        self.bank = lambda t, i: bank if t > 0 else core.ps[2 + i % 5]
        self.turn_bank = lambda t, i: turn_bank if t > 0 or i == 0 else core.ps[3 + i]
        (self.xs, self.qk, self.rot, self.swapped, self.squares, self.cos, self.sin, self.norm,
         self.inverse, self.refine, self.q_tile, self.K,
         self.V, self.V_before) = bufs
        (self.product_ready, self.bank_read, self.raw_ready, self.squares_ready, self.sums_ready, self.roots_ready,
         self.tables_ready, self.rotary_step, self.turns_ready, self.step, self.rotated, self.turned,
         self.turned_read, self.clamped, self.root_step) = (
            st.sem(n) for n in ("product_ready", "bank_read", "raw_ready", "squares_ready", "sums_ready",
                                "roots_ready", "tables_ready", "rotary_step", "turns_ready", "step", "rotated",
                                "turned", "turned_read", "clamped", "root_step"))
        self.links = 0

    def group(self, a, g):
        return a[:, g * 512:(g + 1) * 512].rearrange("p (h d) -> p h d", d=DH)

    def pe(self, t, k):
        nc, pe = self.core.nc, self.core.nc.tensor
        i = self.PRODUCT.get(k)
        if i is not None:
            use = 6 * t + i
            if use > 0:
                pe.wait_ge(self.bank_read, use if t > 0 else max(use - 4, 1))
            g = self.GROUPS[i] if i < 4 else i
            nc.tensor.matmul(self.bank(t, i)[:, :], self.xs[:, t * TILE:(t + 1) * TILE],
                             self.w("Wqkv", g * 512, (g + 1) * 512), start=True, stop=True)\
              .then_inc(self.product_ready, 1)
        i = self.TURN.get(k)
        if i is not None:
            g = self.GROUPS[i]
            pe.wait_ge(self.rotated, 4 * t + i + 1)
            if t > 0:
                pe.wait_ge(self.turned_read, 4 * t + i)
            else:
                pe.wait_ge(self.bank_read, 6)
            if i == 0 and t >= 2:
                pe.wait_ge(self.y_ready, t - 1)
            for c in range(4):
                mm = nc.tensor.transpose(self.turn_bank(t, i)[:, c * P:(c + 1) * P],
                                         self.rot[:, g * 512 + c * P:g * 512 + (c + 1) * P], self.core.ident)
            mm.then_inc(self.turned, 1)

    def before_projection(self, t):
        self.core.nc.tensor.wait_ge(self.turned_read, 4 * min(t + 2, QT))

    def before_scores(self, t, h):
        if h % 8 == 0:
            self.core.nc.tensor.wait_ge(self.turned_read, 4 * t + 2 + h // 4)

    def act(self, t, k):
        nc, act = self.core.nc, self.core.nc.scalar
        i = self.PRODUCT.get(k)
        if i is not None:
            act.wait_ge(self.product_ready, 6 * t + i + 1)
            if i < 4:
                g = self.GROUPS[i]
                if t > 0:
                    act.wait_ge(self.turns_ready, 4 * (t - 1) + i + 1)
                nc.scalar.copy(self.qk[:, g * 512:(g + 1) * 512], self.bank(t, i)[:, :]).then_inc(self.raw_ready, 1)
                act.wait_ge(self.raw_ready, 4 * t + i + 1)
                act.sem_inc(self.bank_read, 1)
            else:
                nc.scalar.copy(self.V[:, t, (i - 4) * 512:(i - 3) * 512], self.bank(t, i)[:, :]).then_inc(self.bank_read, 1)
        i = self.SQUARE.get(k)
        if i is not None:
            g = self.GROUPS[i]
            if 4 * t + i >= 2:
                act.wait_ge(self.sums_ready, 4 * t + i - 1)
            nc.scalar.activation(self.squares[:, (i % 2) * 512:(i % 2 + 1) * 512],
                                 self.qk[:, g * 512:(g + 1) * 512], ACT.Square).then_inc(self.squares_ready, 1)
        i = self.TURN.get(k)
        if i is not None:
            g = self.GROUPS[i]
            act.wait_ge(self.turned, 4 * t + i + 1)
            src = self.turn_bank(t, i)[:, :].rearrange("p (c q) -> p c q", q=P)
            if g < 2:
                nc.scalar.mul(self.q_tile[:, t % 2, 4 * g:4 * g + 4, :], src, self.qk_scale)\
                  .then_inc(self.turned_read, 1)
            else:
                nc.scalar.copy(self.K[:, 4 * (g - 2):4 * (g - 2) + 4, WINDOW + t * TILE:WINDOW + (t + 1) * TILE], src)\
                  .then_inc(self.turned_read, 1)

    def dve(self, t, k):
        nc, dve = self.core.nc, self.core.nc.vector

        def link(ins):
            self.links += 1
            ins.then_inc(self.step, 1)
            dve.wait_ge(self.step, self.links)
        if t == 0:
            self.rotary(dve, t, k)
        if k == self.ROOT:
            if t == 0:
                link(nc.vector.memset(self.K[:, :, 0:WINDOW], 0.0))
                link(nc.vector.memset(self.V_before[:, 0, :], 0.0))
            else:
                dve.wait_ge(self.bank_read, 6 * t)
                link(nc.vector.tensor_copy(self.V_before[:, t % 2, :], self.V[P - WINDOW:P, t - 1, :]))
        i = self.SUM.get(k)
        if i is not None:
            g = self.GROUPS[i]
            dve.wait_ge(self.squares_ready, 4 * t + i + 1)
            nc.vector.tensor_reduce(self.norm[:, t, 8 * g:8 * g + 8],
                                    self.squares[:, (i % 2) * 512:(i % 2 + 1) * 512]
                                    .rearrange("p (h d) -> p h d", d=DH), AX_X, ALU.add)\
              .then_inc(self.sums_ready, 1)
        if i == 3:
            dve.wait_ge(self.sums_ready, 4 * t + 4)
            nc.vector.tensor_scalar(self.norm[:, t, :], self.norm[:, t, :], 1e-24, None, ALU.max)\
              .then_inc(self.clamped, 1)
        if t == 0 and k == self.ROOT:
            self.roots(dve, t)
        i = self.SCALE.get(k)
        if i is not None:
            g = self.GROUPS[i]
            dve.wait_ge(self.roots_ready, t + 1)
            dve.wait_ge(self.turns_ready, 4 * t + i + 1)
            group = self.group(self.rot, g)
            nc.vector.tensor_tensor(group, group, self.inverse[:, t, 8 * g:8 * g + 8].unsqueeze(2)
                                    .broadcast_to([P, 8, DH]), ALU.mult).then_inc(self.rotated, 1)

    def pool(self, t, k):
        if t > 0:
            self.rotary(self.core.nc.gpsimd, t, k)
            if k == 3:
                self.roots(self.core.nc.gpsimd, t)

    def roots(self, eng, t):
        link = Chain(eng, self.root_step)
        link.steps = ROOT_STEPS * t
        eng.wait_ge(self.clamped, t + 1)
        inverse_root(eng, link, self.norm[:, t, :], self.inverse[:, t, :], self.refine[:, :])
        eng.sem_inc(self.roots_ready, 1)

    def rotary(self, eng, t, k):
        HALF = DH // 2
        if k == 0:
            if t > 0:
                eng.wait_ge(self.turns_ready, 4 * t)
            for table, const, scale in ((self.cos, "local_cos", "qk_scale"),
                                        (self.sin, "local_sin", "qk_scale_swapped")):
                eng.tensor_tensor(table[:, :], self.core.c(const)[:, t * P:(t + 1) * P], self.w(scale),
                                  ALU.mult).then_inc(self.tables_ready, 1)
            eng.wait_ge(self.tables_ready, 2 * (t + 1))
        if 1 <= k < 5:
            i = k - 1
            g = self.GROUPS[i]
            a = g // 2
            raw, rot, other = self.group(self.qk, g), self.group(self.rot, g), self.group(self.swapped, 0)
            eng.wait_ge(self.raw_ready, 4 * t + i + 1)
            if t > 0:
                eng.wait_ge(self.turned, 4 * (t - 1) + i + 1)
            if 4 * t + i > 0:
                eng.wait_ge(self.turns_ready, 4 * t + i)
            eng.tensor_tensor(rot, raw, self.cos[:, a * DH:(a + 1) * DH].unsqueeze(1)
                              .broadcast_to([P, 8, DH]), ALU.mult).then_inc(self.rotary_step, 1)
            for lo in (0, HALF):
                eng.tensor_tensor(other[:, :, lo:lo + HALF], raw[:, :, HALF - lo:2 * HALF - lo],
                                  self.sin[:, a * DH + lo:a * DH + lo + HALF].unsqueeze(1)
                                  .broadcast_to([P, 8, HALF]), ALU.mult).then_inc(self.rotary_step, 1)
            eng.wait_ge(self.rotary_step, 3 * (4 * t + i + 1))
            eng.tensor_tensor(rot, rot, other, ALU.add).then_inc(self.turns_ready, 1)


def local_attention(core, arena):
    nc = core.nc
    w = core.weights("L1f_a", arena)
    QK_SCALE = 8.0
    with ExitStack() as mem:
        def tmp(name, shape):
            return mem.enter_context(nc.sbuf_tensor(f"local_{name}_{nc.next_id()}", shape, F32))
        xs = tmp("xs", [P, S])
        qk, rot = tmp("qk", [P, 4 * 512]), tmp("rot", [P, 4 * 512])
        swapped, squares = tmp("swapped", [P, 512]), tmp("squares", [P, 2 * 512])
        cos, sin = tmp("cos", [P, 2 * DH]), tmp("sin", [P, 2 * DH])
        norm, inverse = tmp("norm", [P, QT, 2 * HEADS]), tmp("inverse", [P, QT, 2 * HEADS])
        refine = tmp("refine", [P, 2 * HEADS])
        q_tile, K = tmp("q_tile", [P, 2, CHUNKS, TILE]), tmp("K", [P, CHUNKS, WINDOW + S])
        V, V_before = tmp("V", [P, QT, INNER]), tmp("V_before", [WINDOW, 2, INNER])
        shifted_tokens(core, xs)
        bufs = (xs, qk, rot, swapped, squares, cos, sin, norm, inverse, refine, q_tile, K, V, V_before)
        attention(core, DH,
                  lambda t, h: q_tile[DH * (h % 2):DH * (h % 2) + DH, t % 2, h // 2, :],
                  lambda t, h: K[DH * (h % 2):DH * (h % 2) + DH, h // 2, t * TILE:t * TILE + LOCAL_KEYS],
                  lambda t, h, i: V_before[:, t % 2, h * DH:(h + 1) * DH] if i == 0 else V[:, t, h * DH:(h + 1) * DH],
                  [(0, WINDOW), (WINDOW, TILE)],
                  bias_of=lambda t: core.c("local_mask")[:, t * LOCAL_KEYS:(t + 1) * LOCAL_KEYS],
                  w_out=lambda c: w("Wo", c * P, (c + 1) * P),
                  make_feed=lambda st, *banks: LocalFeed(core, st, *banks, bufs, w, QK_SCALE))
    add_residual(core, core.X)


def gelu_ffn(core, arena):
    nc = core.nc
    w = core.weights("L1f_f", arena)
    M = (FFN_INNER + P - 1) // P
    rows = [min(P, FFN_INNER - m * P) for m in range(M)]
    with nc.sbuf_tensor(f"l1f_xs{nc.next_id()}", [P, S], F32) as xs, \
            nc.sbuf_tensor(f"l1f_h{nc.next_id()}", [P, M, S], F32) as h:
        shifted_tokens(core, xs)
        normalize(core, xs[:, :], xs[:, :], gain=w("ln_g"), shift=w("ln_b"))
        gated(core, M, lambda m: w("W1_gate", m * P, m * P + rows[m]), lambda m: w("W1_lin", m * P, m * P + rows[m]),
              xs[:, :], lambda m: h[0:rows[m], m, :], ACT.Gelu,
              act_bias=lambda m: w("b1_gate", m, m + 1)[0:rows[m], :],
              lin_op=ALU.add, lin=lambda m: w("b1_lin", m, m + 1)[0:rows[m], :])
        dense(core, 1, lambda k, m: w("W2", k * P, (k + 1) * P)[0:rows[k], :], lambda k: h[0:rows[k], k, :],
              lambda m: core.Y[:, :], kcount=M, bias=lambda m: w("b2"))
    add_residual(core, core.X)


def local_transformer(core, b, arena):
    nc = core.nc
    with nc.sbuf_tensor(f"l1f_input{nc.next_id()}", [P, S], F32) as kept:
        with core.stage() as st:
            copied = st.sem("copied")

            @st.block.sync
            def _(sp):
                sp.sem_clear(st.stale)

            @st.block.vector
            def _(dve):
                nc.vector.tensor_copy(kept[:, :], core.X).then_inc(copied, 1)

        with nc.Fori(0, DEPTH) as i:
            turn(core, arena, core.dram["L1f_f"][i, :, :])
            local_attention(core, arena)
            turn(core, 1 - arena, core.dram["L1f_a"][i + 1, :, :])
            gelu_ffn(core, 1 - arena)
        normalize(core, core.X, core.X, add=kept[:, :])



SEG = 10
SEGS = 9
SSM_CHUNK = SEG * SEGS
SSM_CHUNKS = 6
LEAD = SEG - 1
SSM_T = SSM_CHUNK * SSM_CHUNKS
DN = 2 * SSM_N


def soft_clamp_const(lo, hi):
    return (hi + lo) / 2.0, (hi - lo) / 2.0


def state_space(core, b, arena):
    nc = core.nc
    w = core.weights("L2a", arena)
    with ExitStack() as mem:
        def tmp(name, shape):
            return mem.enter_context(nc.sbuf_tensor(f"ssm_{name}_{nc.next_id()}", shape, F32))
        XC, G = tmp("XC", [P, 2, S]), tmp("G", [P, 2, S])
        dt, u, y = tmp("dt", [P, 2, SSM_T]), tmp("u", [P, 2, SSM_T]), tmp("y", [P, 2, SSM_T])
        BC = tmp("BC", [SSM_N, 2, SSM_T])
        rate = tmp("rate", [P, DN])
        real = slice(LEAD, LEAD + S)
        with nc.sbuf_tensor(f"ssm_xn{nc.next_id()}", [P, S], F32) as xn, \
                nc.sbuf_tensor(f"ssm_xb{nc.next_id()}", [P, 2, CONV - 1 + S], F32) as xb, \
                nc.sbuf_tensor(f"ssm_sp{nc.next_id()}", [P, 2, S], F32) as sp_, \
                nc.sbuf_tensor(f"ssm_z{nc.next_id()}", [P, 2, S], F32) as z:
            normalize(core, core.X, xn[:, :], gain=w("norm_w"), centred=False, eps=1e-6)
            dense(core, 2, lambda k, m: w("W_in", m * P, (m + 1) * P), lambda k: xn[:, :],
                  lambda m: xb[:, m, CONV - 1:])
            dense(core, 2, lambda k, m: w("W_in", (m + 2) * P, (m + 3) * P), lambda k: xn[:, :],
                  lambda m: G[:, m, :], func=ACT.Silu)
            with core.stage() as st:
                step, conv_ready, xc_ready, zeroed = (st.sem(n) for n in ("step", "conv_ready", "xc_ready", "zeroed"))

                @st.block.sync
                def _(sp):
                    sp.sem_clear(st.stale)

                @st.block.gpsimd
                def _(pool):
                    for a in (dt, u, BC):
                        nc.gpsimd.memset(a[:, :, 0:LEAD], 0.0).then_inc(zeroed, 1)
                        nc.gpsimd.memset(a[:, :, LEAD + S:SSM_T], 0.0).then_inc(zeroed, 1)

                @st.block.vector
                def _(dve):
                    link = Chain(dve, step)
                    link(nc.vector.memset(xb[:, :, 0:CONV - 1], 0.0))
                    for c in range(2):
                        link(nc.vector.tensor_scalar(z[:, c, :], xb[:, c, 0:S], w("conv_w", 4 * c, 4 * c + 1),
                                                     w("conv_b", c, c + 1), ALU.mult, ALU.add))
                        for j in range(1, CONV):
                            ins = nc.vector.scalar_tensor_tensor(
                                out=z[:, c, :], in0=xb[:, c, j:j + S], scalar=w("conv_w", 4 * c + j, 4 * c + j + 1),
                                in1=z[:, c, :], op0=ALU.mult, op1=ALU.add)
                            if j < CONV - 1:
                                link(ins)
                            else:
                                ins.then_inc(conv_ready, 1)

                @st.block.scalar
                def _(act):
                    for c in range(2):
                        act.wait_ge(conv_ready, c + 1)
                        nc.scalar.activation(XC[:, c, :], z[:, c, :], ACT.Silu).then_inc(xc_ready, 1)

            dense(core, 2, lambda k, m: w("W_dt", k * SSM_D + m * P, k * SSM_D + (m + 1) * P),
                  lambda k: XC[:, k, :], lambda m: z[:, m, :], kcount=2, bias=lambda m: w("b_dt", m, m + 1))
            dense(core, 2, lambda k, m: w("W_BC", (2 * k + m) * SSM_N, (2 * k + m + 1) * SSM_N),
                  lambda k: XC[:, k, :], lambda m: BC[:, m, real], kcount=2)
            mid, half = soft_clamp_const(0.001, 0.1)
            with core.stage() as st:
                step, act_step, log_ready, arg_ready, tanh_ready, rate_ready = (
                    st.sem(n) for n in ("step", "act_step", "log_ready", "arg_ready", "tanh_ready", "rate_ready"))

                @st.block.sync
                def _(sp):
                    sp.sem_clear(st.stale)

                @st.block.scalar
                def _(act):
                    link = Chain(act, act_step)
                    link(nc.scalar.activation(sp_[:, :, :], z[:, :, :], ACT.Abs))
                    link(nc.scalar.activation(sp_[:, :, :], sp_[:, :, :], ACT.Exp, scale=-1.0))
                    nc.scalar.activation(sp_[:, :, :], sp_[:, :, :], ACT.Ln, bias=1.0).then_inc(log_ready, 1)
                    link(nc.scalar.activation(rate[:, :], w("A_log"), ACT.Tanh, scale=0.5 / (5.0 + 1e-8)))
                    nc.scalar.activation(rate[:, :], rate[:, :], ACT.Exp, scale=5.0 / 0.5).then_inc(rate_ready, 1)
                    act.wait_ge(arg_ready, 1)
                    nc.scalar.activation(sp_[:, :, :], sp_[:, :, :], ACT.Tanh).then_inc(tanh_ready, 1)

                @st.block.vector
                def _(dve):
                    link = Chain(dve, step)
                    dve.wait_ge(log_ready, 1)
                    link(nc.vector.scalar_tensor_tensor(out=sp_[:, :, :], in0=z[:, :, :], scalar=0.0,
                                                        in1=sp_[:, :, :], op0=ALU.max, op1=ALU.add))
                    nc.vector.tensor_scalar(sp_[:, :, :], sp_[:, :, :], mid, 0.5 / (half + 1e-8),
                                            ALU.subtract, ALU.mult).then_inc(arg_ready, 1)
                    dve.wait_ge(rate_ready, 1)
                    link(nc.vector.tensor_scalar(rate[:, :], rate[:, :], -0.5 / (8.0 + 1e-8), None, ALU.mult))
                    dve.wait_ge(tanh_ready, 1)
                    link(nc.vector.tensor_scalar(dt[:, :, real], sp_[:, :, :], half / 0.5, mid, ALU.mult, ALU.add))
                    link(nc.vector.tensor_tensor(u[:, :, real], dt[:, :, real], XC[:, :, :], ALU.mult))

        dA, H = tmp("dA", [P, SEGS, DN, SEG]), tmp("H", [P, SEGS, DN, SEG])
        first, carry = tmp("first", [P, SEGS, DN]), tmp("carry", [P, DN])
        scratch, sums, fac = tmp("scratch", [P, DN]), tmp("sums", [P, 1]), tmp("fac", [P, 1])
        C_rows, norm, squares = tmp("C_rows", [P, SSM_N, SSM_CHUNK]), tmp("norm", [P, 1]), tmp("squares", [P, DN])
        with core.stage() as st:
            zeroed = st.sem("zeroed")

            @st.block.sync
            def _(sp):
                sp.sem_clear(st.stale)

            @st.block.vector
            def _(dve):
                nc.vector.memset(carry[:, :], 0.0).then_inc(zeroed, 1)

        with nc.Fori(0, SSM_CHUNKS) as k:
            ssm_chunk(core, bass.ds(k * SSM_CHUNK, SSM_CHUNK), dt, u, y, BC, rate, dA, H, first, carry, scratch,
                      sums, fac, C_rows, norm, squares)

        with core.stage() as st:
            step = st.sem("step")

            @st.block.sync
            def _(sp):
                sp.sem_clear(st.stale)

            @st.block.vector
            def _(dve):
                link = Chain(dve, step)
                for c in range(2):
                    link(nc.vector.scalar_tensor_tensor(out=XC[:, c, :], in0=XC[:, c, :], scalar=w("D", c, c + 1),
                                                        in1=y[:, c, real], op0=ALU.mult, op1=ALU.add))
                link(nc.vector.tensor_tensor(G[:, :, :], G[:, :, :], XC[:, :, :], ALU.mult))

            @st.block.scalar
            def _(act):
                nc.scalar.activation(fac[:, :], w("residual"), ACT.Sigmoid).then_inc(st.sem("sigmoid"), 1)
        with core.stage() as st:
            step = st.sem("step")

            @st.block.sync
            def _(sp):
                sp.sem_clear(st.stale)

            @st.block.vector
            def _(dve):
                nc.vector.tensor_scalar(fac[:, :], fac[:, :], 0.5, None, ALU.mult).then_inc(step, 1)
        dense(core, 1, lambda k, m: w("W_out", k * P, (k + 1) * P), lambda k: G[:, k, :], lambda m: core.Y[:, :],
              kcount=2, scale=lambda m: fac[:, 0:1])
    add_residual(core, core.Y[:, :])
    residual_norm(core)


def ssm_chunk(core, cols, dt, u, y, BC, rate, dA, H, first, carry, scratch, sums, fac, C_rows, norm,
              squares):
    nc = core.nc
    PER_BANK = 5
    C_PART = 4
    C_GROUPS = SSM_N // C_PART
    LIMIT = 20.0
    LAG = 5
    groups = [(n, min(PER_BANK, SSM_N - n)) for n in range(0, SSM_N, PER_BANK)]

    def steps(a, n):
        return a.unsqueeze(1).broadcast_to([P, n, SSM_CHUNK]).rearrange("p n (s j) -> p n s j", j=SEG)

    def states(a, c, n0, n):
        return a[:, :, c * SSM_N + n0:c * SSM_N + n0 + n, :].rearrange("p s n j -> p n s j")

    def rows(bank, n):
        return core.ps[bank][:, 0:n * SSM_CHUNK].rearrange("p (n s j) -> p n s j", n=n, j=SEG)

    def spread_rows(bank, m, n0, n):
        for i in range(n):
            mm = nc.tensor.matmul(core.ps[bank][:, i * SSM_CHUNK:(i + 1) * SSM_CHUNK],
                                  core.ident[0:SSM_N, n0 + i:n0 + i + 1].broadcast_to([SSM_N, P]),
                                  BC[:, m, cols], start=True, stop=True)
        return mm

    with core.stage() as st:
        spread, args_ready, tanh_ready, decay_ready, step = (
            st.sem(n) for n in ("spread", "args_ready", "tanh_ready", "decay_ready", "step"))

        @st.block.sync
        def _(sp):
            sp.sem_clear(st.stale)

        @st.block.tensor
        def _(pe):
            for g, (n0, n) in enumerate(groups):
                spread_rows(g, 0, n0, n).then_inc(spread, 1)

        def decay_args(eng, c):
            eng.tensor_tensor(
                states(dA, c, 0, SSM_N), steps(dt[:, c, cols], SSM_N),
                rate[:, c * SSM_N:(c + 1) * SSM_N].unsqueeze(2).broadcast_to([P, SSM_N, SSM_CHUNK])
                .rearrange("p n (s j) -> p n s j", j=SEG), ALU.mult).then_inc(args_ready, 1)

        @st.block.gpsimd
        def _(pool):
            decay_args(nc.gpsimd, 0)

        @st.block.scalar
        def _(act):
            flat = dA[:, :, :, :].rearrange("p s n j -> p (s n j)")
            act.wait_ge(args_ready, 2)
            nc.scalar.activation(flat, flat, ACT.Tanh).then_inc(tanh_ready, 1)
            act.wait_ge(tanh_ready, 1)
            nc.scalar.activation(flat, flat, ACT.Exp, scale=8.0 / 0.5).then_inc(decay_ready, 1)

        @st.block.vector
        def _(dve):
            link = Chain(dve, step)
            decay_args(nc.vector, 1)
            for g, (n0, n) in enumerate(groups):
                dve.wait_ge(spread, g + 1)
                for c in range(2):
                    link(nc.vector.tensor_tensor(states(H, c, n0, n), steps(u[:, c, cols], n), rows(g, n), ALU.mult))
            dve.wait_ge(decay_ready, 1)
            link(nc.vector.tensor_copy(first[:, :, :], dA[:, :, :, 0]))
            link(nc.vector.memset(dA[:, :, :, 0], 0.0))

    with core.stage() as st:
        spread, step, sums_ready, total_ready, norm_ready, limited, rows_copied, weighed, summed = (
            st.sem(n) for n in ("spread", "step", "sums_ready", "total_ready", "norm_ready", "limited", "rows_copied",
                                "weighed", "summed"))

        @st.block.sync
        def _(sp):
            sp.sem_clear(st.stale)

        @st.block.tensor
        def _(pe):
            for s in range(SEGS):
                if s < C_GROUPS:
                    spread_rows(1 + s, 1, s * C_PART, C_PART).then_inc(spread, 1)
                pe.wait_ge(sums_ready, s + 1)
                nc.tensor.matmul(core.ps[0][:, 0:1], core.c("ones"), sums[:, :], start=True, stop=True)\
                  .then_inc(total_ready, 1)

        @st.block.scalar
        def _(act):
            for s in range(SEGS):
                act.wait_ge(total_ready, s + 1)
                nc.scalar.activation(norm[:, :], core.ps[0][:, 0:1], ACT.Sqrt, scale=LIMIT ** -2)\
                  .then_inc(norm_ready, 1)
                if s < C_GROUPS:
                    act.wait_ge(spread, s + 1)
                    nc.scalar.copy(C_rows[:, s * C_PART:(s + 1) * C_PART, :],
                                   core.ps[1 + s][:, 0:C_PART * SSM_CHUNK].rearrange("p (n j) -> p n j", n=C_PART))\
                      .then_inc(rows_copied, 1)

        @st.block.gpsimd
        def _(pool):
            pool.wait_ge(rows_copied, C_GROUPS)
            for s in range(SEGS):
                pool.wait_ge(limited, s + 1)
                for c in range(2):
                    pairs = slice(c * SSM_N, (c + 1) * SSM_N)
                    nc.gpsimd.tensor_tensor(dA[:, s, pairs, :], H[:, s, pairs, :],
                                            C_rows[:, :, s * SEG:(s + 1) * SEG], ALU.mult).then_inc(weighed, 1)

        @st.block.vector
        def _(dve):
            link = Chain(dve, step)

            def limit(s):
                last = H[:, s, :, SEG - 1]
                nc.vector.tensor_scalar(last, last, fac[:, 0:1], None, ALU.mult).then_inc(limited, 1)

            def output(s):
                dve.wait_ge(weighed, 2 * (s + 1))
                nc.vector.tensor_reduce(
                    y[:, :, cols].rearrange("p c (s j) -> p c s j", j=SEG)[:, :, s, :],
                    dA[:, s, :, :].rearrange("p (c n) j -> p c j n", n=SSM_N), AX_X, ALU.add).then_inc(summed, 1)

            link(nc.vector.tensor_tensor(scratch[:, :], first[:, 0, :], carry[:, :], ALU.mult))
            for s in range(SEGS):
                if s == 0:
                    link(nc.vector.tensor_tensor(H[:, s, :, 0], H[:, s, :, 0], scratch[:, :], ALU.add))
                else:
                    link(nc.vector.scalar_tensor_tensor(out=H[:, s, :, 0], in0=scratch[:, :], scalar=fac[:, 0:1],
                                                        in1=H[:, s, :, 0], op0=ALU.mult, op1=ALU.add))
                segment = H[:, s, :, :].rearrange("p n j -> p (n j)")
                link(nc.vector.tensor_tensor_scan(segment, dA[:, s, :, :].rearrange("p n j -> p (n j)"), segment,
                                                  0.0, ALU.mult, ALU.add))
                last = H[:, s, :, SEG - 1]
                nc.vector.scalar_tensor_tensor(out=squares[:, :], in0=last, scalar=1.0, in1=last, op0=ALU.mult,
                                               op1=ALU.mult, accum_out=sums[:, :]).then_inc(sums_ready, 1)
                if s + 1 < SEGS:
                    link(nc.vector.tensor_tensor(scratch[:, :], first[:, s + 1, :], last, ALU.mult))
                if s >= 1:
                    limit(s - 1)
                for done in range(2 * (s - LAG), min(2 * (s - LAG) + 2, s - 1)):
                    if done >= 0:
                        output(done)
                dve.wait_ge(norm_ready, s + 1)
                if s >= 1:
                    dve.wait_ge(limited, s)
                link(nc.vector.tensor_scalar(fac[:, :], norm[:, :], 1e-8 / LIMIT, 1.0, ALU.add, ALU.max))
                link(nc.vector.reciprocal(fac[:, :], fac[:, :]))
            limit(SEGS - 1)
            dve.wait_ge(limited, SEGS)
            link(nc.vector.tensor_copy(carry[:, :], H[:, SEGS - 1, :, SEG - 1]))
            for s in range(min(2 * (SEGS - LAG), SEGS - 2), SEGS):
                output(s)



ROUND = 1.5 * 2.0 ** 23


def quantize_weights(core, raw, out):
    nc = core.nc
    with core.stage() as st, nc.sbuf_tensor(f"wq_abs{nc.next_id()}", [P, 2, 512], F32) as mag, \
            nc.sbuf_tensor(f"wq_sum{nc.next_id()}", [P, 2], F32) as sums, \
            nc.sbuf_tensor(f"wq_mean{nc.next_id()}", [P, 2], F32) as mean, \
            nc.sbuf_tensor(f"wq_inv{nc.next_id()}", [P, 2], F32) as inv:
        sums_ready, total_ready, step = st.sem("sums_ready"), st.sem("total_ready"), st.sem("step")

        @st.block.sync
        def _(sp):
            sp.sem_clear(st.stale)

        @st.block.scalar
        def _(act):
            for i in range(2):
                nc.scalar.activation(mag[:, i, :], raw[i], ACT.Abs, accum_out=sums[:, i:i + 1]).then_inc(sums_ready, 1)

        @st.block.tensor
        def _(pe):
            pe.wait_ge(sums_ready, 2)
            nc.tensor.matmul(core.ps[0][:, 0:2], core.c("ones"), sums[:, :], start=True, stop=True)\
              .then_inc(total_ready, 1)

        @st.block.vector
        def _(dve):
            link = Chain(dve, step)
            dve.wait_ge(total_ready, 1)
            link(nc.vector.tensor_scalar(mean[:, :], core.ps[0][:, 0:2], 1.0 / (P * 512), 1e-5, ALU.mult, ALU.max))
            link(nc.vector.reciprocal(inv[:, :], mean[:, :]))
            for i in range(2):
                link(nc.vector.tensor_scalar(out[i], raw[i], inv[:, i:i + 1], ROUND, ALU.mult, ALU.add))
                link(nc.vector.tensor_scalar(out[i], out[i], ROUND, 1.0, ALU.subtract, ALU.min))
                link(nc.vector.tensor_scalar(out[i], out[i], -1.0, mean[:, i:i + 1], ALU.max, ALU.mult))


def quantize_tokens(core, src, dst, chunks):
    nc = core.nc
    width = chunks * P
    with core.stage() as st, nc.sbuf_tensor(f"tq{nc.next_id()}", [P, QT, width], F32) as q, \
            nc.sbuf_tensor(f"tq_max{nc.next_id()}", [P, QT], F32) as top, \
            nc.sbuf_tensor(f"tq_scale{nc.next_id()}", [P, QT], F32) as scale:
        turned, step, quantized, back, evac = (st.sem(n) for n in ("turned", "step", "quantized", "back", "evac"))

        @st.block.sync
        def _(sp):
            sp.sem_clear(st.stale)

        @st.block.tensor
        def _(pe):
            for t in range(QT):
                for c in range(chunks):
                    mm = nc.tensor.transpose(core.ps[t][:, c * P:(c + 1) * P], src[:, c, t * P:(t + 1) * P],
                                             core.ident)
                mm.then_inc(turned, 1)
            pe.wait_ge(quantized, QT)
            for c in range(chunks):
                for t in range(QT):
                    mm = nc.tensor.transpose(core.ps[4 + c][:, t * P:(t + 1) * P], q[:, t, c * P:(c + 1) * P],
                                             core.ident)
                mm.then_inc(back, 1)

        @st.block.vector
        def _(dve):
            link = Chain(dve, step)
            for t in range(QT):
                dve.wait_ge(turned, t + 1)
                one = slice(t, t + 1)
                link(nc.vector.tensor_reduce(top[:, one], core.ps[t][:, 0:width], AX_X, ALU.max,
                                             apply_absolute_value=True))
                link(nc.vector.tensor_scalar(top[:, one], top[:, one], 1e-5, None, ALU.max))
                link(nc.vector.reciprocal(scale[:, one], top[:, one]))
                link(nc.vector.tensor_scalar(scale[:, one], scale[:, one], 127.0, None, ALU.mult))
                link(nc.vector.tensor_scalar(top[:, one], top[:, one], 1.0 / 127.0, None, ALU.mult))
                link(nc.vector.tensor_scalar(q[:, t, :], core.ps[t][:, 0:width], scale[:, one], ROUND,
                                             ALU.mult, ALU.add))
                link(nc.vector.tensor_scalar(q[:, t, :], q[:, t, :], ROUND, 127.0, ALU.subtract, ALU.min))
                nc.vector.tensor_scalar(q[:, t, :], q[:, t, :], -128.0, top[:, one], ALU.max, ALU.mult)\
                  .then_inc(quantized, 1)

        @st.block.scalar
        def _(act):
            for c in range(chunks):
                act.wait_ge(back, c + 1)
                nc.scalar.copy(dst[:, c, :], core.ps[4 + c][:, :]).then_inc(evac, 1)


def bit_ffn(core, b, arena):
    nc = core.nc
    w = core.weights("L2f", arena)
    M = 4
    with ExitStack() as mem:
        def tmp(name, shape):
            return mem.enter_context(nc.sbuf_tensor(f"l2f_{name}_{nc.next_id()}", shape, F32))
        W, xq = tmp("W", [P, 2, 512]), tmp("xq", [P, 1, S])
        h, z, hq = tmp("h", [P, M, S + 2]), tmp("z", [P, M, S]), tmp("hq", [P, M, S])
        quantize_weights(core, [w("w1"), w("w2")], [W[:, i, :] for i in range(2)])
        quantize_tokens(core, core.X.unsqueeze(1), xq, 1)
        dense(core, M, lambda k, m: W[:, 0, m * P:(m + 1) * P], lambda k: xq[:, 0, :], lambda m: h[:, m, 1:S + 1])
        with core.stage() as st:
            step, conv_ready, silu_ready = (st.sem(n) for n in ("step", "conv_ready", "silu_ready"))

            @st.block.sync
            def _(sp):
                sp.sem_clear(st.stale)

            @st.block.vector
            def _(dve):
                link = Chain(dve, step)
                link(nc.vector.memset(h[:, :, 0:1], 0.0))
                link(nc.vector.memset(h[:, :, S + 1:S + 2], 0.0))
                for m in range(M):
                    link(nc.vector.tensor_scalar(z[:, m, :], h[:, m, 0:S], w("conv_w", 3 * m, 3 * m + 1),
                                                 w("conv_b", m, m + 1), ALU.mult, ALU.add))
                    for j in (1, 2):
                        ins = nc.vector.scalar_tensor_tensor(
                            out=z[:, m, :], in0=h[:, m, j:j + S], scalar=w("conv_w", 3 * m + j, 3 * m + j + 1),
                            in1=z[:, m, :], op0=ALU.mult, op1=ALU.add)
                        if j == 1:
                            link(ins)
                        else:
                            ins.then_inc(conv_ready, 1)

            @st.block.scalar
            def _(act):
                for m in range(M):
                    act.wait_ge(conv_ready, m + 1)
                    nc.scalar.activation(z[:, m, :], z[:, m, :], ACT.Silu).then_inc(silu_ready, 1)

        quantize_tokens(core, z, hq, M)
        dense(core, 1, lambda k, m: W[:, 1, k * P:(k + 1) * P], lambda k: hq[:, k, :], lambda m: core.Y[:, :],
              kcount=M)
    residual_norm(core)



def experts(core, b, arena):
    nc = core.nc
    w = core.weights("L3f", arena)
    M = (EXPERTS + 1) * EXPERT_H // P
    with ExitStack() as mem:
        def tmp(name, shape, dt=F32):
            return mem.enter_context(nc.sbuf_tensor(f"l3f_{name}_{nc.next_id()}", shape, dt))
        h = tmp("h", [P, M, S])
        logits, best, index = tmp("logits", [P, QT, 8]), tmp("best", [P, QT, 8]), tmp("index", [P, QT, 8], U32)
        indexf, chosen, share = tmp("indexf", [P, QT, 8]), tmp("chosen", [P, QT, 8]), tmp("share", [P, QT, 8])
        total, shareT = tmp("total", [P, QT]), tmp("shareT", [EXPERTS, S])
        gated(core, M, lambda m: w("W1", m * P, (m + 1) * P), lambda m: w("W3", m * P, (m + 1) * P), core.X,
              lambda m: h[:, m, :], ACT.Silu)
        with core.stage() as st:
            product_ready, step, arg_ready, exp_ready, share_ready, turned, evac, spread, weighted = (
                st.sem(n) for n in ("product_ready", "step", "arg_ready", "exp_ready", "share_ready", "turned",
                                    "evac", "spread", "weighted"))

            @st.block.sync
            def _(sp):
                sp.sem_clear(st.stale)

            @st.block.tensor
            def _(pe):
                for t in range(QT):
                    mm = nc.tensor.matmul(core.ps[0][:, t * 8:(t + 1) * 8], core.X[:, t * P:(t + 1) * P], w("Wg"),
                                          start=True, stop=True)
                mm.then_inc(product_ready, 1)
                pe.wait_ge(share_ready, 1)
                for t in range(QT):
                    mm = nc.tensor.transpose(core.ps[1][0:EXPERTS, t * P:(t + 1) * P], share[:, t, :], core.ident)
                mm.then_inc(turned, 1)
                pe.wait_ge(evac, 1)
                for e in range(EXPERTS):
                    if e >= 4:
                        pe.wait_ge(weighted, 2 * (e - 3))
                    nc.tensor.matmul(core.ps[2 + e % 4][:, :],
                                     core.ident[0:EXPERTS, e:e + 1].broadcast_to([EXPERTS, P]), shareT[:, :],
                                     start=True, stop=True).then_inc(spread, 1)

            @st.block.scalar
            def _(act):
                act.wait_ge(arg_ready, 1)
                nc.scalar.activation(share[:, :, :], share[:, :, :], ACT.Exp).then_inc(exp_ready, 1)
                act.wait_ge(turned, 1)
                nc.scalar.copy(shareT[:, :], core.ps[1][0:EXPERTS, :]).then_inc(evac, 1)

            @st.block.vector
            def _(dve):
                link = Chain(dve, step)
                dve.wait_ge(product_ready, 1)
                link(nc.vector.tensor_copy(logits[:, :, :].rearrange("p t e -> p (t e)"), core.ps[0][:, 0:QT * 8]))
                for t in range(QT):
                    link(nc.vector.max(best[:, t, :], logits[:, t, :]))
                    link(nc.vector.max_index(index[:, t, :], best[:, t, :], logits[:, t, :]))
                nc.vector.tensor_tensor(share[:, :, :], logits[:, :, :], best[:, :, 0:1].broadcast_to([P, QT, 8]),
                                        ALU.subtract).then_inc(arg_ready, 1)
                link(nc.vector.tensor_copy(indexf[:, :, :], index[:, :, :]))
                number = core.c("number").unsqueeze(1).broadcast_to([P, QT, 8])
                link(nc.vector.tensor_tensor(chosen[:, :, :], number, indexf[:, :, 0:1].broadcast_to([P, QT, 8]),
                                             ALU.is_equal))
                link(nc.vector.tensor_tensor(logits[:, :, :], number, indexf[:, :, 1:2].broadcast_to([P, QT, 8]),
                                             ALU.is_equal))
                link(nc.vector.tensor_tensor(chosen[:, :, :], chosen[:, :, :], logits[:, :, :], ALU.add))
                dve.wait_ge(exp_ready, 1)
                link(nc.vector.tensor_tensor(share[:, :, :], share[:, :, :], chosen[:, :, :], ALU.mult))
                link(nc.vector.tensor_reduce(total[:, :], share[:, :, :], AX_X, ALU.add))
                link(nc.vector.reciprocal(total[:, :], total[:, :]))
                nc.vector.tensor_tensor(share[:, :, :], share[:, :, :], total[:, :].unsqueeze(2)
                                        .broadcast_to([P, QT, 8]), ALU.mult).then_inc(share_ready, 1)
                for e in range(EXPERTS):
                    dve.wait_ge(spread, e + 1)
                    for i in range(2):
                        nc.vector.tensor_tensor(h[:, 2 * e + i, :], h[:, 2 * e + i, :], core.ps[2 + e % 4][:, :],
                                                ALU.mult).then_inc(weighted, 1)
        dense(core, 1, lambda k, m: w("W2", k * P, (k + 1) * P), lambda k: h[:, k, :], lambda m: core.Y[:, :],
              kcount=M)
    residual_norm(core)


def run_sublayers(core, b, order):
    arena = 0
    for i, (name, f) in enumerate(order):
        if name == "L1f_a":
            f(core, b, arena)
            continue
        nxt = order[(i + 1) % len(order)][0]
        turn(core, arena, core.dram[nxt][0, :, :])
        f(core, b, arena)
        arena = 1 - arena


SUBLAYERS = [("L0x", cross_null), ("L0f", ternary_ffn), ("L1a", latent_attention), ("L1x", cross_plain),
             ("L1f_a", local_transformer), ("L2a", state_space), ("L2x", cross_masked), ("L2f", bit_ffn),
             ("L3a", projected_attention), ("L3x", cross_narrow), ("L3f", experts)]
WITH_RWKV = True


def build(nc, dram, cols):
    with ExitStack() as ctx:
        core = Core(nc, ctx, dram, cols)
        with nc.Block() as block:
            zeroed = core.banks[0][0]

            @block.sync
            def _(sp):
                first = dram[SUBLAYERS[0][0]] if SUBLAYERS else None
                if first is not None:
                    sp.dma_start(core.arenas[0][:, 0:first.shape[-1]], first[0, :, :]).then_inc(core.loaded[0], 16)
                sp.dma_start(core.const[:, :], dram["const"][0, :, :]).then_inc(core.resident_loaded, 16)
                sp.dma_start(core.rwkv[:, :], dram["L0a"][0, :, :]).then_inc(core.resident_loaded, 16)
                sp.wait_ge(core.resident_loaded, 32)

            @block.vector
            def _(dve):
                nc.vector.memset(core.XP[:, 0:PAD], 0.0).then_inc(zeroed, 1)

        with nc.Fori(0, B) as b:
            with nc.Block() as block:
                @block.sync
                def _(sp):
                    for span in core.spans:
                        sp.sem_clear(span)
                    sp.dma_start(core.X, dram["x"][b, :, :]).then_inc(core.tokens_loaded, 16)
                    sp.dma_start(core.ctxT[:, :], dram["ctx"][b, :, :]).then_inc(core.tokens_loaded, 16)
                    sp.wait_ge(core.tokens_loaded, 32)
                    sp.sem_clear(core.tokens_loaded)
            if WITH_RWKV:
                rwkv(core)
            run_sublayers(core, b, SUBLAYERS)
            with nc.Block() as block:
                @block.sync
                def _(sp):
                    sp.dma_start(dram["out"][b, :, :], core.X).then_inc(core.stored, 16)
                    sp.wait_ge(core.stored, 16)
                    sp.sem_clear(core.stored)
        with nc.Block() as block:
            @block.sync
            def _(sp):
                if SUBLAYERS:
                    sp.wait_ge(core.loaded[0], 16)



class Pack:

    def __init__(self):
        self.parts, self.cols, self.width = [], {}, 0

    def add(self, name, a):
        a = np.asarray(a)
        if a.ndim == 1:
            a = a[:, None]
        a = np.concatenate([a, np.zeros((P - a.shape[0], a.shape[1]), a.dtype)], 0)
        self.cols[name] = (self.width, self.width + a.shape[1])
        self.width += a.shape[1]
        self.parts.append(a)

    def array(self, width=None):
        width = width or self.width
        pad = np.zeros((P, width - self.width), np.float32)
        return np.ascontiguousarray(np.concatenate(self.parts + [pad], 1))


def by_chunk(a):
    k = a.shape[0] // P
    return a.reshape(k, P, -1).transpose(1, 0, 2).reshape(P, -1)


def cols_of(v):
    return v.reshape(-1, P).T


def by_tile(a):
    return a.reshape(QT, P, -1).transpose(1, 0, 2).reshape(P, -1).astype(np.float32)


def constants():
    c = Pack()
    c.add("ident", np.eye(P, dtype=np.float32))
    c.add("average", np.full((P, P), 1.0 / P, np.float32))
    c.add("ones", np.ones((P, P), np.float32))
    heads = np.arange(P) // SH
    c.add("head_scale", (heads[:, None] % 4 == np.arange(4)[None, :]).astype(np.float32) * np.float32(SH ** -0.5))
    c.add("number", np.tile(np.arange(8, dtype=np.float32), (P, 1)))
    pos = np.arange(S, dtype=np.float32)
    inv = (1.0 / np.float32(10000.0) ** (np.arange(0, SH, 2, dtype=np.float32) / SH)).astype(np.float32)
    ang = pos[:, None] * inv[None, :]
    c.add("rot_cos", by_tile(np.concatenate([np.cos(ang), np.cos(ang)], 1)))
    c.add("rot_sin", by_tile(np.concatenate([-np.sin(ang), np.sin(ang)], 1)))
    half = np.arange(0, DH, 2, dtype=np.float32)
    inv = (1.0 / np.float32(10000.0) ** (half / DH)).astype(np.float32)
    ang = pos[:, None] * inv[None, :]
    base = (half + np.float32(0.4 * DH)) / np.float32(1.4 * DH)
    length = base[None, :] ** ((pos - S // 2) / np.float32(WINDOW // 2))[:, None]
    cos, sin = np.cos(ang), np.sin(ang)
    c.add("local_cos", by_tile(np.concatenate([cos * length] * 2 + [cos / length] * 2, 1)))
    c.add("local_sin", by_tile(np.concatenate([-sin * length, sin * length, -sin / length, sin / length], 1)))
    i, j = np.arange(TILE)[:, None], np.arange(LOCAL_KEYS)[None, :] - WINDOW
    seen = np.stack([(j <= i) & (j >= i - WINDOW) & (t * TILE + j >= 0) for t in range(QT)])
    c.add("local_mask", by_tile(np.where(seen, 0.0, MASKED).reshape(S, LOCAL_KEYS)))
    return c


def packs(x):
    out = {}
    p = out["L0a"] = Pack()
    for n in ("Wk", "Wv", "Wr", "Wo"):
        p.add(n, x["L0_attn_" + n].T)
    for n in ("W", "U"):
        p.add(n, x["L0_attn_" + n])
    for n in "kvr":
        p.add("mix_" + n, x["L0_attn_time_mix_" + n].reshape(-1))
    p = out["L0x"] = Pack()
    p.add("Wq", x["L0_xattn_Wq"])
    p.add("Wk", x["L0_xattn_Wkv"][:, :INNER])
    p.add("Wv", x["L0_xattn_Wkv"][:, INNER:])
    p.add("Wo", by_chunk(x["L0_xattn_Wout"]))
    p.add("g_norm", x["L0_xattn_g_norm"])
    p.add("g_out", x["L0_xattn_g_out"])
    p.add("null_k", np.concatenate([x["L0_xattn_null_kv"][0]] * 2))
    p = out["L0f"] = Pack()
    p.add("w1", x["L0_ffn_w1_w"].T)
    p.add("w2", x["L0_ffn_w2_w"].T)
    p.add("h1", by_chunk(x["L0_ffn_h1_w"].T))
    p.add("h2", by_chunk(x["L0_ffn_h2_w"].T))
    p.add("w3", by_chunk(x["L0_ffn_w3_w"].T))
    for n, k in (("s1", "w1_s"), ("s2", "w2_s"), ("sh1", "h1_s"), ("sh2", "h2_s"), ("s3", "w3_s")):
        p.add(n, cols_of(x["L0_ffn_" + k]))
    p = out["L1x"] = Pack()
    for n in ("Wq", "Wk", "Wv"):
        p.add(n, x["L1_xattn_" + n])
    p.add("Wo", by_chunk(x["L1_xattn_Wo"]))
    p.add("bo", x["L1_xattn_bo"])
    p = out["L2x"] = Pack()
    p.add("Wq", x["L2_xattn_Wq"])
    p.add("Wk", x["L2_xattn_Wkv"][:, :INNER])
    p.add("Wv", x["L2_xattn_Wkv"][:, INNER:])
    p.add("Wo", by_chunk(x["L2_xattn_Wo"]))
    p.add("gamma", x["L2_xattn_ln_gamma"])
    p.add("beta", x["L2_xattn_ln_beta"])
    p.add("bo", x["L2_xattn_bo"])
    def rows_of(v):
        return np.tile(v[None, :], (P, 1))

    p = out["L1a"] = Pack()
    p.add("Wqkv", np.concatenate([x["L1_attn_Wq"].T, x["L1_attn_Wkv"].T], 1))
    p.add("Wo", x["L1_attn_Wo"].T)
    p.add("bo", x["L1_attn_bo"])
    p.add("ln_g", rows_of(x["L1_attn_ln_g"]))
    p.add("ln_b", rows_of(x["L1_attn_ln_b"]))
    at, key = np.arange(S)[:, None], np.arange(S)[None, :] - (S - LAT)
    p.add("latent_mask", by_tile(np.where((key < 0) | ((at < LAT) & (key <= at)), 0.0, MASKED)))
    p = out["L3a"] = Pack()
    for n in ("Wq", "Wk", "Wv"):
        p.add(n, x["L3_attn_" + n])
    for n in ("bq", "bk", "bv"):
        p.add(n, x["L3_attn_" + n])
    block = np.zeros((P, P), np.float32)
    for h in range(HEADS):
        block[h * SH:(h + 1) * SH, h * SH:(h + 1) * SH] = x["L3_attn_Wp"]
    p.add("Wp", block)
    p = out["L3x"] = Pack()
    p.add("Wq", x["L3_xattn_q_w"])
    p.add("Wk", x["L3_xattn_kv_w"][:, :D])
    p.add("Wv", x["L3_xattn_kv_w"][:, D:])
    p.add("Wo", x["L3_xattn_proj_w"])
    p.add("bq", x["L3_xattn_q_b"])
    p.add("bk", x["L3_xattn_kv_b"][:D])
    p.add("bv", x["L3_xattn_kv_b"][D:])
    p.add("bo", x["L3_xattn_proj_b"])
    p = out["L2a"] = Pack()
    p.add("W_in", x["L2_attn_W_in"].T)
    p.add("W_dt", by_chunk(x["L2_attn_W_dt"].T))
    p.add("W_BC", by_chunk(np.concatenate([x["L2_attn_W_B"].T, x["L2_attn_W_C"].T], 1)))
    p.add("W_out", by_chunk(x["L2_attn_W_out"].T))
    p.add("norm_w", x["L2_attn_norm_w"])
    p.add("conv_w", by_chunk(x["L2_attn_conv_w"][:, 0, :]))
    p.add("conv_b", cols_of(x["L2_attn_conv_b"]))
    p.add("b_dt", cols_of(x["L2_attn_b_dt"]))
    p.add("D", cols_of(x["L2_attn_D_param"]))
    p.add("A_log", by_chunk(x["L2_attn_A_log"]))
    p.add("residual", rows_of(x["L2_attn_residual_scale"].reshape(1)))
    p = out["L2f"] = Pack()
    p.add("w1", x["L2_ffn_w1"].T)
    p.add("w2", by_chunk(x["L2_ffn_w2"].T))
    p.add("conv_w", by_chunk(x["L2_ffn_conv_w"][:, 0, :]))
    p.add("conv_b", cols_of(x["L2_ffn_conv_b"]))
    p = out["L3f"] = Pack()
    p.add("Wg", x["L3_ffn_Wg"].T)
    for n in ("1", "3"):
        p.add("W" + n, np.concatenate([a.T for a in x["L3_ffn_W" + n]] + [x["L3_ffn_sw" + n].T], 1))
    p.add("W2", np.concatenate([by_chunk(a.T) for a in x["L3_ffn_W2"]] + [by_chunk(x["L3_ffn_sw2"].T)], 1))

    out = {k: [p] for k, p in out.items()}
    out["L1f_a"], out["L1f_f"] = [], []
    for i in range(DEPTH):
        p = Pack()
        out["L1f_a"].append(p)
        p.add("Wqkv", x["L1_ffn_Wqkv"][i])
        p.add("Wo", by_chunk(x["L1_ffn_Wo"][i]))
        q, k = x["L1_ffn_q_scale"][i], x["L1_ffn_k_scale"][i]
        p.add("qk_scale", rows_of(np.concatenate([q, k])))
        p.add("qk_scale_swapped", rows_of(np.concatenate([a[s] for a in (q, k) for s in
                                                          (slice(DH // 2, DH), slice(0, DH // 2))])))
        p = Pack()
        out["L1f_f"].append(p)
        W1, b1 = x["L1_ffn_W1"][i], x["L1_ffn_b1"][i]

        def chunk_pad(a):
            more = -a.shape[0] % P
            return np.concatenate([a, np.zeros((more,) + a.shape[1:], a.dtype)], 0)
        p.add("W1_lin", W1[:, :FFN_INNER])
        p.add("W1_gate", W1[:, FFN_INNER:])
        p.add("W2", by_chunk(chunk_pad(x["L1_ffn_W2"][i])))
        p.add("ln_g", x["L1_ffn_ln_g"][i])
        p.add("ln_b", x["L1_ffn_ln_b"][i])
        p.add("b1_lin", cols_of(chunk_pad(b1[:FFN_INNER])))
        p.add("b1_gate", cols_of(chunk_pad(b1[FFN_INNER:])))
        p.add("b2", x["L1_ffn_b2"][i])
    return out


def kernel(**inputs):
    import concourse.bacc as _bacc
    from concourse.bass_utils import run_bass_kernel_spmd as _run

    x = {k: np.asarray(v) for k, v in inputs.items()}
    null_v = np.tile(x["L0_xattn_null_kv"][1], HEADS)
    arrays = {
        "x": x["x"].transpose(0, 2, 1),
        "ctx": x["ctx_768"].transpose(0, 2, 1),
        "mask_b": x["mask_BxS2_bf1"].view(np.uint8),
        "mask_q": np.ascontiguousarray(x["mask_1x1xSxS2_bk0"].reshape(QT, P, CTX_LEN).transpose(1, 0, 2))
        .reshape(P, QT * CTX_LEN).view(np.uint32),
        "null_v": np.stack([null_v, np.zeros_like(null_v)]),
    }
    cols = {}
    packed = dict(packs(x), const=[constants()])
    names = [name for name, _ in SUBLAYERS]
    if "L1f_a" in names:
        packed["L1f_a"] = packed["L1f_a"] + packed[names[(names.index("L1f_a") + 1) % len(names)]][:1]
    for name, rounds in packed.items():
        width = max(p.width for p in rounds)
        arrays[name] = np.stack([p.array(width) for p in rounds])
        cols[name] = dict(rounds[0].cols, width=width)
    arrays = {k: np.ascontiguousarray(a) for k, a in arrays.items()}

    nc = _bacc.Bacc("TRN2", target_bir_lowering=False, num_devices=1)
    dram = {k: nc.dram_tensor("in_" + k, a.shape, mybir.dt.from_np(a.dtype), kind="ExternalInput").ap()
            for k, a in arrays.items()}
    dram["out"] = nc.dram_tensor("out", (B, D, S), F32, kind="ExternalOutput").ap()
    build(nc, dram, cols)
    r = _run(nc, [{"in_" + k: a for k, a in arrays.items()}], core_ids=[0])
    return r.results[0]["out"].transpose(0, 2, 1)
```
